# Optimizing a Trainium2 kernel written in Bass

```python
import numpy as np
import jax
import jax.numpy as jnp

def _softmax(x, axis=-1):
    return jax.nn.softmax(x, axis=axis)

def _gelu(x):
    return jax.nn.gelu(x, approximate=True)

def _silu(x):
    return jax.nn.silu(x)

def _sigmoid(x):
    return jax.nn.sigmoid(x)

def _layernorm(x, axis=-1, eps=1e-05):
    m = jnp.mean(x, axis=axis, keepdims=True)
    v = jnp.var(x, axis=axis, keepdims=True)
    return (x - m) / jnp.sqrt(v + eps)

def _scatter_add(tgt, idx, src, axis=0):
    return tgt.at[idx].add(src)

def _segment_sum(src, seg, n):
    return jax.ops.segment_sum(src, seg, n)
kernel_name = 'mk_vit_tower_cls_d2_tok_img768_r4_6719f8'

def setup_inputs(seed: int=0):
    np.random.seed(seed)
    _w = jnp.asarray

    def _rec_inputs():
        import jax
        import jax.numpy as jnp
        _rk = jax.random.key(seed)
        x = -0.000147625 + 0.999875 * jax.random.normal(jax.random.fold_in(_rk, 1), (64, 3, 224, 224), jnp.float32)
        cls_tok = 0.02 * jax.random.normal(jax.random.fold_in(_rk, 5), (1, 1, 192), jnp.float32)
        return (x, cls_tok)
    x, cls_tok = _rec_inputs()

    def _L0_tok_setup():
        import jax, jax.numpy as jnp
        import numpy as np
        N_PATCHES = 14

        def _patchify(images, n_patches):
            n, c, h, w = images.shape
            ps = h // n_patches
            x = images.reshape(n, c, n_patches, ps, n_patches, ps)
            x = x.transpose(0, 2, 4, 1, 3, 5)
            return x.reshape(n, n_patches * n_patches, c * ps * ps)
        key = jax.random.key(seed)
        k1, k2, k3 = jax.random.split(key, 3)
        batch, c, h, w = (64, 3, 224, 224)
        input_dim = c * (h // N_PATCHES) * (w // N_PATCHES)
        hidden_d = 192
        images = jax.random.normal(k1, (batch, c, h, w), dtype=jnp.float32)
        W = jax.random.normal(k2, (hidden_d, input_dim), dtype=jnp.float32) * input_dim ** (-0.5)
        b = jax.random.normal(k3, (hidden_d,), dtype=jnp.float32) * 0.01
        return {'images': images, 'W': W, 'b': b}
    _L0_tok_all = _L0_tok_setup()
    _L0_tok_in = {k: v for k, v in _L0_tok_all.items() if k in ('W', 'b')}
    del _L0_tok_all

    def _L0_attn_setup():
        import jax, jax.numpy as jnp
        import numpy as np
        MODEL_DIM = 192
        HEADS = 12
        HEAD_DIM = MODEL_DIM // HEADS
        SEQ = 512

        def _rope_tables(seq_len, d):
            i = np.arange(d // 2, dtype=np.float64)
            theta = 10000.0 ** (-2.0 * i / d)
            m = np.arange(1, seq_len + 1, dtype=np.float64)[:, None]
            m_theta = np.repeat(m * theta[None, :], 2, axis=-1)
            return (jnp.asarray(np.cos(m_theta), jnp.float32), jnp.asarray(np.sin(m_theta), jnp.float32))

        def _shuffle(x):
            b, t, d = x.shape
            xp = x.reshape(b, t, d // 2, 2)
            xp = jnp.stack([-xp[..., 1], xp[..., 0]], axis=-1)
            return xp.reshape(b, t, d)

        def _rope(x, cos, sin):
            t = x.shape[-2]
            return x * cos[:t][None] + _shuffle(x) * sin[:t][None]
        key = jax.random.key(seed)
        kx, kq, kk, kv, ko = jax.random.split(key, 5)
        x = jax.random.normal(kx, (4, SEQ, MODEL_DIM), jnp.float32)
        std = 0.02
        W_q = jax.random.normal(kq, (MODEL_DIM, MODEL_DIM), jnp.float32) * std
        W_k = jax.random.normal(kk, (MODEL_DIM, MODEL_DIM), jnp.float32) * std
        W_v = jax.random.normal(kv, (MODEL_DIM, MODEL_DIM), jnp.float32) * std
        W_o = jax.random.normal(ko, (MODEL_DIM, MODEL_DIM), jnp.float32) * std
        return {'x': x, 'W_q': W_q, 'W_k': W_k, 'W_v': W_v, 'W_o': W_o}
    _L0_attn_all = _L0_attn_setup()
    _L0_attn_in = {k: v for k, v in _L0_attn_all.items() if k in ('W_q', 'W_k', 'W_v', 'W_o')}
    del _L0_attn_all

    def _L0_ffn_setup():
        import jax, jax.numpy as jnp
        import numpy as np
        B, T, E = (2, 256, 192)
        H = 768
        N_EXP = 4
        key = jax.random.key(seed)
        ks = jax.random.split(key, 8)
        s_e = 1.0 / np.sqrt(E)
        s_h = 1.0 / np.sqrt(H)
        return {'x': jax.random.normal(ks[0], (B, T, E), dtype=jnp.float32), 'Wg': jax.random.uniform(ks[1], (E, N_EXP), minval=-s_e, maxval=s_e, dtype=jnp.float32), 'bg': jax.random.uniform(ks[2], (N_EXP,), minval=-s_e, maxval=s_e, dtype=jnp.float32), 'W1': jax.random.uniform(ks[3], (N_EXP, E, H), minval=-s_e, maxval=s_e, dtype=jnp.float32), 'b1': jax.random.uniform(ks[4], (N_EXP, H), minval=-s_e, maxval=s_e, dtype=jnp.float32), 'W2': jax.random.uniform(ks[5], (N_EXP, H, E), minval=-s_h, maxval=s_h, dtype=jnp.float32), 'b2': jax.random.uniform(ks[6], (N_EXP, E), minval=-s_h, maxval=s_h, dtype=jnp.float32)}
    _L0_ffn_all = _L0_ffn_setup()
    _L0_ffn_in = {k: v for k, v in _L0_ffn_all.items() if k in ('Wg', 'bg', 'W1', 'b1', 'W2', 'b2')}
    del _L0_ffn_all

    def _L1_attn_setup():
        import jax, jax.numpy as jnp
        import numpy as np
        NUM_HEADS = 12
        NEG = -1000000000.0
        key = jax.random.key(seed)
        ks = jax.random.split(key, 5)
        B, S, D = (4, 512, 192)
        scale = 0.02
        return {'x': jax.random.normal(ks[0], (B, S, D), dtype=jnp.float32), 'wq': jax.random.normal(ks[1], (D, D), dtype=jnp.float32) * scale, 'wk': jax.random.normal(ks[2], (D, D), dtype=jnp.float32) * scale, 'wv': jax.random.normal(ks[3], (D, D), dtype=jnp.float32) * scale, 'wo': jax.random.normal(ks[4], (D, D), dtype=jnp.float32) * scale}
    _L1_attn_all = _L1_attn_setup()
    _L1_attn_in = {k: v for k, v in _L1_attn_all.items() if k in ('wq', 'wk', 'wv', 'wo')}
    del _L1_attn_all

    def _L1_ffn_setup():
        import math
        import jax, jax.numpy as jnp
        import numpy as np
        EMBED_CHOICES = [96, 144, 192]
        RATIO_CHOICES = [2, 3, 4]
        E_MAX = 192
        H_MAX = 768

        def new_gelu(x):
            c = math.sqrt(2.0 / math.pi)
            return 0.5 * x * (1.0 + jnp.tanh(c * (x + 0.044715 * x * x * x)))

        def _mixed_coeffs(alpha_e, alpha_r):
            h_idx = jnp.arange(H_MAX)
            d_idx = jnp.arange(E_MAX)
            C0 = jnp.zeros((H_MAX, E_MAX), jnp.float32)
            c0b = jnp.zeros((H_MAX,), jnp.float32)
            C1 = jnp.zeros((E_MAX, H_MAX), jnp.float32)
            c1b = jnp.zeros((E_MAX,), jnp.float32)
            for i, e in enumerate(EMBED_CHOICES):
                m_in = (d_idx < e).astype(jnp.float32)
                for j, r in enumerate(RATIO_CHOICES):
                    a = alpha_e[i] * alpha_r[j]
                    m_out = (h_idx < r * e).astype(jnp.float32)
                    C0 = C0 + a * (m_out[:, None] * m_in[None, :])
                    c0b = c0b + a * m_out
                    C1 = C1 + a * (m_in[:, None] * m_out[None, :])
                    c1b = c1b + a * m_in
            return (C0, c0b, C1, c1b)
        key = jax.random.key(seed)
        ks = jax.random.split(key, 6)
        x = jax.random.normal(ks[0], (8, 512, E_MAX), jnp.float32)
        w_fc = jax.random.normal(ks[1], (H_MAX, E_MAX), jnp.float32) * 0.02
        b_fc = jnp.zeros((H_MAX,), jnp.float32)
        w_proj = jax.random.normal(ks[2], (E_MAX, H_MAX), jnp.float32) * 0.02
        b_proj = jnp.zeros((E_MAX,), jnp.float32)
        alpha_e = jax.nn.softmax(jax.random.normal(ks[3], (3,), jnp.float32))
        alpha_r = jax.nn.softmax(jax.random.normal(ks[4], (3,), jnp.float32))
        return {'x': x, 'w_fc': w_fc, 'b_fc': b_fc, 'w_proj': w_proj, 'b_proj': b_proj, 'alpha_e': alpha_e, 'alpha_r': alpha_r}
    _L1_ffn_all = _L1_ffn_setup()
    _L1_ffn_in = {k: v for k, v in _L1_ffn_all.items() if k in ('w_fc', 'b_fc', 'w_proj', 'b_proj', 'alpha_e', 'alpha_r')}
    del _L1_ffn_all
    return {'x': x, 'cls_tok': cls_tok, 'L0_tok_W': _L0_tok_in['W'], 'L0_tok_b': _L0_tok_in['b'], 'L0_attn_W_q': _L0_attn_in['W_q'], 'L0_attn_W_k': _L0_attn_in['W_k'], 'L0_attn_W_v': _L0_attn_in['W_v'], 'L0_attn_W_o': _L0_attn_in['W_o'], 'L0_ffn_Wg': _L0_ffn_in['Wg'], 'L0_ffn_bg': _L0_ffn_in['bg'], 'L0_ffn_W1': _L0_ffn_in['W1'], 'L0_ffn_b1': _L0_ffn_in['b1'], 'L0_ffn_W2': _L0_ffn_in['W2'], 'L0_ffn_b2': _L0_ffn_in['b2'], 'L1_attn_wq': _L1_attn_in['wq'], 'L1_attn_wk': _L1_attn_in['wk'], 'L1_attn_wv': _L1_attn_in['wv'], 'L1_attn_wo': _L1_attn_in['wo'], 'L1_ffn_w_fc': _L1_ffn_in['w_fc'], 'L1_ffn_b_fc': _L1_ffn_in['b_fc'], 'L1_ffn_w_proj': _L1_ffn_in['w_proj'], 'L1_ffn_b_proj': _L1_ffn_in['b_proj'], 'L1_ffn_alpha_e': _L1_ffn_in['alpha_e'], 'L1_ffn_alpha_r': _L1_ffn_in['alpha_r']}

def reference(x, cls_tok, L0_tok_W, L0_tok_b, L0_attn_W_q, L0_attn_W_k, L0_attn_W_v, L0_attn_W_o, L0_ffn_Wg, L0_ffn_bg, L0_ffn_W1, L0_ffn_b1, L0_ffn_W2, L0_ffn_b2, L1_attn_wq, L1_attn_wk, L1_attn_wv, L1_attn_wo, L1_ffn_w_fc, L1_ffn_b_fc, L1_ffn_w_proj, L1_ffn_b_proj, L1_ffn_alpha_e, L1_ffn_alpha_r):
    import jax
    import jax.numpy as jnp

    def _L0_tok_ref(images, W, b):
        import jax, jax.numpy as jnp
        import numpy as np
        N_PATCHES = 14

        def _patchify(images, n_patches):
            n, c, h, w = images.shape
            ps = h // n_patches
            x = images.reshape(n, c, n_patches, ps, n_patches, ps)
            x = x.transpose(0, 2, 4, 1, 3, 5)
            return x.reshape(n, n_patches * n_patches, c * ps * ps)
        patches = _patchify(images, N_PATCHES)
        tokens = jnp.einsum('npd,hd->nph', patches, W) + b
        return tokens

    def _L0_attn_ref(x, W_q, W_k, W_v, W_o):
        import jax, jax.numpy as jnp
        import numpy as np
        MODEL_DIM = 192
        HEADS = 12
        HEAD_DIM = MODEL_DIM // HEADS
        SEQ = 512

        def _rope_tables(seq_len, d):
            i = np.arange(d // 2, dtype=np.float64)
            theta = 10000.0 ** (-2.0 * i / d)
            m = np.arange(1, seq_len + 1, dtype=np.float64)[:, None]
            m_theta = np.repeat(m * theta[None, :], 2, axis=-1)
            return (jnp.asarray(np.cos(m_theta), jnp.float32), jnp.asarray(np.sin(m_theta), jnp.float32))

        def _shuffle(x):
            b, t, d = x.shape
            xp = x.reshape(b, t, d // 2, 2)
            xp = jnp.stack([-xp[..., 1], xp[..., 0]], axis=-1)
            return xp.reshape(b, t, d)

        def _rope(x, cos, sin):
            t = x.shape[-2]
            return x * cos[:t][None] + _shuffle(x) * sin[:t][None]
        b, t, d = x.shape
        cos, sin = _rope_tables(t, d)
        Q = _rope(x @ W_q.T, cos, sin)
        K = _rope(x @ W_k.T, cos, sin)
        V = x @ W_v.T
        Qh = Q.reshape(b, t, HEADS, HEAD_DIM)
        Kh = K.reshape(b, t, HEADS, HEAD_DIM)
        Vh = V.reshape(b, t, HEADS, HEAD_DIM)
        scores = jnp.einsum('bthd,bshd->bhts', Qh, Kh) / jnp.sqrt(jnp.float32(HEAD_DIM))
        mask = jnp.triu(jnp.ones((t, t), bool), k=1)
        scores = jnp.where(mask[None, None], -jnp.inf, scores)
        attn = jax.nn.softmax(scores, axis=-1)
        out = jnp.einsum('bhts,bshd->bthd', attn, Vh).reshape(b, t, d)
        return out @ W_o.T

    def _L0_ffn_ref(x, Wg, bg, W1, b1, W2, b2):
        import jax, jax.numpy as jnp
        import numpy as np
        B, T, E = (2, 256, 192)
        H = 768
        N_EXP = 4
        gate_logits = jnp.einsum('bte,en->btn', x, Wg) + bg
        top = jnp.argmax(gate_logits, axis=-1)
        h = jax.nn.gelu(jnp.einsum('bte,neh->nbth', x, W1) + b1[:, None, None, :], approximate=False)
        y = jnp.einsum('nbth,nhe->nbte', h, W2) + b2[:, None, None, :]
        onehot = jax.nn.one_hot(top, N_EXP, dtype=x.dtype)
        out = jnp.einsum('nbte,btn->bte', y, onehot)
        return out

    def _L1_attn_ref(x, wq, wk, wv, wo):
        import jax, jax.numpy as jnp
        import numpy as np
        NUM_HEADS = 12
        NEG = -1000000000.0
        B, S, D = x.shape
        H = NUM_HEADS
        dh = D // H

        def proj(w):
            return (x @ w.T).reshape(B, S, H, dh).transpose(0, 2, 1, 3)
        q, k, v = (proj(wq), proj(wk), proj(wv))
        score = jnp.einsum('bhqd,bhkd->bhqk', q, k) / jnp.float32(np.sqrt(dh))
        causal = jnp.triu(jnp.ones((S, S), dtype=bool), k=1)
        score = score + jnp.where(causal, jnp.float32(NEG), jnp.float32(0.0))
        attn = jax.nn.softmax(score, axis=-1)
        out = jnp.einsum('bhqk,bhkd->bhqd', attn, v)
        out = out.transpose(0, 2, 1, 3).reshape(B, S, D)
        return out @ wo.T

    def _L1_ffn_ref(x, w_fc, b_fc, w_proj, b_proj, alpha_e, alpha_r):
        import math
        import jax, jax.numpy as jnp
        import numpy as np
        EMBED_CHOICES = [96, 144, 192]
        RATIO_CHOICES = [2, 3, 4]
        E_MAX = 192
        H_MAX = 768

        def new_gelu(x):
            c = math.sqrt(2.0 / math.pi)
            return 0.5 * x * (1.0 + jnp.tanh(c * (x + 0.044715 * x * x * x)))

        def _mixed_coeffs(alpha_e, alpha_r):
            h_idx = jnp.arange(H_MAX)
            d_idx = jnp.arange(E_MAX)
            C0 = jnp.zeros((H_MAX, E_MAX), jnp.float32)
            c0b = jnp.zeros((H_MAX,), jnp.float32)
            C1 = jnp.zeros((E_MAX, H_MAX), jnp.float32)
            c1b = jnp.zeros((E_MAX,), jnp.float32)
            for i, e in enumerate(EMBED_CHOICES):
                m_in = (d_idx < e).astype(jnp.float32)
                for j, r in enumerate(RATIO_CHOICES):
                    a = alpha_e[i] * alpha_r[j]
                    m_out = (h_idx < r * e).astype(jnp.float32)
                    C0 = C0 + a * (m_out[:, None] * m_in[None, :])
                    c0b = c0b + a * m_out
                    C1 = C1 + a * (m_in[:, None] * m_out[None, :])
                    c1b = c1b + a * m_in
            return (C0, c0b, C1, c1b)
        C0, c0b, C1, c1b = _mixed_coeffs(alpha_e, alpha_r)
        W0 = w_fc * C0
        b0 = b_fc * c0b
        h = jnp.einsum('bte,he->bth', x, W0) + b0
        h = new_gelu(h)
        W1 = w_proj * C1
        b1 = b_proj * c1b
        out = jnp.einsum('bth,eh->bte', h, W1) + b1
        return out
    h = _L0_tok_ref(x, L0_tok_W, L0_tok_b)
    h = jnp.concatenate([jnp.broadcast_to(cls_tok, (h.shape[0], 1, h.shape[2])), h], axis=1)
    h = h + _L0_attn_ref(_layernorm(h, axis=-1), L0_attn_W_q, L0_attn_W_k, L0_attn_W_v, L0_attn_W_o)
    h = h + _L0_ffn_ref(_layernorm(h, axis=-1), L0_ffn_Wg, L0_ffn_bg, L0_ffn_W1, L0_ffn_b1, L0_ffn_W2, L0_ffn_b2)
    h = h + _L1_attn_ref(_layernorm(h, axis=-1), L1_attn_wq, L1_attn_wk, L1_attn_wv, L1_attn_wo)
    h = h + _L1_ffn_ref(_layernorm(h, axis=-1), L1_ffn_w_fc, L1_ffn_b_fc, L1_ffn_w_proj, L1_ffn_b_proj, L1_ffn_alpha_e, L1_ffn_alpha_r)
    return h

_drawn_inputs = setup_inputs


def setup_inputs(seed=0):
    import zlib

    import numpy as np

    out = dict(_drawn_inputs(seed))
    spreads = {'L1_ffn_b_fc': (0.0, 0.41), 'L1_ffn_b_proj': (0.0, 0.1)}
    factors = {'cls_tok': 3.189,
     'L0_tok_b': 3.927,
     'L0_attn_W_q': 8.0,
     'L0_attn_W_k': 8.0,
     'L0_ffn_b1': 3.899,
     'L1_attn_wq': 8.0,
     'L1_attn_wk': 8.0,
     'L1_attn_wv': 4.226,
     'L1_attn_wo': 4.258,
     'L1_ffn_alpha_r': 4.658}
    for name, (base, spread) in spreads.items():
        noise = np.random.default_rng([zlib.crc32(name.encode()), seed]).standard_normal(out[name].shape)
        drawn = base * np.exp(spread * noise) if base else spread * noise
        out[name] = jnp.asarray(drawn.astype(out[name].dtype))
    for name, factor in factors.items():
        out[name] = (out[name] * factor).astype(out[name].dtype)
    return out
```

```python
from contextlib import ExitStack

import numpy as np

import concourse.bass as bass
from concourse import mybir

F32 = mybir.dt.float32
BF16 = mybir.dt.bfloat16
ALU = mybir.AluOpType
ACT = mybir.ActivationFunctionType
AX_X = mybir.AxisListType.X

P = 128
IMG = 64
TOK = 197
PADT = 2 * P
T1 = TOK - P
D = 192
KC = 96
PATCH = 768
PC = PATCH // P
HEADS = 12
DH = D // HEADS
HIDDEN = 768
HC = HIDDEN // P
EXPERTS = 4
SLOTS = 6
SK = SLOTS * DH
MROWS = 3
SCALE = float(DH) ** -0.5
EPS = 1e-5
NEG = -1e9
UNROLL = 2
E_CHOICES = (96, 144, 192)
R_CHOICES = (2, 3, 4)


def at_least(eng, sem, value):
    if isinstance(value, int) and value <= 0:
        return
    eng.wait_ge(sem, value)


def wait_apart(eng, sem, value, passed):
    if isinstance(value, int) and value <= 0:
        return
    eng.wait_ge(sem, value)
    if not isinstance(value, int):
        eng.sem_inc(passed, 1)


def pipeline(eng, images, depth, lead, step):
    steps = images + depth - 1
    full = lead + (images - 2 - lead) // UNROLL * UNROLL
    for s in range(lead):
        step(s, s % UNROLL)
    with eng.Fori(lead, full, UNROLL) as s:
        for u in range(UNROLL):
            step(s + u, u)
    for s in range(full, steps):
        step(s, s % UNROLL)


def attention_phase(nc, name, x_dram, h_in, h_out, w, tables, embed):
    with ExitStack() as ctx:
        def sb(n, shape, dt=F32):
            return ctx.enter_context(nc.sbuf_tensor(f"{name}_{n}", shape, dt))

        def sem(n):
            return ctx.enter_context(nc.semaphore(f"{name}_{n}"))

        def psum(n, shape, dt=F32):
            return ctx.enter_context(nc.psum_tensor(f"{name}_{n}", shape, dt))

        rope = tables["cos"] is not None
        ident = sb("ident", [P, P])
        ident_b = sb("ident_b", [P, P], BF16)
        mask_q = sb("mask_q", [P, P], BF16)
        mask_k = sb("mask_k", [P, P], BF16)
        neg_half = sb("neg_half", [P, 2])
        wqk = sb("wqk", [KC, 2, 2 * D])
        wv = sb("wv", [KC, 2, D])
        wo = sb("wo", [P, 3, D])
        if rope:
            cos = sb("cos", [P, 2, D])
            sin = sb("sin", [P, 2, D])
        if embed:
            w_tok = sb("w_tok", [P, PC, D])
            tok_add = sb("tok_add", [P, 2, D])
            patches = sb("patches", [P, 2, PC, PADT])
        h = sb("h", [P, 2, 2, D])
        stats = sb("stats", [P, 2, 6])
        mv = sb("mv", [P, 2, 2])
        veps = sb("veps", [P, 2])
        rstd = sb("rstd", [P, 2])
        xn = sb("xn", [P, 2, D])
        xT = sb("xT", [KC, 2, PADT])
        rc = sb("rc", [P, 2 * D])
        rs = sb("rs", [P, 2 * D])
        qk = sb("qk", [P, 2, 2 * D])
        rest = sb("rest", [P, 2, 2 * D])
        stack = sb("stack", [P, 2, 2, HEADS, SLOTS, DH], BF16)
        QT = [sb(f"QT{u}", [P, HEADS, TOK], BF16) for u in range(2)]
        KT = [sb(f"KT{u}", [P, HEADS, TOK], BF16) for u in range(2)]
        V = [sb(f"V{u}", [P, 2, HEADS, 2 * DH]) for u in range(2)]
        mx = sb("mx", [P, 2, HEADS])
        nm = sb("nm", [P, 2, HEADS])
        nm_rest = sb("nm_rest", [P, 2, HEADS])
        nm_parts = sb("nm_parts", [P, 2, MROWS, HEADS], BF16)
        mT = sb("mT", [MROWS * HEADS, TOK], BF16)
        probs0 = sb("probs0", [P, HEADS, TOK])
        probs1 = sb("probs1", [T1, HEADS, T1])
        inv = sb("inv", [P, 3, TOK])
        inv_b = sb("inv_b", [P, 3, TOK])
        OT = sb("OT", [P, 3, PADT])
        h_res = sb("h_res", [P, 2, 2, D])
        y = sb("y", [P, 2, 2, D])
        ps_front = psum("ps_front", [P, 512])
        ps_qk = psum("ps_qk", [P, 512])
        ps_b = [psum(f"ps_b{n}", [P, 512]) for n in range(2)]
        ps_c = [psum(f"ps_c{n}", [P, 512]) for n in range(2)]
        ps_o = psum("ps_o", [P, 2, 512])

        passed_sp, passed_pool, passed_dve, passed_pe = (sem(f"passed_{e}") for e in ("sp", "pool", "dve", "pe"))
        weights_in = sem("weights_in")
        n_weights = 3 + 2 * rope + 2 * embed + 1
        ident_sem, consts = sem("ident"), sem("consts")
        patches_in, h_in_sem = sem("patches_in"), sem("h_in")
        tok_done, h_ready, h_kept = sem("tok_done"), sem("h_ready"), sem("h_kept")
        stats_done, mv_done, veps_done, rstd_done = sem("stats_done"), sem("mv_done"), sem("veps_done"), sem("rstd_done")
        xn_done, xt_ps, xt_done = sem("xn_done"), sem("xt_ps"), sem("xt_done")
        qk_ps, qk_taken, v_ps, v_done = sem("qk_ps"), sem("qk_taken"), sem("v_ps"), sem("v_done")
        rope_done, qk_done = sem("rope_done"), sem("qk_done")
        hi_done, rest_done, mid_done, lo_done, dup_done = sem("hi_done"), sem("rest_done"), sem("mid_done"), sem("lo_done"), sem("dup_done")
        stack_ps, stack_act, stack_dve = sem("stack_ps"), sem("stack_act"), sem("stack_dve")
        sq_ps, max_done = sem("sq_ps"), sem("max_done")
        nm_sem, mt_ps, mt_done, mrows_in = sem("nm"), sem("mt_ps"), sem("mt_done"), sem("mrows_in")
        sk_ps, exp_done = sem("sk_ps"), sem("exp_done")
        av_ps, inv_done, invb_done, ot_done = sem("av_ps"), sem("inv_done"), sem("invb_done"), sem("ot_done")
        y_ps, hres_in, y_done, y_out = sem("y_ps"), sem("hres_in"), sem("y_done"), sem("y_out")

        CONSTS = 11
        NT = 6
        ACT_T = (0, 1, 3, 4)
        NS = 8
        block = ctx.enter_context(nc.Block())

        def score_banks(k):
            return (range(2 * k, 2 * k + 2), False) if k < 6 else (range(6 * (k - 6), 6 * (k - 5)), True)

        def four(ap):
            return ap.rearrange("p (j h d) -> p j h d", j=2, h=HEADS)

        @block.sync
        def _(sp):
            sp.dma_start(wqk[:], w["qk"]).then_inc(weights_in, 16)
            sp.dma_start(wv[:], w["v"]).then_inc(weights_in, 16)
            sp.dma_start(wo[:], w["o"]).then_inc(weights_in, 16)
            sp.dma_start(ident[:], tables["ident"]).then_inc(weights_in, 16)
            if rope:
                sp.dma_start(cos[:], tables["cos"]).then_inc(weights_in, 16)
                sp.dma_start(sin[:], tables["sin"]).then_inc(weights_in, 16)
            if embed:
                sp.dma_start(w_tok[:], w["tok"]).then_inc(weights_in, 16)
                sp.dma_start(tok_add[:], w["tok_add"]).then_inc(weights_in, 16)

            def step(s, u):
                def load_front(i, p):
                    if embed:
                        wait_apart(sp, tok_done, i - 1, passed_sp)
                        wait_apart(sp, patches_in, 16 * i, passed_sp)
                        sp.dma_start(patches[:, p], x_dram[i]).then_inc(patches_in, 16)
                    else:
                        wait_apart(sp, xn_done, 2 * (i - 1), passed_sp)
                        wait_apart(sp, h_in_sem, 16 * i, passed_sp)
                        sp.dma_start(h[:, p], h_in[i]).then_inc(h_in_sem, 16)
                if isinstance(s, int) and s == 0:
                    load_front(0, 0)
                    load_front(1, 1)
                elif not isinstance(s, int) or s + 1 < IMG:
                    load_front(s + 1, 1 - u)
                if embed and (not isinstance(s, int) or s < IMG):
                    wait_apart(sp, h_kept, 16 * s, passed_sp)
                    wait_apart(sp, h_ready, 2 * (s + 1), passed_sp)
                    sp.dma_start(h_in[s], h[:, u]).then_inc(h_kept, 16)
                if not isinstance(s, int) or 1 <= s <= IMG:
                    i, p = s - 1, 1 - u
                    if embed:
                        wait_apart(sp, h_kept, 16 * (i + 1), passed_sp)
                    wait_apart(sp, hres_in, 16 * i, passed_sp)
                    wait_apart(sp, y_done, i - 1, passed_sp)
                    sp.dma_start(h_res[:, p], h_in[i]).then_inc(hres_in, 16)
                    wait_apart(sp, mrows_in, 16 * i, passed_sp)
                    wait_apart(sp, mt_done, i + 1, passed_sp)
                    sp.dma_start(QT[p][SK:SK + MROWS], mT[:]).then_inc(mrows_in, 16)
                if not isinstance(s, int) or s >= 2:
                    i, p = s - 2, u
                    wait_apart(sp, y_out, 16 * i, passed_sp)
                    wait_apart(sp, y_done, i + 1, passed_sp)
                    sp.dma_start(h_out[i], y[:, p]).then_inc(y_out, 16)
            pipeline(sp, IMG, 3, 4, step)
            sp.wait_ge(y_out, 16 * IMG)
            if embed:
                sp.wait_ge(h_kept, 16 * IMG)

        @block.gpsimd
        def _(pool):
            setup = [lambda: nc.gpsimd.memset(mask_q[:], 0.0), lambda: nc.gpsimd.memset(mask_k[:], 0.0),
                     lambda: nc.gpsimd.memset(neg_half[:], -0.5), lambda: nc.gpsimd.memset(OT[:], 0.0),
                     lambda: nc.gpsimd.memset(mx[:], 0.0)]
            for n, fill in enumerate(setup):
                at_least(pool, consts, n)
                fill().then_inc(consts, 1)
            for u in range(2):
                pool.wait_ge(consts, 5 + 2 * u)
                nc.gpsimd.memset(V[u][:], 1.0).then_inc(consts, 1)
                pool.wait_ge(consts, 6 + 2 * u)
                nc.gpsimd.memset(KT[u][SK:P], 1.0).then_inc(consts, 1)
            pool.wait_ge(consts, 9)
            nc.gpsimd.affine_select(out=mask_q[:], in_=mask_q[:], compare_op=ALU.is_ge, fill=NEG, base=0,
                                    pattern=[[-1, P]], channel_multiplier=1).then_inc(consts, 1)
            pool.wait_ge(consts, 10)
            nc.gpsimd.affine_select(out=mask_k[:], in_=mask_k[:], compare_op=ALU.is_ge, fill=NEG, base=0,
                                    pattern=[[1, P]], channel_multiplier=-1).then_inc(consts, 1)
            pool.wait_ge(consts, CONSTS)

            def step(s, u):
                if not isinstance(s, int) or s < IMG:
                    i = s
                    wait_apart(pool, mv_done, 2 * (i + 1), passed_pool)
                    nc.gpsimd.tensor_scalar_add(veps[:], mv[:, :, 1], EPS).then_inc(veps_done, 1)
                    pool.wait_ge(veps_done, i + 1)
                    nc.gpsimd.tensor_tensor(rstd[:], veps[:], neg_half[:], ALU.pow).then_inc(rstd_done, 1)
                    for t in range(2):
                        n = 2 * i + t + 1
                        if rope:
                            pool.wait_ge(rope_done, 3 * n)
                            nc.gpsimd.tensor_tensor(qk[:, t], rc[:], rs[:], ALU.add).then_inc(qk_done, 1)
                        pool.wait_ge(hi_done, n)
                        pool.wait_ge(qk_done, n)
                        hi = stack[:, t, :, :, 0, :]
                        at_least(pool, lo_done, 2 * (n - 2))
                        nc.gpsimd.tensor_tensor(four(rest[:, t]), four(qk[:, t]), hi, ALU.subtract)\
                            .then_inc(rest_done, 1)
                        pool.wait_ge(mid_done, n)
                        pool.wait_ge(rest_done, n)
                        for j, slot in ((0, 4), (1, 5)):
                            nc.gpsimd.tensor_tensor(stack[:, t, j, :, slot, :],
                                                    four(rest[:, t])[:, j], stack[:, t, j, :, 1 + j, :],
                                                    ALU.subtract).then_inc(lo_done, 1)
                if not isinstance(s, int) or 1 <= s <= IMG:
                    i = s - 1
                    wait_apart(pool, max_done, NS * (i + 1), passed_pool)
                    wait_apart(pool, mt_ps, i, passed_pool)
                    nc.gpsimd.tensor_scalar_mul(nm[:], mx[:], -1.0).then_inc(nm_sem, 1)
                    wait_apart(pool, nm_sem, 5 * i + 1, passed_pool)
                    nc.gpsimd.tensor_copy(nm_parts[:, :, 0], nm[:]).then_inc(nm_sem, 1)
                    pool.wait_ge(nm_sem, 5 * i + 2)
                    nc.gpsimd.tensor_tensor(nm_rest[:], nm[:], nm_parts[:, :, 0], ALU.subtract).then_inc(nm_sem, 1)
                    wait_apart(pool, nm_sem, 5 * i + 3, passed_pool)
                    nc.gpsimd.tensor_copy(nm_parts[:, :, 1], nm_rest[:]).then_inc(nm_sem, 1)
                    pool.wait_ge(nm_sem, 5 * i + 4)
                    nc.gpsimd.tensor_tensor(nm_parts[:, :, 2], nm_rest[:], nm_parts[:, :, 1], ALU.subtract)\
                        .then_inc(nm_sem, 1)
            pipeline(pool, IMG, 3, 4, step)

        @block.scalar
        def _(act):
            act.wait_ge(weights_in, 16 * (n_weights))
            nc.scalar.copy(ident_b[:], ident[:]).then_inc(ident_sem, 1)
            act.wait_ge(consts, CONSTS)

            def step(s, u):
                if not isinstance(s, int) or s >= 2:
                    i = s - 2
                    for k in range(NS):
                        heads, small = score_banks(k)
                        act.wait_ge(sk_ps, NS * i + k + 1)
                        at_least(act, av_ps, i)
                        n = len(heads)
                        if not small:
                            nc.scalar.activation(probs0[:, heads[0]:heads[0] + n],
                                                 ps_c[k % 2][:, 0:n * TOK].rearrange("p (h q) -> p h q", h=n),
                                                 ACT.Exp, scale=SCALE).then_inc(exp_done, 1)
                        else:
                            nc.scalar.activation(probs1[:, heads[0]:heads[0] + n],
                                                 ps_c[k % 2][0:T1, 0:n * T1].rearrange("p (h q) -> p h q", h=n),
                                                 ACT.Exp, scale=SCALE).then_inc(exp_done, 1)
                if not isinstance(s, int) or s < IMG:
                    i = s
                    act.wait_ge(xt_ps, i + 1)
                    at_least(act, v_ps, i)
                    nc.scalar.copy(xT[:], ps_front[0:KC, :].rearrange("p (c t) -> p c t", c=2)).then_inc(xt_done, 1)
                if not isinstance(s, int) or 1 <= s <= IMG:
                    i, p = s - 1, 1 - u
                    for n, k in enumerate(ACT_T):
                        act.wait_ge(stack_ps, NT * i + k + 1)
                        at_least(act, sk_ps, NS * (i - 1))
                        dst = QT[p] if k < 3 else KT[p]
                        hh = 4 * (k % 3)
                        nc.scalar.copy(dst[0:SK, hh:hh + 4],
                                       ps_b[k % 2][0:SK, :].bitcast(BF16).rearrange("p (h t) -> p h t", h=4)[:, :, 0:TOK])\
                            .then_inc(stack_act, 1)
                if not isinstance(s, int) or s < IMG:
                    i = s
                    act.wait_ge(v_ps, i + 1)
                    at_least(act, av_ps, i - 1)
                    nc.scalar.copy(V[u][:, :, :, 0:DH],
                                   ps_front[:, 0:2 * D].rearrange("p (t h d) -> p t h d", t=2, h=HEADS))\
                        .then_inc(v_done, 1)
                    for t in range(2):
                        n = 2 * i + t + 1
                        act.wait_ge(qk_done, n)
                        at_least(act, stack_ps, NT * i)
                        nc.scalar.copy(stack[:, t, :, :, 0, :], four(qk[:, t])).then_inc(hi_done, 1)
                        act.wait_ge(rest_done, n)
                        nc.scalar.copy(stack[:, t, 0, :, 1, :], four(rest[:, t])[:, 0])
                        nc.scalar.copy(stack[:, t, 1, :, 2, :], four(rest[:, t])[:, 1]).then_inc(mid_done, 1)
                if not isinstance(s, int) or 1 <= s <= IMG:
                    i = s - 1
                    act.wait_ge(mt_ps, i + 1)
                    at_least(act, mrows_in, 16 * i)
                    m_bank = ps_b[0][0:MROWS * HEADS, 0:PADT // 2].bitcast(BF16)
                    nc.scalar.copy(mT[:, T1:TOK], m_bank[:, 0:P])
                    nc.scalar.copy(mT[:, 0:T1], m_bank[:, P:TOK]).then_inc(mt_done, 1)
            pipeline(act, IMG, 3, 4, step)

        @block.vector
        def _(dve):
            dve.wait_ge(weights_in, 16 * (n_weights))
            dve.wait_ge(consts, CONSTS)

            def step(s, u):
                if not isinstance(s, int) or s < IMG:
                    i = s
                    if embed:
                        dve.wait_ge(tok_done, i + 1)
                        at_least(dve, h_kept, 16 * (i - 1))
                        nc.vector.tensor_tensor(h[:, u], ps_front[:, 0:2 * D].rearrange("p (t d) -> p t d", t=2),
                                                tok_add[:], ALU.add).then_inc(h_ready, 2)
                        dve.wait_ge(h_ready, 2 * (i + 1))
                    else:
                        dve.wait_ge(h_in_sem, 16 * (i + 1))
                    for t in range(2):
                        nc.vector.bn_stats(stats[:, t], h[:, u, t]).then_inc(stats_done, 1)
                    wait_apart(dve, stats_done, 2 * (i + 1), passed_dve)
                    wait_apart(dve, veps_done, i, passed_dve)
                    for t in range(2):
                        nc.vector.bn_aggr(mv[:, t], stats[:, t]).then_inc(mv_done, 1)
                if not isinstance(s, int) or s < IMG:
                    i = s
                    dve.wait_ge(rstd_done, i + 1)
                    at_least(dve, xt_ps, i)
                    for t in range(2):
                        nc.vector.tensor_scalar(xn[:, t], h[:, u, t], mv[:, t, 0:1], rstd[:, t:t + 1],
                                                ALU.subtract, ALU.mult).then_inc(xn_done, 1)
                if not isinstance(s, int) or 1 <= s <= IMG:
                    i, p = s - 1, 1 - u
                    for n, k in enumerate(k for k in range(NT) if k not in ACT_T):
                        dve.wait_ge(stack_ps, NT * i + k + 1)
                        at_least(dve, sk_ps, NS * (i - 1))
                        dst = QT[p] if k < 3 else KT[p]
                        hh = 4 * (k % 3)
                        nc.vector.tensor_copy(dst[0:SK, hh:hh + 4],
                                              ps_b[k % 2][0:SK, :].bitcast(BF16).rearrange("p (h t) -> p h t", h=4)[:, :, 0:TOK])\
                            .then_inc(stack_dve, 1)
                if not isinstance(s, int) or s >= 2:
                    i, p = s - 2, u
                    dve.wait_ge(av_ps, i + 1)
                    at_least(dve, invb_done, i)
                    nc.vector.reciprocal(inv[:, 0:2], ps_o[:, 0, 0:2 * TOK].rearrange("p (g q) -> p g q", g=2))
                    nc.vector.reciprocal(inv[:, 2], ps_o[:, 1, 0:TOK]).then_inc(inv_done, 1)
                    at_least(dve, ot_done, 2 * i)
                    wait_apart(dve, inv_done, i + 1, passed_dve)
                    nc.vector.stream_shuffle(inv_b[:], inv[:], [DH] * 32).then_inc(invb_done, 1)
                    dve.wait_ge(invb_done, i + 1)
                    at_least(dve, y_ps, i)
                    nc.vector.tensor_tensor(OT[:, 0:2, 0:TOK], ps_o[:, 0, 0:2 * TOK].rearrange("p (g q) -> p g q", g=2),
                                            inv_b[:, 0:2], ALU.mult).then_inc(ot_done, 1)
                    nc.vector.tensor_tensor(OT[:, 2, 0:TOK], ps_o[:, 1, 0:TOK], inv_b[:, 2], ALU.mult).then_inc(ot_done, 1)
                if not isinstance(s, int) or s < IMG:
                    i = s
                    for t in range(2):
                        n = 2 * i + t + 1
                        dve.wait_ge(qk_ps, n)
                        q = ps_qk[:, 0:2 * D]
                        if rope:
                            at_least(dve, qk_done, n - 1)
                            q3 = q.rearrange("p (j d) -> p j d", j=2)
                            bc = cos[:, t, None, :].broadcast_to([P, 2, D])
                            nc.vector.tensor_tensor(rc[:].rearrange("p (j d) -> p j d", j=2), q3, bc, ALU.mult)\
                                .then_inc(rope_done, 1)
                            for e in range(2):
                                qs = q.rearrange("p (j d e) -> p j d e", j=2, e=2)[:, :, :, 1 - e]
                                sn = sin[:, t, :].rearrange("p (d e) -> p d e", e=2)[:, None, :, e].broadcast_to([P, 2, D // 2])
                                nc.vector.tensor_tensor(rs[:].rearrange("p (j d e) -> p j d e", j=2, e=2)[:, :, :, e],
                                                        qs, sn, ALU.mult).then_inc(rope_done, 1)
                        else:
                            at_least(dve, rest_done, n - 2)
                            at_least(dve, hi_done, n - 2)
                            nc.vector.tensor_copy(qk[:, t], q).then_inc(qk_done, 1)
                if not isinstance(s, int) or 1 <= s <= IMG:
                    i = s - 1
                    at_least(dve, nm_sem, 5 * i)
                    for k in range(NS):
                        heads, small = score_banks(k)
                        n = len(heads)
                        dve.wait_ge(sq_ps, NS * i + k + 1)
                        if not small:
                            nc.vector.tensor_reduce(mx[:, 0, heads[0]:heads[0] + n],
                                                    ps_b[k % 2][:, 0:n * TOK].rearrange("p (h q) -> p h q", h=n),
                                                    AX_X, ALU.max).then_inc(max_done, 1)
                        else:
                            nc.vector.tensor_reduce(mx[0:T1, 1, heads[0]:heads[0] + n],
                                                    ps_b[k % 2][0:T1, 0:n * T1].rearrange("p (h q) -> p h q", h=n),
                                                    AX_X, ALU.max).then_inc(max_done, 1)
                if not isinstance(s, int) or s < IMG:
                    i = s
                    for t in range(2):
                        n = 2 * i + t + 1
                        dve.wait_ge(mid_done, n)
                        st = stack[:, t]
                        for j, slot, src in ((0, 2, 0), (0, 3, 1), (0, 5, 0), (1, 1, 0), (1, 3, 2), (1, 4, 0)):
                            nc.vector.tensor_copy(st[:, j, :, slot], st[:, j, :, src]).then_inc(dup_done, 1)
                if not isinstance(s, int) or s >= 2:
                    i, p = s - 2, u
                    dve.wait_ge(y_ps, i + 1)
                    dve.wait_ge(hres_in, 16 * (i + 1))
                    at_least(dve, y_out, 16 * (i - 1))
                    nc.vector.tensor_tensor(y[:, p], ps_c[0][:, 0:2 * D].rearrange("p (t d) -> p t d", t=2),
                                            h_res[:, p], ALU.add).then_inc(y_done, 1)
            pipeline(dve, IMG, 3, 4, step)

        @block.tensor
        def _(pe):
            pe.wait_ge(weights_in, 16 * (n_weights))
            pe.wait_ge(consts, CONSTS)
            pe.wait_ge(ident_sem, 1)
            mm = nc.tensor.matmul

            def scores(bank, k, left, right, rows, first, mask, big):
                heads, small = score_banks(k)
                (l0, l1), (r0, r1), m0 = big if not small else first
                width = r1 - r0
                for n, hd in enumerate(heads):
                    mm(bank[0:l1 - l0, n * width:(n + 1) * width], left[0:rows, hd, l0:l1], right[0:rows, hd, r0:r1],
                       start=(n == 0), stop=False, skip_group_check=True)
                span = width - m0 if m0 else min(width, l1 - l0)
                out = bank[0:l1 - l0, 0:len(heads) * width].rearrange("p (h q) -> p h q", h=len(heads))[:, :, m0:m0 + span]
                rhs = mask[0:l1 - l0, None, 0:span].broadcast_to([l1 - l0, len(heads), span])
                return mm(out, ident_b[0:l1 - l0, 0:l1 - l0], rhs, start=False, stop=True, skip_group_check=True)

            def step(s, u):
                do_a = not isinstance(s, int) or s < IMG
                do_b = not isinstance(s, int) or 1 <= s <= IMG
                do_c = not isinstance(s, int) or s >= 2

                def c_scores(ks):
                    i, p = s - 2, u
                    pe.wait_ge(mrows_in, 16 * (i + 1))
                    for k in ks:
                        if k < 2:
                            at_least(pe, y_done, i)
                            at_least(pe, exp_done, NS * i)
                        else:
                            pe.wait_ge(exp_done, NS * i + k - 1)
                        scores(ps_c[k % 2], k, KT[p], QT[p], SK + MROWS, ((P, TOK), (P, TOK), 0), mask_k,
                               ((0, P), (0, TOK), 0)).then_inc(sk_ps, 1)

                def c_values():
                    i, p = s - 2, u
                    pe.wait_ge(exp_done, NS * (i + 1))
                    pe.wait_ge(v_done, i + 1)
                    at_least(pe, ot_done, 2 * i)
                    for hd in range(HEADS):
                        g, q0 = hd // 4, 32 * (hd % 4)
                        o = ps_o[q0:q0 + 2 * DH, g // 2, (g % 2) * TOK:(g % 2 + 1) * TOK]
                        mm(o, V[p][:, 0, hd], probs0[:, hd], start=True, stop=True, tile_position=(0, q0))
                        last = mm(o[:, P:TOK], V[p][0:T1, 1, hd], probs1[:, hd], start=False, stop=True,
                                  tile_position=(0, q0), skip_group_check=True)
                    last.then_inc(av_ps, 1)

                def c_out():
                    i = s - 2
                    pe.wait_ge(ot_done, 2 * (i + 1))
                    for t in range(2):
                        for c in range(3):
                            last = mm(ps_c[0][:, t * D:(t + 1) * D], OT[:, c, t * P:(t + 1) * P], wo[:, c],
                                      start=(c == 0), stop=(c == 2))
                    last.then_inc(y_ps, 1)

                def a_embed():
                    i = s
                    pe.wait_ge(patches_in, 16 * (i + 1))
                    at_least(pe, v_done, i)
                    for t in range(2):
                        for c in range(PC):
                            last = mm(ps_front[:, t * D:(t + 1) * D], patches[:, u, c, t * P:(t + 1) * P], w_tok[:, c],
                                      start=(c == 0), stop=(c == PC - 1))
                    last.then_inc(tok_done, 1)

                def a_transpose():
                    i = s
                    pe.wait_ge(xn_done, 2 * (i + 1))
                    if embed:
                        pe.wait_ge(h_ready, 2 * (i + 1))
                    else:
                        at_least(pe, v_done, i)
                    for c in range(2):
                        for t in range(2):
                            last = nc.tensor.transpose(ps_front[0:KC, c * PADT + t * P:c * PADT + (t + 1) * P],
                                                       xn[:, t, c * KC:(c + 1) * KC], ident[:])
                    last.then_inc(xt_ps, 1)

                def a_qk(t):
                    i = s
                    pe.wait_ge(xt_done, i + 1)
                    if rope:
                        at_least(pe, rope_done, 3 * (2 * i + t))
                    else:
                        at_least(pe, qk_done, 2 * i + t)
                    for c in range(2):
                        last = mm(ps_qk[:, 0:2 * D], xT[:, c, t * P:(t + 1) * P], wqk[:, c], start=(c == 0), stop=(c == 1))
                    last.then_inc(qk_ps, 1)

                def a_v():
                    for t in range(2):
                        for c in range(2):
                            last = mm(ps_front[:, t * D:(t + 1) * D], xT[:, c, t * P:(t + 1) * P], wv[:, c],
                                      start=(c == 0), stop=(c == 1))
                    last.then_inc(v_ps, 1)

                def b_stack(k):
                    i = s - 1
                    n_act = [n for n, a in enumerate(ACT_T) if a == k - 2]
                    if k == 0:
                        pe.wait_ge(lo_done, 4 * (i + 1))
                        pe.wait_ge(hi_done, 2 * (i + 1))
                        pe.wait_ge(mid_done, 2 * (i + 1))
                        pe.wait_ge(dup_done, 12 * (i + 1))
                    if k < 2:
                        at_least(pe, mt_done, i)
                        at_least(pe, max_done, NS * i)
                    elif n_act:
                        pe.wait_ge(stack_act, len(ACT_T) * i + n_act[0] + 1)
                    else:
                        pe.wait_ge(stack_dve, (NT - len(ACT_T)) * i + [x for x in range(NT) if x not in ACT_T].index(k - 2) + 1)
                    bank = ps_b[k % 2][0:SK, :].bitcast(BF16).rearrange("p (h t) -> p h t", h=4)
                    for n in range(4):
                        hd = 4 * (k % 3) + n
                        for t in range(2):
                            last = nc.tensor.transpose(bank[:, n, t * P:(t + 1) * P],
                                                       stack[:, t, k // 3, hd].rearrange("p s d -> p (s d)"), ident_b[:])
                    last.then_inc(stack_ps, 1)

                def b_scores(k):
                    i, p = s - 1, 1 - u
                    if k < 2:
                        pe.wait_ge(stack_act, len(ACT_T) * (i + 1))
                        pe.wait_ge(stack_dve, (NT - len(ACT_T)) * (i + 1))
                    else:
                        pe.wait_ge(max_done, NS * i + k - 1)
                    scores(ps_b[k % 2], k, QT[p], KT[p], SK, ((0, T1), (0, T1), 0), mask_q,
                           ((T1, TOK), (0, TOK), T1)).then_inc(sq_ps, 1)

                def b_maxima():
                    i = s - 1
                    wait_apart(pe, nm_sem, 5 * (i + 1), passed_pe)
                    m_bank = ps_b[0][0:MROWS * HEADS, 0:PADT // 2].bitcast(BF16)
                    parts = nm_parts[:].rearrange("p t r h -> p t (r h)")
                    nc.tensor.transpose(m_bank[:, 0:P], parts[:, 0], ident_b[:])
                    nc.tensor.transpose(m_bank[:, P:TOK], parts[0:T1, 1], ident_b[0:T1, 0:T1]).then_inc(mt_ps, 1)

                if do_a and embed:
                    a_embed()
                if do_c:
                    c_scores(range(NS))
                if do_a:
                    a_transpose()
                if do_b:
                    for k in range(NT):
                        b_stack(k)
                if do_c:
                    c_values()
                if do_a:
                    a_qk(0)
                    a_v()
                    a_qk(1)
                if do_b:
                    for k in range(NS):
                        b_scores(k)
                if do_c:
                    c_out()
                if do_b:
                    b_maxima()
            pipeline(pe, IMG, 3, 4, step)


def ffn_phase(nc, name, h_in, h_out, w, tables, experts, act_fn, mix, last):
    pairs = IMG // 2
    moe = experts > 1
    with ExitStack() as ctx:
        def sb(n, shape, dt=F32):
            return ctx.enter_context(nc.sbuf_tensor(f"{name}_{n}", shape, dt))

        def sem(n):
            return ctx.enter_context(nc.semaphore(f"{name}_{n}"))

        def psum(n, shape, dt=F32):
            return ctx.enter_context(nc.psum_tensor(f"{name}_{n}", shape, dt))

        ident = sb("ident", [P, P])
        neg_half = sb("neg_half", [P, 4])
        w1 = sb("w1", [KC, experts, 2, HIDDEN])
        b1 = sb("b1", [P, experts, HC])
        w2 = sb("w2", [P, experts, HC, D])
        b2 = sb("b2", [P, experts, D])
        if moe:
            wg = sb("wg", [KC, 2, EXPERTS])
            bg = sb("bg", [P, 4, EXPERTS])
            logits = sb("logits", [P, 4, EXPERTS])
            top = sb("top", [P, 4])
            eq = sb("eq", [P, 4, EXPERTS])
            taken = sb("taken", [P, EXPERTS - 1, 4])
            onehot = [sb(f"onehot{u}", [P, EXPERTS, 4]) for u in range(2)]
            tmp = sb("tmp", [P, 2, 2, D])
        h = [sb(f"h{u}", [P, 4, D]) for u in range(2)]
        stats = sb("stats", [P, 4, 6])
        mv = sb("mv", [P, 4, 2])
        veps = sb("veps", [P, 4])
        rstd = sb("rstd", [P, 4])
        xn = sb("xn", [P, 4, D])
        xT = [sb(f"xT{u}", [KC, 2, 2, PADT]) for u in range(2)]
        hid = [sb(f"hid{u}", [P, HC, 2, PADT]) for u in range(2)]
        y = [sb(f"y{u}", [P, 4, D]) for u in range(2)]
        ps_x = [psum(f"ps_x{n}", [P, 512]) for n in range(2)]
        ps_up = [psum(f"ps_up{n}", [P, 512]) for n in range(2)]
        ps_y = [psum(f"ps_y{n}", [P, 2, 512]) for n in range(2)]

        passed_sp, passed_pool, passed_dve = (sem(f"passed_{e}") for e in ("sp", "pool", "dve"))
        weights_in, mixed, consts = sem("weights_in"), sem("mixed"), sem("consts")
        h_in_sem = sem("h_in")
        stats_done, mv_done, veps_done, rstd_done = sem("stats_done"), sem("mv_done"), sem("veps_done"), sem("rstd_done")
        xn_done, xt_ps, xt_done = sem("xn_done"), sem("xt_ps"), sem("xt_done")
        gate_ps, gate_step = sem("gate_ps"), sem("gate_step")
        up_ps, gelu_done, down_ps, y_taken = sem("up_ps"), sem("gelu_done"), sem("down_ps"), sem("y_taken")
        tmp_done, acc_done, y_done, y_out = sem("tmp_done"), sem("acc_done"), sem("y_done"), sem("y_out")
        GATE = 3 + 2 * (EXPERTS - 1) + 1
        n_weights = 5 + 2 * moe
        MIXED = 4 + 3 + 9 * 3 + 1 + 4
        if mix:
            alpha_e = sb("alpha_e", [P, 3])
            alpha_r = sb("alpha_r", [P, 3])
            in_mask = sb("in_mask", [KC, 2, 3])
            out_mask = sb("out_mask", [P, HC, 9])
            a = sb("a", [P, 3, 3])
            a_in = sb("a_in", [KC, 2, 3, 3])
            a_out = sb("a_out", [P, HC, 9])
            c_up = sb("c_up", [KC, 2, HIDDEN])
            c_down = sb("c_down", [P, HC, D])
            c_b1 = sb("c_b1", [P, HC])
            c_b2 = sb("c_b2", [P, D])
            n_weights += 4
        block = ctx.enter_context(nc.Block())

        def job_of(i, e, u):
            return experts * i + e, (experts * u + e) % 2

        @block.sync
        def _(sp):
            sp.dma_start(ident[:], tables["ident"]).then_inc(weights_in, 16)
            sp.dma_start(w1[:], w["w1"]).then_inc(weights_in, 16)
            sp.dma_start(b1[:], w["b1"]).then_inc(weights_in, 16)
            sp.dma_start(w2[:], w["w2"]).then_inc(weights_in, 16)
            sp.dma_start(b2[:], w["b2"]).then_inc(weights_in, 16)
            if moe:
                sp.dma_start(wg[:], w["wg"]).then_inc(weights_in, 16)
                sp.dma_start(bg[:], w["bg"]).then_inc(weights_in, 16)
            if mix:
                sp.dma_start(alpha_e[:], w["alpha_e"]).then_inc(weights_in, 16)
                sp.dma_start(alpha_r[:], w["alpha_r"]).then_inc(weights_in, 16)
                sp.dma_start(in_mask[:], tables["in_mask"]).then_inc(weights_in, 16)
                sp.dma_start(out_mask[:], tables["out_mask"]).then_inc(weights_in, 16)

            def load(i, p):
                wait_apart(sp, h_in_sem, 16 * i, passed_sp)
                wait_apart(sp, y_done, i - 1, passed_sp)
                src = h_in[bass.ds(2 * i, 2)] if not isinstance(i, int) else h_in[2 * i:2 * i + 2]
                sp.dma_start(h[p][:].rearrange("p (g t) d -> p g t d", g=2), src.rearrange("g p t d -> p g t d"))\
                    .then_inc(h_in_sem, 16)

            def step(s, u):
                if isinstance(s, int) and s == 0:
                    load(0, 0)
                if not isinstance(s, int) or s + 1 < pairs:
                    load(s + 1, 1 - u)
                if not isinstance(s, int) or s >= 1:
                    i, p = s - 1, 1 - u
                    wait_apart(sp, y_out, 16 * (4 if last else 2) * i, passed_sp)
                    wait_apart(sp, y_done, i + 1, passed_sp)
                    if last:
                        for g in range(2):
                            sp.dma_start(h_out[2 * i + g, 0:P], y[p][:, 2 * g]).then_inc(y_out, 16)
                            sp.dma_start(h_out[2 * i + g, P:TOK], y[p][0:T1, 2 * g + 1]).then_inc(y_out, 16)
                    else:
                        for g in range(2):
                            sp.dma_start(h_out[2 * i + g], y[p][:, 2 * g:2 * g + 2]).then_inc(y_out, 16)
            pipeline(sp, pairs, 2, 4, step)
            sp.wait_ge(y_out, 16 * (4 if last else 2) * pairs)

        @block.gpsimd
        def _(pool):
            nc.gpsimd.memset(neg_half[:], -0.5).then_inc(consts, 1)
            for u in range(2):
                pool.wait_ge(consts, u + 1)
                nc.gpsimd.memset(hid[u][:, :, :, TOK:PADT], 0.0).then_inc(consts, 1)
            pool.wait_ge(consts, 3)

            def step(s, u):
                if not isinstance(s, int) or s < pairs:
                    wait_apart(pool, mv_done, 4 * (s + 1), passed_pool)
                    nc.gpsimd.tensor_scalar_add(veps[:], mv[:, :, 1], EPS).then_inc(veps_done, 1)
                    pool.wait_ge(veps_done, s + 1)
                    nc.gpsimd.tensor_tensor(rstd[:], veps[:], neg_half[:], ALU.pow).then_inc(rstd_done, 1)
            pipeline(pool, pairs, 2, 4, step)

        @block.scalar
        def _(act):
            act.wait_ge(weights_in, 16 * n_weights)
            act.wait_ge(consts, 3)
            if mix:
                act.wait_ge(mixed, MIXED)

            def gelu(s, u, e):
                i, p = s - 1, 1 - u
                job, b = job_of(i, e, p)
                for m in range(HC):
                    act.wait_ge(up_ps, HC * job + m + 1)
                    at_least(act, down_ps, job - 1)
                    nc.scalar.activation(hid[b][:, m, :, 0:TOK],
                                         ps_up[m % 2][:, 0:2 * TOK].rearrange("p (g t) -> p g t", g=2),
                                         act_fn, bias=b1[:, e, m:m + 1]).then_inc(gelu_done, 1)

            def step(s, u):
                if not isinstance(s, int) or s >= 1:
                    gelu(s, u, 0)
                if not isinstance(s, int) or s < pairs:
                    act.wait_ge(xt_ps, s + 1)
                    at_least(act, down_ps, experts * (s - 1))
                    for c in range(2):
                        nc.scalar.copy(xT[u][:, c].rearrange("p g t -> p (g t)"), ps_x[c][0:KC]).then_inc(xt_done, 1)
                if not isinstance(s, int) or s >= 1:
                    for e in range(1, experts):
                        gelu(s, u, e)
            pipeline(act, pairs, 2, 4, step)

        @block.vector
        def _(dve):
            dve.wait_ge(weights_in, 16 * n_weights)
            if mix:
                mixes = [0]

                def mixing(ins):
                    mixes[0] += 1
                    ins.then_inc(mixed, 1)
                    dve.wait_ge(mixed, mixes[0])
                tt = nc.vector.tensor_tensor
                mixing(tt(a[:], alpha_e[:, :, None].broadcast_to([P, 3, 3]), alpha_r[:, None, :].broadcast_to([P, 3, 3]), ALU.mult))
                mixing(nc.vector.memset(c_up[:], 0.0))
                mixing(nc.vector.memset(c_down[:], 0.0))
                mixing(nc.vector.memset(c_b2[:], 0.0))
                for c in range(2):
                    mixing(tt(a_in[:, c], a[0:KC], in_mask[:, c, :, None].broadcast_to([KC, 3, 3]), ALU.mult))
                mixing(tt(a_out[:], a[:, None].rearrange("p o i j -> p o (i j)").broadcast_to([P, HC, 9]), out_mask[:], ALU.mult))
                for i, width in enumerate(E_CHOICES):
                    for j, ratio in enumerate(R_CHOICES):
                        n = ratio * width
                        mixing(tt(c_up[:, :, 0:n], c_up[:, :, 0:n], a_in[:, :, i, j:j + 1].broadcast_to([KC, 2, n]), ALU.add))
                        mixing(tt(c_down[:, :, 0:width], c_down[:, :, 0:width],
                                  a_out[:, :, 3 * i + j:3 * i + j + 1].broadcast_to([P, HC, width]), ALU.add))
                        mixing(nc.vector.tensor_scalar_add(c_b2[:, 0:width], c_b2[:, 0:width], a[:, i, j:j + 1]))
                mixing(nc.vector.tensor_reduce(c_b1[:], a_out[:], AX_X, ALU.add))
                mixing(tt(w1[:, 0], w1[:, 0], c_up[:], ALU.mult))
                mixing(tt(w2[:, 0], w2[:, 0], c_down[:], ALU.mult))
                mixing(tt(b1[:, 0], b1[:, 0], c_b1[:], ALU.mult))
                mixing(tt(b2[:, 0], b2[:, 0], c_b2[:], ALU.mult))
                assert mixes[0] == MIXED, mixes

            def combine(s, u, e):
                i, p = s - 1, 1 - u
                job, b = job_of(i, e, p)
                src = ps_y[b][:, :, 0:2 * D].rearrange("p g (t d) -> p g t d", t=2)
                dve.wait_ge(down_ps, job + 1)
                if e == 0:
                    at_least(dve, y_out, 16 * (4 if last else 2) * (i - 1))
                if moe:
                    at_least(dve, acc_done, 4 * job)
                    for g in range(2):
                        nc.vector.tensor_tensor(tmp[:, g], src[:, g], b2[:, e, None, :].broadcast_to([P, 2, D]), ALU.add)\
                            .then_inc(tmp_done, 1)
                    dve.wait_ge(tmp_done, 2 * (job + 1))
                    for j in range(4):
                        prev = h[p] if e == 0 else y[p]
                        acc = nc.vector.scalar_tensor_tensor(y[p][:, j], tmp[:, j // 2, j % 2], onehot[p][:, e, j:j + 1],
                                                             prev[:, j], ALU.mult, ALU.add)
                        acc.then_inc(acc_done, 1)
                    if e == experts - 1:
                        dve.wait_ge(acc_done, 4 * (job + 1))
                        dve.sem_inc(y_done, 1)
                else:
                    at_least(dve, tmp_done, 2 * job)
                    for g in range(2):
                        nc.vector.tensor_tensor(h[p][:, 2 * g:2 * g + 2], h[p][:, 2 * g:2 * g + 2],
                                                b2[:, 0, None, :].broadcast_to([P, 2, D]), ALU.add).then_inc(tmp_done, 1)
                    dve.wait_ge(tmp_done, 2 * (job + 1))
                    for g in range(2):
                        acc = nc.vector.tensor_tensor(y[p][:, 2 * g:2 * g + 2], src[:, g], h[p][:, 2 * g:2 * g + 2], ALU.add)
                    acc.then_inc(y_done, 1)

            def step(s, u):
                if not isinstance(s, int) or s < pairs:
                    i = s
                    dve.wait_ge(h_in_sem, 16 * (i + 1))
                    for j in range(4):
                        nc.vector.bn_stats(stats[:, j], h[u][:, j]).then_inc(stats_done, 1)
                    wait_apart(dve, stats_done, 4 * (i + 1), passed_dve)
                    wait_apart(dve, veps_done, i, passed_dve)
                    for j in range(4):
                        nc.vector.bn_aggr(mv[:, j], stats[:, j]).then_inc(mv_done, 1)
                    dve.wait_ge(rstd_done, i + 1)
                    at_least(dve, xt_ps, i)
                    for j in range(4):
                        nc.vector.tensor_scalar(xn[:, j], h[u][:, j], mv[:, j, 0:1], rstd[:, j:j + 1],
                                                ALU.subtract, ALU.mult).then_inc(xn_done, 1)
                if not isinstance(s, int) or s >= 1:
                    combine(s, u, 0)
                if moe and (not isinstance(s, int) or s < pairs):
                    i = s
                    k = [GATE * i]

                    def gate(ins):
                        k[0] = k[0] + 1
                        ins.then_inc(gate_step, 1)
                        dve.wait_ge(gate_step, k[0])
                    dve.wait_ge(gate_ps, i + 1)
                    gate(nc.vector.tensor_tensor(logits[:], ps_x[0][:, 0:4 * EXPERTS].rearrange("p (j n) -> p j n", j=4),
                                                 bg[:], ALU.add))
                    gate(nc.vector.tensor_reduce(top[:], logits[:], AX_X, ALU.max))
                    gate(nc.vector.tensor_tensor(eq[:], logits[:], top[:, :, None].broadcast_to([P, 4, EXPERTS]), ALU.is_equal))
                    gate(nc.vector.tensor_copy(onehot[u][:, 0], eq[:, :, 0]))
                    before = eq[:, :, 0]
                    for n in range(1, EXPERTS):
                        gate(nc.vector.tensor_tensor(onehot[u][:, n], eq[:, :, n], before, ALU.is_gt))
                        gate(nc.vector.tensor_tensor(taken[:, n - 1], eq[:, :, n], before, ALU.max))
                        before = taken[:, n - 1]
                if not isinstance(s, int) or s >= 1:
                    for e in range(1, experts):
                        combine(s, u, e)
            pipeline(dve, pairs, 2, 4, step)

        @block.tensor
        def _(pe):
            pe.wait_ge(weights_in, 16 * n_weights)
            pe.wait_ge(consts, 3)
            if mix:
                pe.wait_ge(mixed, MIXED)
            mm = nc.tensor.matmul

            def up(s, u, e):
                i, p = s - 1, 1 - u
                job, _ = job_of(i, e, p)
                pe.wait_ge(xt_done, 2 * (i + 1))
                for m in range(HC):
                    at_least(pe, gelu_done, HC * job + m - 1)
                    for c in range(2):
                        last_mm = mm(ps_up[m % 2][:, 0:2 * TOK].rearrange("p (g t) -> p g t", g=2),
                                     w1[:, e, c, m * P:(m + 1) * P], xT[p][:, c, :, 0:TOK], start=(c == 0), stop=(c == 1))
                    last_mm.then_inc(up_ps, 1)

            def down(s, u, e):
                i, p = s - 1, 1 - u
                job, b = job_of(i, e, p)
                pe.wait_ge(gelu_done, HC * (job + 1))
                at_least(pe, tmp_done if moe else y_done, (2 if moe else 1) * (job - 1))
                for g in range(2):
                    for t in range(2):
                        for m in range(HC):
                            last_mm = mm(ps_y[b][:, g, t * D:(t + 1) * D], hid[b][:, m, g, t * P:(t + 1) * P],
                                         w2[:, e, m], start=(m == 0), stop=(m == HC - 1))
                last_mm.then_inc(down_ps, 1)

            def transposes(s, u):
                pe.wait_ge(xn_done, 4 * (s + 1))
                at_least(pe, xt_done, 2 * s)
                if moe:
                    at_least(pe, gate_step, GATE * (s - 1) + 1)
                for c in range(2):
                    for j in range(4):
                        last_mm = nc.tensor.transpose(ps_x[c][0:KC, j * P:(j + 1) * P], xn[:, j, c * KC:(c + 1) * KC], ident[:])
                last_mm.then_inc(xt_ps, 1)

            def gates(s, u):
                pe.wait_ge(xt_done, 2 * (s + 1))
                for j in range(4):
                    for c in range(2):
                        last_mm = mm(ps_x[0][:, j * EXPERTS:(j + 1) * EXPERTS], xT[u][:, c, j // 2, (j % 2) * P:(j % 2 + 1) * P],
                                     wg[:, c], start=(c == 0), stop=(c == 1))
                last_mm.then_inc(gate_ps, 1)

            def step(s, u):
                do_a = not isinstance(s, int) or s < pairs
                do_b = not isinstance(s, int) or s >= 1
                if do_b:
                    up(s, u, 0)
                if do_a:
                    transposes(s, u)
                if do_b:
                    if experts > 1:
                        up(s, u, 1)
                    down(s, u, 0)
                if do_a and moe:
                    gates(s, u)
                if do_b:
                    for e in range(1, experts):
                        if e + 1 < experts:
                            up(s, u, e + 1)
                        down(s, u, e)
            pipeline(pe, pairs, 2, 4, step)


def build(nc, t, out):
    scratch = [nc.dram_tensor(f"h{n}", [IMG, P, 2, D], F32, kind="Internal").ap() for n in range(4)]
    tables0 = {"ident": t["ident"], "cos": t["cos"], "sin": t["sin"]}
    tables1 = {"ident": t["ident"], "cos": None, "sin": None, "in_mask": t["in_mask"], "out_mask": t["out_mask"]}
    attention_phase(nc, "a0", t["patches"], scratch[0], scratch[1],
                    {"tok": t["w_tok"], "tok_add": t["tok_add"], "qk": t["wqk0"], "v": t["wv0"], "o": t["wo0"]}, tables0, True)
    ffn_phase(nc, "f0", scratch[1], scratch[2],
              {"w1": t["w1_0"], "b1": t["b1_0"], "w2": t["w2_0"], "b2": t["b2_0"], "wg": t["wg"], "bg": t["bg"]},
              tables1, EXPERTS, ACT.Gelu, False, False)
    attention_phase(nc, "a1", None, scratch[2], scratch[3], {"qk": t["wqk1"], "v": t["wv1"], "o": t["wo1"]}, tables1, False)
    ffn_phase(nc, "f1", scratch[3], out,
              {"w1": t["w1_1"], "b1": t["b1_1"], "w2": t["w2_1"], "b2": t["b2_1"], "alpha_e": t["alpha_e"], "alpha_r": t["alpha_r"]},
              tables1, 1, ACT.Gelu_apprx_tanh, True, True)


def shape_constants():
    i = np.arange(D // 2, dtype=np.float64)
    theta = 10000.0 ** (-2.0 * i / D)
    angle = np.repeat(np.arange(1, PADT + 1, dtype=np.float64)[:, None] * theta[None, :], 2, axis=-1)
    sign = np.tile([-1.0, 1.0], D // 2)

    def tiles(a):
        return np.ascontiguousarray(a.reshape(2, P, D).transpose(1, 0, 2).astype(np.float32))
    in_mask = np.zeros((KC, 2, 3), np.float32)
    out_mask = np.zeros((P, HC, 9), np.float32)
    for a, e in enumerate(E_CHOICES):
        in_mask[:, :, a] = (np.arange(D).reshape(2, KC).T < e)
        for b, r in enumerate(R_CHOICES):
            out_mask[:, :, 3 * a + b] = (np.arange(HIDDEN).reshape(HC, P).T < r * e)
    return {"ident": np.eye(P, dtype=np.float32), "cos": tiles(np.cos(angle)), "sin": tiles(np.sin(angle) * sign),
            "in_mask": in_mask, "out_mask": out_mask}


def kernel(**inputs):
    import concourse.bacc as bacc
    from concourse.bass_utils import run_bass_kernel_spmd as run

    x = {k: np.asarray(v) for k, v in inputs.items()}

    def chunks(w, rows):
        return np.ascontiguousarray(w.reshape(-1, rows, w.shape[-1]).transpose(1, 0, 2))

    def every_partition(v):
        return np.ascontiguousarray(np.broadcast_to(v, (P,) + v.shape))

    def heads_padded(wo):
        padded = np.zeros((HEADS, 2 * DH, D), np.float32)
        padded[:, 0:DH] = wo.T.reshape(HEADS, DH, D)
        return chunks(padded.reshape(HEADS * 2 * DH, D), P)

    side, n = 16, 14
    pixels = x["x"].reshape(IMG, 3, n, side, n, side).transpose(0, 1, 3, 5, 2, 4).reshape(IMG, PATCH, n * n)
    patches = np.zeros((IMG, P, PC, PADT), np.float32)
    patches[:, :, :, 1:TOK] = pixels.reshape(IMG, PC, P, n * n).transpose(0, 2, 1, 3)
    tok_add = every_partition(x["L0_tok_b"])[:, None, :].repeat(2, axis=1)
    tok_add[0, 0] = x["cls_tok"][0, 0]
    arrays = {
        "patches": patches, "tok_add": tok_add, "w_tok": chunks(x["L0_tok_W"].T, P),
        "wqk0": chunks(np.concatenate([x["L0_attn_W_q"].T, x["L0_attn_W_k"].T], axis=1), KC),
        "wv0": chunks(x["L0_attn_W_v"].T, KC), "wo0": heads_padded(x["L0_attn_W_o"]),
        "wqk1": chunks(np.concatenate([x["L1_attn_wq"].T, x["L1_attn_wk"].T], axis=1), KC),
        "wv1": chunks(x["L1_attn_wv"].T, KC), "wo1": heads_padded(x["L1_attn_wo"]),
        "w1_0": np.ascontiguousarray(x["L0_ffn_W1"].reshape(EXPERTS, 2, KC, HIDDEN).transpose(2, 0, 1, 3)),
        "b1_0": np.ascontiguousarray(x["L0_ffn_b1"].reshape(EXPERTS, HC, P).transpose(2, 0, 1)),
        "w2_0": np.ascontiguousarray(x["L0_ffn_W2"].reshape(EXPERTS, HC, P, D).transpose(2, 0, 1, 3)),
        "b2_0": every_partition(x["L0_ffn_b2"]),
        "wg": chunks(x["L0_ffn_Wg"], KC), "bg": every_partition(x["L0_ffn_bg"])[:, None, :].repeat(4, axis=1),
        "w1_1": chunks(x["L1_ffn_w_fc"].T, KC)[:, None], "b1_1": np.ascontiguousarray(x["L1_ffn_b_fc"].reshape(1, HC, P).transpose(2, 0, 1)),
        "w2_1": chunks(x["L1_ffn_w_proj"].T, P)[:, None], "b2_1": every_partition(x["L1_ffn_b_proj"][None]),
        "alpha_e": every_partition(x["L1_ffn_alpha_e"]), "alpha_r": every_partition(x["L1_ffn_alpha_r"]),
        **shape_constants(),
    }
    nc = bacc.Bacc("TRN2", target_bir_lowering=False, num_devices=1)
    tensors = {k: nc.dram_tensor(f"in_{k}", a.shape, F32, kind="ExternalInput").ap() for k, a in arrays.items()}
    out = nc.dram_tensor("out", (IMG, TOK, D), F32, kind="ExternalOutput").ap()
    build(nc, tensors, out)
    result = run(nc, [{f"in_{k}": np.ascontiguousarray(a) for k, a in arrays.items()}], core_ids=[0])
    return result.results[0]["out"]
```

```python
from contextlib import ExitStack

import numpy as np

import concourse.bass as bass
from concourse import mybir

F32 = mybir.dt.float32
BF16 = mybir.dt.bfloat16
I32 = mybir.dt.int32
ALU = mybir.AluOpType
ACT = mybir.ActivationFunctionType
AX_X = mybir.AxisListType.X

P = 128
IMG = 64
TOK = 197
PADT = 2 * P
T1 = TOK - P
D = 192
KC = 96
PATCH = 768
PC = PATCH // P
HEADS = 12
DH = D // HEADS
HIDDEN = 768
HC = HIDDEN // P
EXPERTS = 4
SLOTS = 6
SK = SLOTS * DH
MROWS = 3
SCALE = float(DH) ** -0.5
EPS = 1e-5
NEG = -1e9
UNROLL = 2
LEAD = 6
ROUTE_LEAD = 8
TS = 3 * P
SPARE_TILES = EXPERTS + 1
E_CHOICES = (96, 144, 192)
R_CHOICES = (2, 3, 4)


def at_least(eng, sem, value):
    if isinstance(value, int) and value <= 0:
        return
    eng.wait_ge(sem, value)


def wait_apart(eng, sem, value, passed):
    if isinstance(value, int) and value <= 0:
        return
    eng.wait_ge(sem, value)
    if not isinstance(value, int):
        eng.sem_inc(passed, 1)


def pipeline(eng, items, depth, lead, step, unroll=UNROLL):
    steps = items + depth - 1
    full = lead + (items - 2 - lead) // unroll * unroll
    for s in range(lead):
        step(s, s % unroll)
    with eng.Fori(lead, full, unroll) as s:
        for u in range(unroll):
            step(s + u, u)
    for s in range(full, steps):
        step(s, s % unroll)


def n_tiles():
    return (IMG * TOK + EXPERTS * (TS - 1)) // TS + 1


def capacity():
    return -(-(IMG * TOK) // TS) * TS + TS


def attention_phase(nc, name, passed, x_dram, h_in, h_out, w, tables, embed, experts=None):
    with ExitStack() as ctx:
        def sb(n, shape, dt=F32):
            return ctx.enter_context(nc.sbuf_tensor(f"{name}_{n}", shape, dt))

        def sem(n):
            return ctx.enter_context(nc.semaphore(f"{name}_{n}"))

        def psum(n, shape, dt=F32):
            return ctx.enter_context(nc.psum_tensor(f"{name}_{n}", shape, dt))

        rope = tables["cos"] is not None
        ident = sb("ident", [P, P])
        ident_b = sb("ident_b", [P, P], BF16)
        mask_q = sb("mask_q", [P, P], BF16)
        mask_k = sb("mask_k", [P, P], BF16)
        neg_half = sb("neg_half", [P, 2])
        wqk = sb("wqk", [KC, 2, 2 * D])
        wv = sb("wv", [KC, 2, D])
        wo = sb("wo", [KC, 2, D])
        if rope:
            cos = sb("cos", [P, 2, D])
            sin = sb("sin", [P, 2, D])
        if embed:
            w_tok = sb("w_tok", [P, PC, D])
            tok_add = sb("tok_add", [P, 2, D])
            patches = sb("patches", [P, 2, PC, PADT])
        else:
            y_rows, index_all = experts
            h_before = sb("h_before", [P, 2, 2, D])
            gathered = sb("gathered", [P, 2, 2, D])
            row_of = [sb(f"row_of{u}", [P, 2], I32) for u in range(2)]
        h = sb("h", [P, 2, 2, D])
        stats = sb("stats", [P, 2, 6])
        mv = sb("mv", [P, 2, 2])
        veps = sb("veps", [P, 2])
        rstd = sb("rstd", [P, 2])
        xn = sb("xn", [P, 2, D])
        xT = sb("xT", [KC, 2, PADT])
        if rope:
            rc = sb("rc", [P, 2, 2 * D])
            rs = sb("rs", [P, 2, 2 * D])
        qk = sb("qk", [P, 2, 2 * D])
        rest = sb("rest", [P, 2, 2 * D])
        stack = [sb(f"stack{u}", [P, 2, 2, HEADS, SLOTS, DH], BF16) for u in range(2)]
        QT = [sb(f"QT{u}", [P, HEADS, TOK], BF16) for u in range(2)]
        KT = [sb(f"KT{u}", [P, HEADS, TOK], BF16) for u in range(2)]
        V = [sb(f"V{u}", [P, 2, HEADS, 2 * DH]) for u in range(2)]
        mx = sb("mx", [P, 2, HEADS])
        nm = sb("nm", [P, 2, HEADS])
        nm_rest = sb("nm_rest", [P, 2, HEADS])
        nm_parts = sb("nm_parts", [P, 2, MROWS, HEADS], BF16)
        mT = sb("mT", [MROWS * HEADS, TOK], BF16)
        probs0 = sb("probs0", [P, HEADS, TOK])
        probs1 = sb("probs1", [T1, HEADS, T1])
        OT = sb("OT", [P, 3, PADT])
        inv = sb("inv", [P, 2, HEADS])
        ON = sb("ON", [P, 2, HEADS, DH])
        ONT = sb("ONT", [KC, 2, PADT])
        h_res = sb("h_res", [P, 2, 2, D])
        y = sb("y", [P, 2, 2, D])
        ps_front = psum("ps_front", [P, 512])
        ps_qk = psum("ps_qk", [P, 512])
        ps_b = [psum(f"ps_b{n}", [P, 512]) for n in range(2)]
        ps_c = [psum(f"ps_c{n}", [P, 512]) for n in range(2)]
        ps_o = psum("ps_o", [P, 2, 512])

        weights_in = sem("weights_in")
        n_weights = 4 + 2 * rope + 2 * embed
        passed_sp, passed_pool, passed_dve, passed_pe = passed
        ident_sem, consts = sem("ident"), sem("consts")
        if embed:
            patches_in, tok_done = sem("patches_in"), sem("tok_done")
        else:
            h_in_sem, index_in, rows_in = sem("h_in"), sem("index_in"), sem("rows_in")
        h_ready, h_kept = sem("h_ready"), sem("h_kept")
        stats_done, mv_done, veps_done, rstd_done = sem("stats_done"), sem("mv_done"), sem("veps_done"), sem("rstd_done")
        xn_done, xt_ps, xt_done = sem("xn_done"), sem("xt_ps"), sem("xt_done")
        qk_ps, v_ps, v_done = sem("qk_ps"), sem("v_ps"), sem("v_done")
        rope_done, qk_done = sem("rope_done"), sem("qk_done")
        hi_done, rest_done, mid_done, lo_done, dup_done = sem("hi_done"), sem("rest_done"), sem("mid_done"), sem("lo_done"), sem("dup_done")
        stack_ps, stack_act, stack_dve = sem("stack_ps"), sem("stack_act"), sem("stack_dve")
        sq_ps, max_done = sem("sq_ps"), sem("max_done")
        nm_sem, mt_ps, mt_done, mrows_in = sem("nm"), sem("mt_ps"), sem("mt_done"), sem("mrows_in")
        sk_ps, exp_done = sem("sk_ps"), sem("exp_done")
        av_ps, o_done, ot_ps, inv_done, on_done, ont_ps, ont_done = (sem(n) for n in (
            "av_ps", "o_done", "ot_ps", "inv_done", "on_done", "ont_ps", "ont_done"))
        y_ps, hres_in, y_done, y_out = sem("y_ps"), sem("hres_in"), sem("y_done"), sem("y_out")

        CONSTS = 11 + (not embed)
        NT = 6
        ACT_T = (0, 1, 3, 4)
        DVE_T = (2, 5)
        NS = 8
        DUPS = 8
        DEPTH = 5
        E, PR, M, O, Y = range(DEPTH)
        block = ctx.enter_context(nc.Block())

        def item(s, u, stage):
            if isinstance(s, int) and not 0 <= s - stage < IMG:
                return None, None
            return s - stage, (u - stage) % 2

        def score_banks(k):
            return (range(2 * k, 2 * k + 2), False) if k < 6 else (range(6 * (k - 6), 6 * (k - 5)), True)

        def four(ap):
            return ap.rearrange("p (j h d) -> p j h d", j=2, h=HEADS)

        def stack_bank(k):
            return ps_b[k % 2][0:SK, :].bitcast(BF16).rearrange("p (h t) -> p h t", h=4)

        def stack_dst(k, p):
            return (QT[p] if k < 3 else KT[p])[0:SK, 4 * (k % 3):4 * (k % 3) + 4]

        @block.sync
        def _(sp):
            sp.dma_start(wqk[:], w["qk"]).then_inc(weights_in, 16)
            sp.dma_start(wv[:], w["v"]).then_inc(weights_in, 16)
            sp.dma_start(wo[:], w["o"]).then_inc(weights_in, 16)
            sp.dma_start(ident[:], tables["ident"]).then_inc(weights_in, 16)
            if rope:
                sp.dma_start(cos[:], tables["cos"]).then_inc(weights_in, 16)
                sp.dma_start(sin[:], tables["sin"]).then_inc(weights_in, 16)
            if embed:
                sp.dma_start(w_tok[:], w["tok"]).then_inc(weights_in, 16)
                sp.dma_start(tok_add[:], w["tok_add"]).then_inc(weights_in, 16)

            def load(i, p):
                if embed:
                    wait_apart(sp, tok_done, i - 1, passed_sp)
                    wait_apart(sp, patches_in, 16 * i, passed_sp)
                    sp.dma_start(patches[:, p], x_dram[i]).then_inc(patches_in, 16)
                else:
                    wait_apart(sp, h_ready, i - 1, passed_sp)
                    wait_apart(sp, h_in_sem, 16 * i, passed_sp)
                    sp.dma_start(h_before[:, p], x_dram[i]).then_inc(h_in_sem, 16)

            def step(s, u):
                i, p = item(s, u, O)
                if i is not None:
                    wait_apart(sp, mrows_in, 16 * i, passed_sp)
                    wait_apart(sp, mt_done, i + 1, passed_sp)
                    sp.dma_start(QT[p][SK:SK + MROWS], mT[:]).then_inc(mrows_in, 16)
                i, p = item(s, u, Y)
                if i is not None:
                    wait_apart(sp, y_out, 16 * i, passed_sp)
                    wait_apart(sp, y_done, i + 1, passed_sp)
                    sp.dma_start(h_out[i], y[:, p]).then_inc(y_out, 16)
                if isinstance(s, int) and s == 0:
                    load(0, 0)
                if not isinstance(s, int) or s + 1 < IMG:
                    load(s + 1, 1 - u)
                i, p = item(s, u, O)
                if i is not None:
                    wait_apart(sp, h_kept, 16 * (i + 1), passed_sp)
                    wait_apart(sp, hres_in, 16 * i, passed_sp)
                    wait_apart(sp, y_done, i - 1, passed_sp)
                    sp.dma_start(h_res[:, p], h_in[i]).then_inc(hres_in, 16)
                i, p = item(s, u, E)
                if i is not None:
                    wait_apart(sp, h_kept, 16 * i, passed_sp)
                    wait_apart(sp, h_ready, i + 1, passed_sp)
                    sp.dma_start(h_in[i], h[:, p]).then_inc(h_kept, 16)
            pipeline(sp, IMG, DEPTH, LEAD, step)
            sp.wait_ge(y_out, 16 * IMG)
            sp.wait_ge(h_kept, 16 * IMG)

        @block.gpsimd
        def _(pool):
            setup = [lambda: nc.gpsimd.memset(mask_q[:], 0.0), lambda: nc.gpsimd.memset(mask_k[:], 0.0),
                     lambda: nc.gpsimd.memset(neg_half[:], -0.5), lambda: nc.gpsimd.memset(OT[:], 1.0),
                     lambda: nc.gpsimd.memset(mx[:], 0.0)]
            for n, fill in enumerate(setup):
                at_least(pool, consts, n)
                fill().then_inc(consts, 1)
            for u in range(2):
                pool.wait_ge(consts, 5 + 2 * u)
                nc.gpsimd.memset(V[u][:], 1.0).then_inc(consts, 1)
                pool.wait_ge(consts, 6 + 2 * u)
                nc.gpsimd.memset(KT[u][SK:P], 1.0).then_inc(consts, 1)
            pool.wait_ge(consts, 9)
            nc.gpsimd.affine_select(out=mask_q[:], in_=mask_q[:], compare_op=ALU.is_ge, fill=NEG, base=0,
                                    pattern=[[-1, P]], channel_multiplier=1).then_inc(consts, 1)
            pool.wait_ge(consts, 10)
            nc.gpsimd.affine_select(out=mask_k[:], in_=mask_k[:], compare_op=ALU.is_ge, fill=NEG, base=0,
                                    pattern=[[1, P]], channel_multiplier=-1).then_inc(consts, 1)
            if not embed:
                pool.wait_ge(consts, 11)
                nc.gpsimd.memset(gathered[:], 0.0).then_inc(consts, 1)
            pool.wait_ge(consts, CONSTS)

            def gather(i, p):
                at_least(pool, h_ready, i - 1)
                wait_apart(pool, rows_in, 32 * i, passed_pool)
                at = index_all[:, 2 * i:2 * i + 2] if isinstance(i, int) else index_all[:, bass.ds(2 * i, 2)]
                nc.gpsimd.tensor_copy(row_of[p][:], at).then_inc(index_in, 1)
                wait_apart(pool, index_in, i + 1, passed_pool)
                for t, n in ((0, P), (1, T1)):
                    nc.gpsimd.indirect_dma_start(out=gathered[0:n, p, t], out_offset=None, in_=y_rows,
                                                 in_offset=bass.IndirectOffsetOnAxis(ap=row_of[p][0:n, t:t + 1], axis=0))\
                        .then_inc(rows_in, 16)

            def parts(i, p, t):
                n = 2 * i + t + 1
                if rope:
                    pool.wait_ge(rope_done, 3 * n)
                    nc.gpsimd.tensor_tensor(qk[:, t], rc[:, t], rs[:, t], ALU.add).then_inc(qk_done, 1)
                pool.wait_ge(hi_done, n)
                pool.wait_ge(qk_done, n)
                at_least(pool, lo_done, 2 * (n - 2))
                nc.gpsimd.tensor_tensor(four(rest[:, t]), four(qk[:, t]), stack[p][:, t, :, :, 0, :], ALU.subtract)\
                    .then_inc(rest_done, 1)
                pool.wait_ge(mid_done, n)
                pool.wait_ge(rest_done, n)
                for j, slot in ((0, 4), (1, 5)):
                    nc.gpsimd.tensor_tensor(stack[p][:, t, j, :, slot, :], four(rest[:, t])[:, j],
                                            stack[p][:, t, j, :, 1 + j, :], ALU.subtract).then_inc(lo_done, 1)

            def step(s, u):
                if not embed:
                    if isinstance(s, int) and s == 0:
                        gather(0, 0)
                    if not isinstance(s, int) or s + 1 < IMG:
                        gather(s + 1, 1 - u)
                i, p = item(s, u, PR)
                if i is not None:
                    parts(i, p, 0)
                i, p = item(s, u, E)
                if i is not None:
                    wait_apart(pool, mv_done, 2 * (i + 1), passed_pool)
                    nc.gpsimd.tensor_scalar_add(veps[:], mv[:, :, 1], EPS).then_inc(veps_done, 1)
                    pool.wait_ge(veps_done, i + 1)
                    nc.gpsimd.tensor_tensor(rstd[:], veps[:], neg_half[:], ALU.pow).then_inc(rstd_done, 1)
                i, p = item(s, u, PR)
                if i is not None:
                    parts(i, p, 1)
                i, p = item(s, u, M)
                if i is not None:
                    wait_apart(pool, mt_ps, i, passed_pool)
                    wait_apart(pool, max_done, NS * (i + 1), passed_pool)
                    nc.gpsimd.tensor_scalar_mul(nm[:], mx[:], -1.0).then_inc(nm_sem, 1)
                    wait_apart(pool, nm_sem, 5 * i + 1, passed_pool)
                    nc.gpsimd.tensor_copy(nm_parts[:, :, 0], nm[:]).then_inc(nm_sem, 1)
                    pool.wait_ge(nm_sem, 5 * i + 2)
                    nc.gpsimd.tensor_tensor(nm_rest[:], nm[:], nm_parts[:, :, 0], ALU.subtract).then_inc(nm_sem, 1)
                    wait_apart(pool, nm_sem, 5 * i + 3, passed_pool)
                    nc.gpsimd.tensor_copy(nm_parts[:, :, 1], nm_rest[:]).then_inc(nm_sem, 1)
                    pool.wait_ge(nm_sem, 5 * i + 4)
                    nc.gpsimd.tensor_tensor(nm_parts[:, :, 2], nm_rest[:], nm_parts[:, :, 1], ALU.subtract)\
                        .then_inc(nm_sem, 1)
            pipeline(pool, IMG, DEPTH, LEAD, step)

        @block.scalar
        def _(act):
            act.wait_ge(weights_in, 16 * n_weights)
            nc.scalar.copy(ident_b[:], ident[:]).then_inc(ident_sem, 1)
            act.wait_ge(consts, CONSTS)

            def step(s, u):
                def tokens():
                    i, p = item(s, u, E)
                    if i is not None:
                        act.wait_ge(xt_ps, i + 1)
                        at_least(act, v_ps, i)
                        nc.scalar.copy(xT[:], ps_front[0:KC, :].rearrange("p (c t) -> p c t", c=2)).then_inc(xt_done, 1)

                def value():
                    i, p = item(s, u, PR)
                    if i is not None:
                        act.wait_ge(v_ps, i + 1)
                        at_least(act, av_ps, i - 1)
                        nc.scalar.copy(V[p][:, :, :, 0:DH],
                                       ps_front[:, 0:2 * D].rearrange("p (t h d) -> p t h d", t=2, h=HEADS))\
                            .then_inc(v_done, 1)

                def first_part(t):
                    i, p = item(s, u, PR)
                    if i is not None:
                        act.wait_ge(qk_done, 2 * i + t + 1)
                        at_least(act, stack_ps, NT * (i - 1))
                        nc.scalar.copy(stack[p][:, t, :, :, 0, :], four(qk[:, t])).then_inc(hi_done, 1)

                def second_part(t):
                    i, p = item(s, u, PR)
                    if i is not None:
                        act.wait_ge(rest_done, 2 * i + t + 1)
                        nc.scalar.copy(stack[p][:, t, 0, :, 1, :], four(rest[:, t])[:, 0])
                        nc.scalar.copy(stack[p][:, t, 1, :, 2, :], four(rest[:, t])[:, 1]).then_inc(mid_done, 1)

                def stacks(k):
                    i, p = item(s, u, M)
                    if i is not None:
                        act.wait_ge(stack_ps, NT * i + k + 1)
                        at_least(act, sk_ps, NS * (i - 1))
                        nc.scalar.copy(stack_dst(k, p), stack_bank(k)[:, :, 0:TOK]).then_inc(stack_act, 1)

                def maxima():
                    i, p = item(s, u, O)
                    if i is not None:
                        act.wait_ge(mt_ps, i + 1)
                        at_least(act, mrows_in, 16 * i)
                        m_bank = ps_b[0][0:MROWS * HEADS, 0:PADT // 2].bitcast(BF16)
                        nc.scalar.copy(mT[:, T1:TOK], m_bank[:, 0:P])
                        nc.scalar.copy(mT[:, 0:T1], m_bank[:, P:TOK]).then_inc(mt_done, 1)

                def exponentials(k):
                    i, p = item(s, u, O)
                    if i is not None:
                        heads, small = score_banks(k)
                        n = len(heads)
                        act.wait_ge(sk_ps, NS * i + k + 1)
                        at_least(act, av_ps, i)
                        rows, width, dst = (T1, T1, probs1) if small else (P, TOK, probs0)
                        nc.scalar.activation(dst[:, heads[0]:heads[0] + n],
                                             ps_c[k % 2][0:rows, 0:n * width].rearrange("p (h q) -> p h q", h=n),
                                             ACT.Exp, scale=SCALE).then_inc(exp_done, 1)

                def outputs():
                    i, p = item(s, u, O)
                    if i is not None:
                        act.wait_ge(av_ps, i + 1)
                        at_least(act, ot_ps, i)
                        nc.scalar.copy(OT[:, 0:2, 0:TOK], ps_o[:, 0, 0:2 * TOK].rearrange("p (g q) -> p g q", g=2))
                        nc.scalar.copy(OT[:, 2, 0:TOK], ps_o[:, 1, 0:TOK]).then_inc(o_done, 1)

                def normalized():
                    i, p = item(s, u, O)
                    if i is not None:
                        act.wait_ge(ont_ps, i + 1)
                        at_least(act, y_ps, i)
                        nc.scalar.copy(ONT[:], ps_c[1][0:KC, :].rearrange("p (c t) -> p c t", c=2)).then_inc(ont_done, 1)

                maxima()
                stacks(0)
                first_part(0)
                stacks(1)
                exponentials(0)
                second_part(0)
                exponentials(1)
                stacks(3)
                exponentials(2)
                stacks(4)
                first_part(1)
                exponentials(3)
                exponentials(4)
                second_part(1)
                for k in range(5, NS):
                    exponentials(k)
                outputs()
                value()
                tokens()
                normalized()
            pipeline(act, IMG, DEPTH, LEAD, step)

        @block.vector
        def _(dve):
            dve.wait_ge(weights_in, 16 * n_weights)
            dve.wait_ge(consts, CONSTS)

            def step(s, u):
                def statistics():
                    i, p = item(s, u, E)
                    if i is None:
                        return
                    if embed:
                        dve.wait_ge(tok_done, i + 1)
                        at_least(dve, h_kept, 16 * (i - 1))
                        nc.vector.tensor_tensor(h[:, p], ps_front[:, 0:2 * D].rearrange("p (t d) -> p t d", t=2),
                                                tok_add[:], ALU.add).then_inc(h_ready, 1)
                    else:
                        dve.wait_ge(h_in_sem, 16 * (i + 1))
                        dve.wait_ge(rows_in, 32 * (i + 1))
                        at_least(dve, h_kept, 16 * (i - 1))
                        nc.vector.tensor_tensor(h[:, p], h_before[:, p], gathered[:, p], ALU.add).then_inc(h_ready, 1)
                    dve.wait_ge(h_ready, i + 1)
                    for t in range(2):
                        nc.vector.bn_stats(stats[:, t], h[:, p, t]).then_inc(stats_done, 1)
                    wait_apart(dve, veps_done, i, passed_dve)
                    wait_apart(dve, stats_done, 2 * (i + 1), passed_dve)
                    for t in range(2):
                        nc.vector.bn_aggr(mv[:, t], stats[:, t]).then_inc(mv_done, 1)

                def normalize():
                    i, p = item(s, u, E)
                    if i is not None:
                        dve.wait_ge(rstd_done, i + 1)
                        at_least(dve, xt_ps, i)
                        for t in range(2):
                            nc.vector.tensor_scalar(xn[:, t], h[:, p, t], mv[:, t, 0:1], rstd[:, t:t + 1],
                                                    ALU.subtract, ALU.mult).then_inc(xn_done, 1)

                def rotate(t):
                    i, p = item(s, u, PR)
                    if i is None:
                        return
                    n = 2 * i + t + 1
                    dve.wait_ge(qk_ps, n)
                    q = ps_qk[:, 0:2 * D]
                    if rope:
                        at_least(dve, qk_done, n - 2)
                        bc = cos[:, t, None, :].broadcast_to([P, 2, D])
                        nc.vector.tensor_tensor(rc[:, t].rearrange("p (j d) -> p j d", j=2),
                                                q.rearrange("p (j d) -> p j d", j=2), bc, ALU.mult).then_inc(rope_done, 1)
                        for e in range(2):
                            qs = q.rearrange("p (j d e) -> p j d e", j=2, e=2)[:, :, :, 1 - e]
                            sn = sin[:, t, :].rearrange("p (d e) -> p d e", e=2)[:, None, :, e].broadcast_to([P, 2, D // 2])
                            nc.vector.tensor_tensor(rs[:, t].rearrange("p (j d e) -> p j d e", j=2, e=2)[:, :, :, e],
                                                    qs, sn, ALU.mult).then_inc(rope_done, 1)
                    else:
                        at_least(dve, rest_done, n - 2)
                        nc.vector.tensor_copy(qk[:, t], q).then_inc(qk_done, 1)

                def stacks(k):
                    i, p = item(s, u, M)
                    if i is not None:
                        dve.wait_ge(stack_ps, NT * i + k + 1)
                        at_least(dve, sk_ps, NS * (i - 1))
                        nc.vector.tensor_copy(stack_dst(k, p), stack_bank(k)[:, :, 0:TOK]).then_inc(stack_dve, 1)

                def maximum(k):
                    i, p = item(s, u, M)
                    if i is not None:
                        heads, small = score_banks(k)
                        n = len(heads)
                        if k == 0:
                            at_least(dve, nm_sem, 5 * i)
                        dve.wait_ge(sq_ps, NS * i + k + 1)
                        rows, width, t = (T1, T1, 1) if small else (P, TOK, 0)
                        nc.vector.tensor_reduce(mx[0:rows, t, heads[0]:heads[0] + n],
                                                ps_b[k % 2][0:rows, 0:n * width].rearrange("p (h q) -> p h q", h=n),
                                                AX_X, ALU.max).then_inc(max_done, 1)

                def duplicate(t):
                    i, p = item(s, u, PR)
                    if i is not None:
                        dve.wait_ge(mid_done, 2 * i + t + 1)
                        q, k = stack[p][:, t, 0], stack[p][:, t, 1]
                        nc.vector.tensor_copy(q[:, :, 2:4], q[:, :, 0:2]).then_inc(dup_done, 1)
                        nc.vector.tensor_copy(q[:, :, 5], q[:, :, 0]).then_inc(dup_done, 1)
                        nc.vector.tensor_copy(k[:, :, 1:5:3], k[:, :, 0:1].broadcast_to([P, HEADS, 2, DH])).then_inc(dup_done, 1)
                        nc.vector.tensor_copy(k[:, :, 3], k[:, :, 2]).then_inc(dup_done, 1)

                def divide():
                    i, p = item(s, u, O)
                    if i is not None:
                        dve.wait_ge(ot_ps, i + 1)
                        at_least(dve, ont_ps, i)
                        o = ps_o[:, :, 0:2 * D].rearrange("p t (h e) -> p t h e", h=HEADS)
                        nc.vector.reciprocal(inv[:], o[:, :, :, DH]).then_inc(inv_done, 1)
                        dve.wait_ge(inv_done, i + 1)
                        for t in range(2):
                            nc.vector.tensor_tensor(ON[:, t], o[:, t, :, 0:DH], inv[:, t, :, None].broadcast_to([P, HEADS, DH]),
                                                    ALU.mult).then_inc(on_done, 1)

                def residual():
                    i, p = item(s, u, Y)
                    if i is not None:
                        dve.wait_ge(y_ps, i + 1)
                        dve.wait_ge(hres_in, 16 * (i + 1))
                        at_least(dve, y_out, 16 * (i - 1))
                        nc.vector.tensor_tensor(y[:, p], ps_c[0][:, 0:2 * D].rearrange("p (t d) -> p t d", t=2),
                                                h_res[:, p], ALU.add).then_inc(y_done, 1)

                rotate(0)
                residual()
                rotate(1)
                statistics()
                stacks(2)
                normalize()
                stacks(5)
                duplicate(0)
                maximum(0)
                maximum(1)
                maximum(2)
                maximum(3)
                duplicate(1)
                maximum(4)
                maximum(5)
                divide()
                maximum(6)
                maximum(7)
            pipeline(dve, IMG, DEPTH, LEAD, step)

        @block.tensor
        def _(pe):
            pe.wait_ge(weights_in, 16 * n_weights)
            pe.wait_ge(consts, CONSTS)
            pe.wait_ge(ident_sem, 1)
            mm = nc.tensor.matmul

            def scores(bank, k, left, right, rows, first, mask, big):
                heads, small = score_banks(k)
                (l0, l1), (r0, r1), m0 = first if small else big
                width = r1 - r0
                for n, hd in enumerate(heads):
                    mm(bank[0:l1 - l0, n * width:(n + 1) * width], left[0:rows, hd, l0:l1], right[0:rows, hd, r0:r1],
                       start=(n == 0), stop=False, skip_group_check=True)
                span = width - m0 if m0 else min(width, l1 - l0)
                out = bank[0:l1 - l0, 0:len(heads) * width].rearrange("p (h q) -> p h q", h=len(heads))[:, :, m0:m0 + span]
                rhs = mask[0:l1 - l0, None, 0:span].broadcast_to([l1 - l0, len(heads), span])
                return mm(out, ident_b[0:l1 - l0, 0:l1 - l0], rhs, start=False, stop=True, skip_group_check=True)

            def step(s, u):
                def embedding(pieces):
                    i, p = item(s, u, E)
                    if i is None or not embed:
                        return
                    for n in pieces:
                        t, c = divmod(n, PC)
                        if n == 0:
                            pe.wait_ge(patches_in, 16 * (i + 1))
                            at_least(pe, xt_done, i)
                        last = mm(ps_front[:, t * D:(t + 1) * D], patches[:, p, c, t * P:(t + 1) * P], w_tok[:, c],
                                  start=(c == 0), stop=(c == PC - 1))
                        if n == 2 * PC - 1:
                            last.then_inc(tok_done, 1)

                def transpose_tokens():
                    i, p = item(s, u, E)
                    if i is None:
                        return
                    pe.wait_ge(xn_done, 2 * (i + 1))
                    at_least(pe, v_done, i)
                    for c in range(2):
                        for t in range(2):
                            last = nc.tensor.transpose(ps_front[0:KC, c * PADT + t * P:c * PADT + (t + 1) * P],
                                                       xn[:, t, c * KC:(c + 1) * KC], ident[:])
                    last.then_inc(xt_ps, 1)

                def project_qk(t):
                    i, p = item(s, u, PR)
                    if i is None:
                        return
                    pe.wait_ge(xt_done, i + 1)
                    at_least(pe, rope_done if rope else qk_done, (3 if rope else 1) * (2 * i + t))
                    for c in range(2):
                        last = mm(ps_qk[:, 0:2 * D], xT[:, c, t * P:(t + 1) * P], wqk[:, c], start=(c == 0), stop=(c == 1))
                    last.then_inc(qk_ps, 1)

                def project_v():
                    i, p = item(s, u, PR)
                    if i is None:
                        return
                    if embed:
                        if item(s, u, E)[0] is not None:
                            pe.wait_ge(h_ready, i + 2)
                    else:
                        pe.wait_ge(xt_done, i + 1)
                    for t in range(2):
                        for c in range(2):
                            last = mm(ps_front[:, t * D:(t + 1) * D], xT[:, c, t * P:(t + 1) * P], wv[:, c],
                                      start=(c == 0), stop=(c == 1))
                    last.then_inc(v_ps, 1)

                def transpose_stacks(k):
                    i, p = item(s, u, M)
                    if i is None:
                        return
                    if k == 0:
                        pe.wait_ge(lo_done, 4 * (i + 1))
                        pe.wait_ge(dup_done, DUPS * (i + 1))
                        at_least(pe, mt_done, i)
                    elif k == 1:
                        at_least(pe, max_done, NS * i)
                    elif k - 2 in ACT_T:
                        pe.wait_ge(stack_act, len(ACT_T) * i + ACT_T.index(k - 2) + 1)
                    else:
                        pe.wait_ge(stack_dve, len(DVE_T) * i + DVE_T.index(k - 2) + 1)
                    for n in range(4):
                        for t in range(2):
                            last = nc.tensor.transpose(stack_bank(k)[:, n, t * P:(t + 1) * P],
                                                       stack[p][:, t, k // 3, 4 * (k % 3) + n].rearrange("p s d -> p (s d)"),
                                                       ident_b[:])
                    last.then_inc(stack_ps, 1)

                def row_scores(k):
                    i, p = item(s, u, M)
                    if i is None:
                        return
                    if k < 2:
                        pe.wait_ge(stack_act, len(ACT_T) * (i + 1))
                        pe.wait_ge(stack_dve, len(DVE_T) * (i + 1))
                    else:
                        pe.wait_ge(max_done, NS * i + k - 1)
                    scores(ps_b[k % 2], k, QT[p], KT[p], SK, ((0, T1), (0, T1), 0), mask_q,
                           ((T1, TOK), (0, TOK), T1)).then_inc(sq_ps, 1)

                def transpose_maxima():
                    i, p = item(s, u, O)
                    if i is None:
                        return
                    wait_apart(pe, nm_sem, 5 * (i + 1), passed_pe)
                    m_bank = ps_b[0][0:MROWS * HEADS, 0:PADT // 2].bitcast(BF16)
                    parts = nm_parts[:].rearrange("p t r h -> p t (r h)")
                    nc.tensor.transpose(m_bank[:, 0:P], parts[:, 0], ident_b[:])
                    nc.tensor.transpose(m_bank[:, P:TOK], parts[0:T1, 1], ident_b[0:T1, 0:T1]).then_inc(mt_ps, 1)

                def key_scores(k):
                    i, p = item(s, u, O)
                    if i is None:
                        return
                    if k == 0:
                        pe.wait_ge(mrows_in, 16 * (i + 1))
                        at_least(pe, y_done, i)
                    elif k == 1:
                        at_least(pe, ont_done, i)
                    else:
                        pe.wait_ge(exp_done, NS * i + k - 1)
                    scores(ps_c[k % 2], k, KT[p], QT[p], SK + MROWS, ((P, TOK), (P, TOK), 0), mask_k,
                           ((0, P), (0, TOK), 0)).then_inc(sk_ps, 1)

                def weigh_values():
                    i, p = item(s, u, O)
                    if i is None:
                        return
                    pe.wait_ge(exp_done, NS * (i + 1))
                    pe.wait_ge(v_done, i + 1)
                    at_least(pe, on_done, 2 * i)
                    for hd in range(HEADS):
                        g, q0 = hd // 4, 32 * (hd % 4)
                        o = ps_o[q0:q0 + 2 * DH, g // 2, (g % 2) * TOK:(g % 2 + 1) * TOK]
                        mm(o, V[p][:, 0, hd], probs0[:, hd], start=True, stop=True, tile_position=(0, q0))
                        last = mm(o[:, P:TOK], V[p][0:T1, 1, hd], probs1[:, hd], start=False, stop=True,
                                  tile_position=(0, q0), skip_group_check=True)
                    last.then_inc(av_ps, 1)

                def transpose_outputs():
                    i, p = item(s, u, O)
                    if i is None:
                        return
                    pe.wait_ge(o_done, i + 1)
                    for t in range(2):
                        for g in range(3):
                            last = nc.tensor.transpose(ps_o[:, t, g * P:(g + 1) * P], OT[:, g, t * P:(t + 1) * P], ident[:])
                    last.then_inc(ot_ps, 1)

                def transpose_normalized():
                    i, p = item(s, u, O)
                    if i is None:
                        return
                    pe.wait_ge(on_done, 2 * (i + 1))
                    for c in range(2):
                        for t in range(2):
                            last = nc.tensor.transpose(ps_c[1][0:KC, c * PADT + t * P:c * PADT + (t + 1) * P],
                                                       ON[:, t].rearrange("p h d -> p (h d)")[:, c * KC:(c + 1) * KC], ident[:])
                    last.then_inc(ont_ps, 1)

                def project_output():
                    i, p = item(s, u, Y)
                    if i is None:
                        return
                    pe.wait_ge(ont_done, i + 1)
                    for t in range(2):
                        for c in range(2):
                            last = mm(ps_c[0][:, t * D:(t + 1) * D], ONT[:, c, t * P:(t + 1) * P], wo[:, c],
                                      start=(c == 0), stop=(c == 1))
                    last.then_inc(y_ps, 1)

                embedding(range(0, 4))
                project_qk(0)
                project_output()
                transpose_maxima()
                embedding(range(4, 8))
                transpose_stacks(0)
                transpose_stacks(1)
                project_qk(1)
                embedding(range(8, 12))
                key_scores(0)
                transpose_stacks(2)
                key_scores(1)
                transpose_stacks(3)
                key_scores(2)
                transpose_stacks(4)
                key_scores(3)
                transpose_stacks(5)
                for k in range(4):
                    key_scores(4 + k)
                    row_scores(k)
                weigh_values()
                row_scores(4)
                row_scores(5)
                project_v()
                transpose_outputs()
                row_scores(6)
                row_scores(7)
                transpose_tokens()
                transpose_normalized()
            pipeline(pe, IMG, DEPTH, LEAD, step)


def ffn_phase(nc, name, passed, h_in, h_out, w, tables, experts, act_fn, mix, last):
    pairs = IMG // 2
    moe = experts > 1
    with ExitStack() as ctx:
        def sb(n, shape, dt=F32):
            return ctx.enter_context(nc.sbuf_tensor(f"{name}_{n}", shape, dt))

        def sem(n):
            return ctx.enter_context(nc.semaphore(f"{name}_{n}"))

        def psum(n, shape, dt=F32):
            return ctx.enter_context(nc.psum_tensor(f"{name}_{n}", shape, dt))

        ident = sb("ident", [P, P])
        neg_half = sb("neg_half", [P, 4])
        w1 = sb("w1", [KC, experts, 2, HIDDEN])
        b1 = sb("b1", [P, experts, HC])
        w2 = sb("w2", [P, experts, HC, D])
        b2 = sb("b2", [P, experts, D])
        if moe:
            wg = sb("wg", [KC, 2, EXPERTS])
            bg = sb("bg", [P, 4, EXPERTS])
            logits = sb("logits", [P, 4, EXPERTS])
            top = sb("top", [P, 4])
            eq = sb("eq", [P, 4, EXPERTS])
            taken = sb("taken", [P, EXPERTS - 1, 4])
            onehot = [sb(f"onehot{u}", [P, EXPERTS, 4]) for u in range(2)]
            tmp = sb("tmp", [P, 2, 2, D])
        h = [sb(f"h{u}", [P, 4, D]) for u in range(2)]
        stats = sb("stats", [P, 4, 6])
        mv = sb("mv", [P, 4, 2])
        veps = sb("veps", [P, 4])
        rstd = sb("rstd", [P, 4])
        xn = sb("xn", [P, 4, D])
        xT = [sb(f"xT{u}", [KC, 2, 2, PADT]) for u in range(2)]
        hid = [sb(f"hid{u}", [P, HC, 2, PADT]) for u in range(2)]
        y = [sb(f"y{u}", [P, 4, D]) for u in range(2)]
        ps_x = [psum(f"ps_x{n}", [P, 512]) for n in range(2)]
        ps_up = [psum(f"ps_up{n}", [P, 512]) for n in range(2)]
        ps_y = [psum(f"ps_y{n}", [P, 2, 512]) for n in range(2)]

        passed_sp, passed_pool, passed_dve, _ = passed
        weights_in, mixed, consts = sem("weights_in"), sem("mixed"), sem("consts")
        h_in_sem = sem("h_in")
        stats_done, mv_done, veps_done, rstd_done = sem("stats_done"), sem("mv_done"), sem("veps_done"), sem("rstd_done")
        xn_done, xt_ps, xt_done = sem("xn_done"), sem("xt_ps"), sem("xt_done")
        gate_ps, gate_step = sem("gate_ps"), sem("gate_step")
        up_ps, gelu_done, down_ps, y_taken = sem("up_ps"), sem("gelu_done"), sem("down_ps"), sem("y_taken")
        tmp_done, acc_done, y_done, y_out = sem("tmp_done"), sem("acc_done"), sem("y_done"), sem("y_out")
        GATE = 3 + 2 * (EXPERTS - 1) + 1
        n_weights = 5 + 2 * moe
        MIXED = 4 + 3 + 9 * 3 + 1 + 4
        if mix:
            alpha_e = sb("alpha_e", [P, 3])
            alpha_r = sb("alpha_r", [P, 3])
            in_mask = sb("in_mask", [KC, 2, 3])
            out_mask = sb("out_mask", [P, HC, 9])
            a = sb("a", [P, 3, 3])
            a_in = sb("a_in", [KC, 2, 3, 3])
            a_out = sb("a_out", [P, HC, 9])
            c_up = sb("c_up", [KC, 2, HIDDEN])
            c_down = sb("c_down", [P, HC, D])
            c_b1 = sb("c_b1", [P, HC])
            c_b2 = sb("c_b2", [P, D])
            n_weights += 4
        block = ctx.enter_context(nc.Block())

        def job_of(i, e, u):
            return experts * i + e, (experts * u + e) % 2

        @block.sync
        def _(sp):
            sp.dma_start(ident[:], tables["ident"]).then_inc(weights_in, 16)
            sp.dma_start(w1[:], w["w1"]).then_inc(weights_in, 16)
            sp.dma_start(b1[:], w["b1"]).then_inc(weights_in, 16)
            sp.dma_start(w2[:], w["w2"]).then_inc(weights_in, 16)
            sp.dma_start(b2[:], w["b2"]).then_inc(weights_in, 16)
            if moe:
                sp.dma_start(wg[:], w["wg"]).then_inc(weights_in, 16)
                sp.dma_start(bg[:], w["bg"]).then_inc(weights_in, 16)
            if mix:
                sp.dma_start(alpha_e[:], w["alpha_e"]).then_inc(weights_in, 16)
                sp.dma_start(alpha_r[:], w["alpha_r"]).then_inc(weights_in, 16)
                sp.dma_start(in_mask[:], tables["in_mask"]).then_inc(weights_in, 16)
                sp.dma_start(out_mask[:], tables["out_mask"]).then_inc(weights_in, 16)

            def load(i, p):
                wait_apart(sp, h_in_sem, 16 * i, passed_sp)
                wait_apart(sp, y_done, i - 1, passed_sp)
                src = h_in[bass.ds(2 * i, 2)] if not isinstance(i, int) else h_in[2 * i:2 * i + 2]
                sp.dma_start(h[p][:].rearrange("p (g t) d -> p g t d", g=2), src.rearrange("g p t d -> p g t d"))\
                    .then_inc(h_in_sem, 16)

            def step(s, u):
                if isinstance(s, int) and s == 0:
                    load(0, 0)
                if not isinstance(s, int) or s + 1 < pairs:
                    load(s + 1, 1 - u)
                if not isinstance(s, int) or s >= 1:
                    i, p = s - 1, 1 - u
                    wait_apart(sp, y_out, 16 * (4 if last else 2) * i, passed_sp)
                    wait_apart(sp, y_done, i + 1, passed_sp)
                    if last:
                        for g in range(2):
                            sp.dma_start(h_out[2 * i + g, 0:P], y[p][:, 2 * g]).then_inc(y_out, 16)
                            sp.dma_start(h_out[2 * i + g, P:TOK], y[p][0:T1, 2 * g + 1]).then_inc(y_out, 16)
                    else:
                        for g in range(2):
                            sp.dma_start(h_out[2 * i + g], y[p][:, 2 * g:2 * g + 2]).then_inc(y_out, 16)
            pipeline(sp, pairs, 2, 4, step)
            sp.wait_ge(y_out, 16 * (4 if last else 2) * pairs)

        @block.gpsimd
        def _(pool):
            nc.gpsimd.memset(neg_half[:], -0.5).then_inc(consts, 1)
            for u in range(2):
                pool.wait_ge(consts, u + 1)
                nc.gpsimd.memset(hid[u][:, :, :, TOK:PADT], 0.0).then_inc(consts, 1)
            pool.wait_ge(consts, 3)

            def step(s, u):
                if not isinstance(s, int) or s < pairs:
                    wait_apart(pool, mv_done, 4 * (s + 1), passed_pool)
                    nc.gpsimd.tensor_scalar_add(veps[:], mv[:, :, 1], EPS).then_inc(veps_done, 1)
                    pool.wait_ge(veps_done, s + 1)
                    nc.gpsimd.tensor_tensor(rstd[:], veps[:], neg_half[:], ALU.pow).then_inc(rstd_done, 1)
            pipeline(pool, pairs, 2, 4, step)

        @block.scalar
        def _(act):
            act.wait_ge(weights_in, 16 * n_weights)
            act.wait_ge(consts, 3)
            if mix:
                act.wait_ge(mixed, MIXED)

            def gelu(s, u, e):
                i, p = s - 1, 1 - u
                job, b = job_of(i, e, p)
                for m in range(HC):
                    act.wait_ge(up_ps, HC * job + m + 1)
                    at_least(act, down_ps, job - 1)
                    nc.scalar.activation(hid[b][:, m, :, 0:TOK],
                                         ps_up[m % 2][:, 0:2 * TOK].rearrange("p (g t) -> p g t", g=2),
                                         act_fn, bias=b1[:, e, m:m + 1]).then_inc(gelu_done, 1)

            def step(s, u):
                if not isinstance(s, int) or s >= 1:
                    gelu(s, u, 0)
                if not isinstance(s, int) or s < pairs:
                    act.wait_ge(xt_ps, s + 1)
                    at_least(act, down_ps, experts * (s - 1))
                    for c in range(2):
                        nc.scalar.copy(xT[u][:, c].rearrange("p g t -> p (g t)"), ps_x[c][0:KC]).then_inc(xt_done, 1)
                if not isinstance(s, int) or s >= 1:
                    for e in range(1, experts):
                        gelu(s, u, e)
            pipeline(act, pairs, 2, 4, step)

        @block.vector
        def _(dve):
            dve.wait_ge(weights_in, 16 * n_weights)
            if mix:
                mixes = [0]

                def mixing(ins):
                    mixes[0] += 1
                    ins.then_inc(mixed, 1)
                    dve.wait_ge(mixed, mixes[0])
                tt = nc.vector.tensor_tensor
                mixing(tt(a[:], alpha_e[:, :, None].broadcast_to([P, 3, 3]), alpha_r[:, None, :].broadcast_to([P, 3, 3]), ALU.mult))
                mixing(nc.vector.memset(c_up[:], 0.0))
                mixing(nc.vector.memset(c_down[:], 0.0))
                mixing(nc.vector.memset(c_b2[:], 0.0))
                for c in range(2):
                    mixing(tt(a_in[:, c], a[0:KC], in_mask[:, c, :, None].broadcast_to([KC, 3, 3]), ALU.mult))
                mixing(tt(a_out[:], a[:, None].rearrange("p o i j -> p o (i j)").broadcast_to([P, HC, 9]), out_mask[:], ALU.mult))
                for i, width in enumerate(E_CHOICES):
                    for j, ratio in enumerate(R_CHOICES):
                        n = ratio * width
                        mixing(tt(c_up[:, :, 0:n], c_up[:, :, 0:n], a_in[:, :, i, j:j + 1].broadcast_to([KC, 2, n]), ALU.add))
                        mixing(tt(c_down[:, :, 0:width], c_down[:, :, 0:width],
                                  a_out[:, :, 3 * i + j:3 * i + j + 1].broadcast_to([P, HC, width]), ALU.add))
                        mixing(nc.vector.tensor_scalar_add(c_b2[:, 0:width], c_b2[:, 0:width], a[:, i, j:j + 1]))
                mixing(nc.vector.tensor_reduce(c_b1[:], a_out[:], AX_X, ALU.add))
                mixing(tt(w1[:, 0], w1[:, 0], c_up[:], ALU.mult))
                mixing(tt(w2[:, 0], w2[:, 0], c_down[:], ALU.mult))
                mixing(tt(b1[:, 0], b1[:, 0], c_b1[:], ALU.mult))
                mixing(tt(b2[:, 0], b2[:, 0], c_b2[:], ALU.mult))
                assert mixes[0] == MIXED, mixes

            def combine(s, u, e):
                i, p = s - 1, 1 - u
                job, b = job_of(i, e, p)
                src = ps_y[b][:, :, 0:2 * D].rearrange("p g (t d) -> p g t d", t=2)
                dve.wait_ge(down_ps, job + 1)
                if e == 0:
                    at_least(dve, y_out, 16 * (4 if last else 2) * (i - 1))
                if moe:
                    at_least(dve, acc_done, 4 * job)
                    for g in range(2):
                        nc.vector.tensor_tensor(tmp[:, g], src[:, g], b2[:, e, None, :].broadcast_to([P, 2, D]), ALU.add)\
                            .then_inc(tmp_done, 1)
                    dve.wait_ge(tmp_done, 2 * (job + 1))
                    for j in range(4):
                        prev = h[p] if e == 0 else y[p]
                        acc = nc.vector.scalar_tensor_tensor(y[p][:, j], tmp[:, j // 2, j % 2], onehot[p][:, e, j:j + 1],
                                                             prev[:, j], ALU.mult, ALU.add)
                        acc.then_inc(acc_done, 1)
                    if e == experts - 1:
                        dve.wait_ge(acc_done, 4 * (job + 1))
                        dve.sem_inc(y_done, 1)
                else:
                    at_least(dve, tmp_done, 2 * job)
                    for g in range(2):
                        nc.vector.tensor_tensor(h[p][:, 2 * g:2 * g + 2], h[p][:, 2 * g:2 * g + 2],
                                                b2[:, 0, None, :].broadcast_to([P, 2, D]), ALU.add).then_inc(tmp_done, 1)
                    dve.wait_ge(tmp_done, 2 * (job + 1))
                    for g in range(2):
                        acc = nc.vector.tensor_tensor(y[p][:, 2 * g:2 * g + 2], src[:, g], h[p][:, 2 * g:2 * g + 2], ALU.add)
                    acc.then_inc(y_done, 1)

            def step(s, u):
                if not isinstance(s, int) or s < pairs:
                    i = s
                    dve.wait_ge(h_in_sem, 16 * (i + 1))
                    for j in range(4):
                        nc.vector.bn_stats(stats[:, j], h[u][:, j]).then_inc(stats_done, 1)
                    wait_apart(dve, stats_done, 4 * (i + 1), passed_dve)
                    wait_apart(dve, veps_done, i, passed_dve)
                    for j in range(4):
                        nc.vector.bn_aggr(mv[:, j], stats[:, j]).then_inc(mv_done, 1)
                    dve.wait_ge(rstd_done, i + 1)
                    at_least(dve, xt_ps, i)
                    for j in range(4):
                        nc.vector.tensor_scalar(xn[:, j], h[u][:, j], mv[:, j, 0:1], rstd[:, j:j + 1],
                                                ALU.subtract, ALU.mult).then_inc(xn_done, 1)
                if not isinstance(s, int) or s >= 1:
                    combine(s, u, 0)
                if moe and (not isinstance(s, int) or s < pairs):
                    i = s
                    k = [GATE * i]

                    def gate(ins):
                        k[0] = k[0] + 1
                        ins.then_inc(gate_step, 1)
                        dve.wait_ge(gate_step, k[0])
                    dve.wait_ge(gate_ps, i + 1)
                    gate(nc.vector.tensor_tensor(logits[:], ps_x[0][:, 0:4 * EXPERTS].rearrange("p (j n) -> p j n", j=4),
                                                 bg[:], ALU.add))
                    gate(nc.vector.tensor_reduce(top[:], logits[:], AX_X, ALU.max))
                    gate(nc.vector.tensor_tensor(eq[:], logits[:], top[:, :, None].broadcast_to([P, 4, EXPERTS]), ALU.is_equal))
                    gate(nc.vector.tensor_copy(onehot[u][:, 0], eq[:, :, 0]))
                    before = eq[:, :, 0]
                    for n in range(1, EXPERTS):
                        gate(nc.vector.tensor_tensor(onehot[u][:, n], eq[:, :, n], before, ALU.is_gt))
                        gate(nc.vector.tensor_tensor(taken[:, n - 1], eq[:, :, n], before, ALU.max))
                        before = taken[:, n - 1]
                if not isinstance(s, int) or s >= 1:
                    for e in range(1, experts):
                        combine(s, u, e)
            pipeline(dve, pairs, 2, 4, step)

        @block.tensor
        def _(pe):
            pe.wait_ge(weights_in, 16 * n_weights)
            pe.wait_ge(consts, 3)
            if mix:
                pe.wait_ge(mixed, MIXED)
            mm = nc.tensor.matmul

            def up(s, u, e):
                i, p = s - 1, 1 - u
                job, _ = job_of(i, e, p)
                pe.wait_ge(xt_done, 2 * (i + 1))
                for m in range(HC):
                    at_least(pe, gelu_done, HC * job + m - 1)
                    for c in range(2):
                        last_mm = mm(ps_up[m % 2][:, 0:2 * TOK].rearrange("p (g t) -> p g t", g=2),
                                     w1[:, e, c, m * P:(m + 1) * P], xT[p][:, c, :, 0:TOK], start=(c == 0), stop=(c == 1))
                    last_mm.then_inc(up_ps, 1)

            def down(s, u, e):
                i, p = s - 1, 1 - u
                job, b = job_of(i, e, p)
                pe.wait_ge(gelu_done, HC * (job + 1))
                at_least(pe, tmp_done if moe else y_done, (2 if moe else 1) * (job - 1))
                for g in range(2):
                    for t in range(2):
                        for m in range(HC):
                            last_mm = mm(ps_y[b][:, g, t * D:(t + 1) * D], hid[b][:, m, g, t * P:(t + 1) * P],
                                         w2[:, e, m], start=(m == 0), stop=(m == HC - 1))
                last_mm.then_inc(down_ps, 1)

            def transposes(s, u):
                pe.wait_ge(xn_done, 4 * (s + 1))
                at_least(pe, xt_done, 2 * s)
                if moe:
                    at_least(pe, gate_step, GATE * (s - 1) + 1)
                for c in range(2):
                    for j in range(4):
                        last_mm = nc.tensor.transpose(ps_x[c][0:KC, j * P:(j + 1) * P], xn[:, j, c * KC:(c + 1) * KC], ident[:])
                last_mm.then_inc(xt_ps, 1)

            def gates(s, u):
                pe.wait_ge(xt_done, 2 * (s + 1))
                for j in range(4):
                    for c in range(2):
                        last_mm = mm(ps_x[0][:, j * EXPERTS:(j + 1) * EXPERTS], xT[u][:, c, j // 2, (j % 2) * P:(j % 2 + 1) * P],
                                     wg[:, c], start=(c == 0), stop=(c == 1))
                last_mm.then_inc(gate_ps, 1)

            def step(s, u):
                do_a = not isinstance(s, int) or s < pairs
                do_b = not isinstance(s, int) or s >= 1
                if do_b:
                    up(s, u, 0)
                if do_a:
                    transposes(s, u)
                if do_b:
                    if experts > 1:
                        up(s, u, 1)
                    down(s, u, 0)
                if do_a and moe:
                    gates(s, u)
                if do_b:
                    for e in range(1, experts):
                        if e + 1 < experts:
                            up(s, u, e + 1)
                        down(s, u, e)
            pipeline(pe, pairs, 2, 4, step)


def route_phase(nc, name, passed, h_in, sorted_x, index, tables, w):
    pairs = IMG // 2
    index_all, table = index
    with ExitStack() as ctx:
        def sb(n, shape, dt=F32):
            return ctx.enter_context(nc.sbuf_tensor(f"{name}_{n}", shape, dt))

        def sem(n):
            return ctx.enter_context(nc.semaphore(f"{name}_{n}"))

        def psum(n, shape, dt=F32):
            return ctx.enter_context(nc.psum_tensor(f"{name}_{n}", shape, dt))

        tiles = n_tiles()
        ident = sb("ident", [P, P])
        neg_half = sb("neg_half", [P, 4])
        wg = sb("wg", [KC, 2, EXPERTS])
        bg = sb("bg", [P, 4, EXPERTS])
        valid = sb("valid", [P, 4])
        base = sb("base", [P, EXPERTS])
        region = sb("region", [P, EXPERTS])
        tile_no = sb("tile_no", [1, tiles])
        tile_row = sb("tile_row", [P, tiles])
        before = sb("before", [P, P], BF16)
        ones = sb("ones", [P, P], BF16)
        zeros = sb("zeros", [P, TS // P, D])
        h = [sb(f"h{u}", [P, 4, D]) for u in range(2)]
        stats = sb("stats", [P, 4, 6])
        mv = sb("mv", [P, 4, 2])
        veps = sb("veps", [P, 4])
        rstd = sb("rstd", [P, 4])
        xn = [sb(f"xn{u}", [P, 4, D]) for u in range(4)]
        xT = sb("xT", [KC, 2, 4 * P])
        logits = sb("logits", [P, 4, EXPERTS])
        top = sb("top", [P, 4])
        eq = sb("eq", [P, 4, EXPERTS])
        at_top = sb("at_top", [P, 4, EXPERTS])
        taken = sb("taken", [P, EXPERTS - 1, 4])
        onehot = sb("onehot", [P, 4, EXPERTS], BF16)
        rows = sb("rows", [P, 4, EXPERTS])
        picked = sb("picked", [P, 4, EXPERTS])
        row = sb("row", [P, 4])
        row_i = [sb(f"row_i{u}", [P, 4], I32) for u in range(2)]
        count = sb("count", [P, EXPERTS])
        more = sb("more", [P, EXPERTS, tiles])
        n_of = sb("n_of", [P, EXPERTS])
        start = sb("start", [P, EXPERTS])
        jump = sb("jump", [P, EXPERTS])
        past = sb("past", [1, EXPERTS, tiles])
        jumps = sb("jumps", [1, EXPERTS, tiles])
        total = sb("total", [1, 2, tiles])
        total2 = sb("total2", [1, tiles])
        row_all = sb("row_all", [P, 2 * IMG])
        moved = sb("moved", [P, EXPERTS - 1, 2 * IMG])
        base_i = sb("base_i", [1, EXPERTS], I32)
        ps_x = [psum(f"ps_x{n}", [P, 512]) for n in range(2)]
        ps_g = psum("ps_g", [P, 512])
        ps_r = psum("ps_r", [P, 512])

        passed_sp, passed_pool, passed_dve, _ = passed
        weights_in, consts, h_in_sem = sem("weights_in"), sem("consts"), sem("h_in")
        stats_done, mv_done, veps_done, rstd_done = sem("stats_done"), sem("mv_done"), sem("veps_done"), sem("rstd_done")
        xn_done, xt_ps, xt_done, gate_ps = sem("xn_done"), sem("xt_ps"), sem("xt_done"), sem("gate_ps")
        picks, onehot_done, rank_ps, ranks, scattered = sem("picks"), sem("onehot_done"), sem("rank_ps"), sem("ranks"), sem("scattered")
        table_step, table_done, zeroed = sem("table_step"), sem("table_done"), sem("zeroed")
        PICKS = 4 + (EXPERTS - 1)
        RANKS = 6
        WEIGHTS = 7
        CONSTS = 6
        DEPTH = 3
        L, G, R = range(DEPTH)
        block = ctx.enter_context(nc.Block())

        def item(s, u, stage):
            if isinstance(s, int) and not 0 <= s - stage < pairs:
                return None, None
            return s - stage, (u - stage) % 4

        @block.sync
        def _(sp):
            for dst, src in ((ident, "ident"), (wg, "wg"), (bg, "bg"), (valid, "valid"), (region, "region"),
                             (tile_no, "tile_no"), (tile_row, "tile_row")):
                sp.dma_start(dst[:], (w if src in w else tables)[src]).then_inc(weights_in, 16)

            def load(i, p):
                wait_apart(sp, h_in_sem, 16 * i, passed_sp)
                wait_apart(sp, xn_done, 4 * (i - 1), passed_sp)
                src = h_in[bass.ds(2 * i, 2)] if not isinstance(i, int) else h_in[2 * i:2 * i + 2]
                sp.dma_start(h[p][:].rearrange("p (g t) d -> p g t d", g=2), src.rearrange("g p t d -> p g t d"))\
                    .then_inc(h_in_sem, 16)

            def step(s, u):
                if isinstance(s, int) and s == 0:
                    load(0, 0)
                if not isinstance(s, int) or s + 1 < pairs:
                    load(s + 1, (u + 1) % 2)
            pipeline(sp, pairs, DEPTH, ROUTE_LEAD, step, 4)
            sp.wait_ge(consts, CONSTS)
            spare = EXPERTS * capacity()
            for n in range(SPARE_TILES):
                sp.dma_start(sorted_x[spare + n * TS:spare + (n + 1) * TS].rearrange("(k p) d -> p k d", p=P), zeros[:])\
                    .then_inc(zeroed, 16)
            sp.wait_ge(table_done, 1)
            for e in range(EXPERTS):
                first = sp.value_load(base_i[0:1, e:e + 1], min_val=0, max_val=spare - TS)
                sp.dma_start(sorted_x[bass.ds(first, TS)].rearrange("(k p) d -> p k d", p=P), zeros[:]).then_inc(zeroed, 16)
            sp.wait_ge(zeroed, 16 * (SPARE_TILES + EXPERTS))

        @block.gpsimd
        def _(pool):
            setup = [lambda: nc.gpsimd.memset(neg_half[:], -0.5), lambda: nc.gpsimd.memset(ones[:], 1.0),
                     lambda: nc.gpsimd.memset(before[:], 0.0), lambda: nc.gpsimd.memset(zeros[:], 0.0),
                     lambda: nc.gpsimd.memset(row_all[:], 0.0),
                     lambda: nc.gpsimd.affine_select(out=before[:], in_=before[:], compare_op=ALU.is_ge, fill=1.0, base=0,
                                                     pattern=[[-1, P]], channel_multiplier=1)]
            for n, fill in enumerate(setup):
                at_least(pool, consts, n)
                fill().then_inc(consts, 1)
            pool.wait_ge(consts, CONSTS)

            def step(s, u):
                i, p = item(s, u, L)
                if i is not None:
                    wait_apart(pool, mv_done, 4 * (i + 1), passed_pool)
                    nc.gpsimd.tensor_scalar_add(veps[:], mv[:, :, 1], EPS).then_inc(veps_done, 1)
                    pool.wait_ge(veps_done, i + 1)
                    nc.gpsimd.tensor_tensor(rstd[:], veps[:], neg_half[:], ALU.pow).then_inc(rstd_done, 1)
                i, p = item(s, u, R)
                if i is not None:
                    wait_apart(pool, ranks, RANKS * (i + 1), passed_pool)
                    wait_apart(pool, scattered, 64 * i, passed_pool)
                    for j in range(4):
                        n = P if j % 2 == 0 else T1
                        nc.gpsimd.indirect_dma_start(out=sorted_x, out_offset=bass.IndirectOffsetOnAxis(ap=row_i[p % 2][0:n, j:j + 1], axis=0),
                                                     in_=xn[p][0:n, j], in_offset=None).then_inc(scattered, 16)
            pipeline(pool, pairs, DEPTH, ROUTE_LEAD, step, 4)
            pool.wait_ge(scattered, 64 * pairs)

        @block.scalar
        def _(act):
            act.wait_ge(weights_in, 16 * WEIGHTS)

            def step(s, u):
                i, p = item(s, u, G)
                if i is not None:
                    act.wait_ge(xt_ps, i + 1)
                    at_least(act, gate_ps, i)
                    for c in range(2):
                        nc.scalar.copy(xT[:, c], ps_x[c][0:KC]).then_inc(xt_done, 1)
            pipeline(act, pairs, DEPTH, ROUTE_LEAD, step, 4)

        @block.vector
        def _(dve):
            dve.wait_ge(weights_in, 16 * WEIGHTS)
            dve.wait_ge(consts, CONSTS)
            nc.vector.tensor_copy(count[:], region[:]).then_inc(table_step, 1)
            tt = nc.vector.tensor_tensor
            for e in range(EXPERTS):
                nc.vector.memset(base[:, e:e + 1], float(e * capacity())).then_inc(table_step, 1)
            dve.wait_ge(table_step, 1 + EXPERTS)

            def step(s, u):
                i, p = item(s, u, L)
                if i is not None:
                    hp = h[p % 2]
                    dve.wait_ge(h_in_sem, 16 * (i + 1))
                    for j in range(4):
                        nc.vector.bn_stats(stats[:, j], hp[:, j]).then_inc(stats_done, 1)
                    wait_apart(dve, stats_done, 4 * (i + 1), passed_dve)
                    wait_apart(dve, veps_done, i, passed_dve)
                    for j in range(4):
                        nc.vector.bn_aggr(mv[:, j], stats[:, j]).then_inc(mv_done, 1)
                i, p = item(s, u, R)
                if i is not None:
                    k = [0]

                    def pick(ins):
                        k[0] += 1
                        ins.then_inc(picks, 1)
                        dve.wait_ge(picks, PICKS * i + k[0])
                    dve.wait_ge(gate_ps, i + 1)
                    pick(tt(logits[:], ps_g[:, 0:4 * EXPERTS].rearrange("p (j n) -> p j n", j=4), bg[:], ALU.add))
                    pick(nc.vector.tensor_reduce(top[:], logits[:], AX_X, ALU.max))
                    pick(tt(eq[:], logits[:], top[:, :, None].broadcast_to([P, 4, EXPERTS]), ALU.is_equal))
                    pick(tt(at_top[:], eq[:], valid[:, :, None].broadcast_to([P, 4, EXPERTS]), ALU.mult))
                    at_least(dve, rank_ps, i)
                    nc.vector.tensor_copy(onehot[:, :, 0], at_top[:, :, 0]).then_inc(onehot_done, 1)
                    so_far = at_top[:, :, 0]
                    for n in range(1, EXPERTS):
                        nc.vector.tensor_tensor(onehot[:, :, n], at_top[:, :, n], so_far, ALU.is_gt).then_inc(onehot_done, 1)
                        pick(tt(taken[:, n - 1], at_top[:, :, n], so_far, ALU.max))
                        so_far = taken[:, n - 1]
                i, p = item(s, u, L)
                if i is not None:
                    dve.wait_ge(rstd_done, i + 1)
                    at_least(dve, scattered, 64 * (i - 3))
                    for j in range(4):
                        nc.vector.tensor_scalar(xn[p][:, j], h[p % 2][:, j], mv[:, j, 0:1], rstd[:, j:j + 1],
                                                ALU.subtract, ALU.mult).then_inc(xn_done, 1)
                i, p = item(s, u, R)
                if i is not None:
                    k = [0]

                    def rank(ins):
                        k[0] += 1
                        ins.then_inc(ranks, 1)
                        dve.wait_ge(ranks, RANKS * i + k[0])
                    dve.wait_ge(rank_ps, i + 1)
                    rank(tt(rows[:], ps_r[:, 0:4 * EXPERTS].rearrange("p (j n) -> p j n", j=4),
                            base[:, None, :].broadcast_to([P, 4, EXPERTS]), ALU.add))
                    rank(tt(picked[:], rows[:], onehot[:], ALU.mult))
                    rank(nc.vector.tensor_reduce(row[:], picked[:], AX_X, ALU.add))
                    at_least(dve, scattered, 64 * (i - 1))
                    rank(nc.vector.tensor_copy(row_i[p % 2][:], row[:]))
                    rank(tt(base[:], base[:], ps_r[:, 4 * EXPERTS:5 * EXPERTS], ALU.add))
                    at = row_all[:, bass.ds(4 * i, 4)] if not isinstance(i, int) else row_all[:, 4 * i:4 * i + 4]
                    rank(nc.vector.tensor_copy(at, row[:]))
            pipeline(dve, pairs, DEPTH, ROUTE_LEAD, step, 4)

            steps = [1 + EXPERTS]

            def then(ins):
                steps[0] += 1
                ins.then_inc(table_step, 1)
                dve.wait_ge(table_step, steps[0])
            E = EXPERTS
            then(tt(count[:], base[:], region[:], ALU.subtract))
            then(tt(more[:], count[:, :, None].broadcast_to([P, E, tiles]), tile_row[:, None, :].broadcast_to([P, E, tiles]), ALU.is_gt))
            then(nc.vector.tensor_reduce(n_of[:], more[:], AX_X, ALU.add))
            then(nc.vector.tensor_copy(start[:], n_of[:]))
            for e in range(1, E):
                then(tt(start[:, e:e + 1], start[:, e:e + 1], start[:, e - 1:e], ALU.add))
            then(nc.vector.tensor_scalar(jump[:], n_of[:], -float(TS), float(capacity()), ALU.mult, ALU.add))
            then(tt(past[:], tile_no[:, None, :].broadcast_to([1, E, tiles]), start[0:1, :, None].broadcast_to([1, E, tiles]), ALU.is_ge))
            then(tt(jumps[:], past[:], jump[0:1, :, None].broadcast_to([1, E, tiles]), ALU.mult))
            then(nc.vector.tensor_reduce(total[:, 0], jumps[:].rearrange("o e t -> o t e"), AX_X, ALU.add))
            then(nc.vector.tensor_reduce(total[:, 1], past[:, 0:E - 1].rearrange("o e t -> o t e"), AX_X, ALU.add))
            then(tt(total2[:], total[:, 0], tile_row[0:1], ALU.add))
            then(nc.vector.tensor_copy(table[:, 0], total2[:]))
            then(nc.vector.tensor_copy(table[:, 1], total[:, 1]))
            nc.vector.tensor_copy(base_i[:], base[0:1, :]).then_inc(table_done, 1)
            for e in range(1, E):
                then(nc.vector.tensor_scalar(moved[:, e - 1], row_all[:], float(e * capacity()), jump[:, e - 1:e],
                                             ALU.is_ge, ALU.mult))
            for e in range(1, E):
                then(tt(row_all[:], row_all[:], moved[:, e - 1], ALU.subtract))
            then(nc.vector.tensor_copy(index_all[:], row_all[:]))

        @block.tensor
        def _(pe):
            pe.wait_ge(weights_in, 16 * WEIGHTS)
            pe.wait_ge(consts, CONSTS)
            mm = nc.tensor.matmul

            def step(s, u):
                i, p = item(s, u, G)
                if i is not None:
                    pe.wait_ge(xn_done, 4 * (i + 1))
                    at_least(pe, xt_done, 2 * i)
                    for c in range(2):
                        for j in range(4):
                            last = nc.tensor.transpose(ps_x[c][0:KC, j * P:(j + 1) * P], xn[p][:, j, c * KC:(c + 1) * KC], ident[:])
                    last.then_inc(xt_ps, 1)
                i, p = item(s, u, R)
                if i is not None:
                    pe.wait_ge(onehot_done, EXPERTS * (i + 1))
                    at_least(pe, ranks, RANKS * i)
                    for j in range(4):
                        mm(ps_r[:, j * EXPERTS:(j + 1) * EXPERTS], before[:], onehot[:, j], start=True, stop=(j == 0))
                        for q in range(j):
                            mm(ps_r[:, j * EXPERTS:(j + 1) * EXPERTS], ones[:], onehot[:, q], start=False, stop=(q == j - 1))
                    for j in range(4):
                        last = mm(ps_r[:, 4 * EXPERTS:5 * EXPERTS], ones[:], onehot[:, j], start=(j == 0), stop=(j == 3))
                    last.then_inc(rank_ps, 1)
                i, p = item(s, u, G)
                if i is not None:
                    pe.wait_ge(xt_done, 2 * (i + 1))
                    at_least(pe, picks, PICKS * (i - 1) + 1)
                    for j in range(4):
                        for c in range(2):
                            last = mm(ps_g[:, j * EXPERTS:(j + 1) * EXPERTS], xT[:, c, j * P:(j + 1) * P], wg[:, c],
                                      start=(c == 0), stop=(c == 1))
                    last.then_inc(gate_ps, 1)
            pipeline(pe, pairs, DEPTH, ROUTE_LEAD, step, 4)


def expert_phase(nc, name, passed, sorted_x, sorted_y, table, tables, w):
    with ExitStack() as ctx:
        def sb(n, shape, dt=F32):
            return ctx.enter_context(nc.sbuf_tensor(f"{name}_{n}", shape, dt))

        def sem(n):
            return ctx.enter_context(nc.semaphore(f"{name}_{n}"))

        def psum(n, shape, dt=F32):
            return ctx.enter_context(nc.psum_tensor(f"{name}_{n}", shape, dt))

        tiles = n_tiles()
        NK = TS // P
        ident = sb("ident", [P, P])
        w1_all = sb("w1_all", [KC, EXPERTS, 2 * HIDDEN])
        b1_all = sb("b1_all", [P, EXPERTS, HC])
        w2_all = sb("w2_all", [P, EXPERTS, HC * D])
        b2_all = sb("b2_all", [P, EXPERTS, D])
        w1 = [sb(f"w1_{u}", [KC, 2, HIDDEN]) for u in range(2)]
        b1 = [sb(f"b1_{u}", [P, HC]) for u in range(2)]
        w2 = [sb(f"w2_{u}", [P, HC, D]) for u in range(2)]
        b2 = [sb(f"b2_{u}", [P, D]) for u in range(2)]
        x = [sb(f"x{u}", [P, NK, D]) for u in range(2)]
        xT = [sb(f"xT{u}", [KC, 2, TS]) for u in range(2)]
        hid = [sb(f"hid{u}", [P, HC, TS]) for u in range(2)]
        y = [sb(f"y{u}", [P, NK, D]) for u in range(2)]
        ps_x = [psum(f"ps_x{n}", [P, 512]) for n in range(2)]
        ps_up = [psum(f"ps_up{n}", [P, 512]) for n in range(2)]
        ps_y = [psum(f"ps_y{n}", [P, 2, 512]) for n in range(2)]

        passed_sp, _, passed_dve, _ = passed
        weights_in, x_in, picked = sem("weights_in"), sem("x_in"), sem("picked")
        xt_ps, xt_done = sem("xt_ps"), sem("xt_done")
        up_ps, gelu_done, down_ps, y_done, y_out = sem("up_ps"), sem("gelu_done"), sem("down_ps"), sem("y_done"), sem("y_out")
        WEIGHTS = 5
        block = ctx.enter_context(nc.Block())

        def item(s, u, stage):
            if isinstance(s, int) and not 0 <= s - stage < tiles:
                return None, None
            return s - stage, (u - stage) % 2

        def rows_of(eng, i):
            at = table[0:1, 0, i:i + 1] if isinstance(i, int) else table[0:1, 0, bass.ds(i, 1)]
            return eng.value_load(at, min_val=0, max_val=EXPERTS * capacity() + (SPARE_TILES - 1) * TS)

        @block.sync
        def _(sp):
            for dst, src in ((ident, tables["ident"]), (w1_all, w["w1"].rearrange("p e c n -> p e (c n)")), (b1_all, w["b1"]),
                             (w2_all, w["w2"].rearrange("p e c n -> p e (c n)")), (b2_all, w["b2"])):
                sp.dma_start(dst[:], src).then_inc(weights_in, 16)

            def step(s, u):
                i, p = item(s, u, 0)
                if i is not None:
                    wait_apart(sp, x_in, 16 * i, passed_sp)
                    wait_apart(sp, xt_ps, i - 1, passed_sp)
                    sp.dma_start(x[p][:], sorted_x[bass.ds(rows_of(sp, i), TS)].rearrange("(k p) d -> p k d", p=P))\
                        .then_inc(x_in, 16)
                i, p = item(s, u, 2)
                if i is not None:
                    wait_apart(sp, y_out, 16 * i, passed_sp)
                    wait_apart(sp, y_done, i + 1, passed_sp)
                    at = sorted_y[i * TS:(i + 1) * TS] if isinstance(i, int) else sorted_y[bass.ds(i * TS, TS)]
                    sp.dma_start(at.rearrange("(k p) d -> p k d", p=P), y[p][:])\
                        .then_inc(y_out, 16)
            pipeline(sp, tiles, 3, LEAD, step)
            sp.wait_ge(y_out, 16 * tiles)

        @block.scalar
        def _(act):
            def step(s, u):
                i, p = item(s, u, 2)
                if i is not None:
                    act.wait_ge(picked, 4 * (i + 1))
                    for m in range(HC):
                        act.wait_ge(up_ps, HC * i + m + 1)
                        at_least(act, down_ps, i - 1)
                        nc.scalar.activation(hid[p][:, m], ps_up[m % 2][:, 0:TS], ACT.Gelu, bias=b1[p][:, m:m + 1])\
                            .then_inc(gelu_done, 1)
                i, p = item(s, u, 1)
                if i is not None:
                    act.wait_ge(xt_ps, i + 1)
                    at_least(act, up_ps, HC * (i - 1))
                    for c in range(2):
                        nc.scalar.copy(xT[p][:, c], ps_x[c][0:KC, 0:TS]).then_inc(xt_done, 1)
            pipeline(act, tiles, 3, LEAD, step)

        @block.vector
        def _(dve):
            dve.wait_ge(weights_in, 16 * WEIGHTS)

            def step(s, u):
                i, p = item(s, u, 1)
                if i is not None:
                    at = table[0:1, 1, i:i + 1] if isinstance(i, int) else table[0:1, 1, bass.ds(i, 1)]
                    expert = dve.value_load(at, min_val=0, max_val=EXPERTS - 1)
                    wait_apart(dve, down_ps, i - 1, passed_dve)
                    wait_apart(dve, y_done, i - 1, passed_dve)
                    for dst, src in ((w1[p][:].rearrange("p c n -> p (c n)"), w1_all), (b1[p][:], b1_all),
                                     (w2[p][:].rearrange("p c n -> p (c n)"), w2_all), (b2[p][:], b2_all)):
                        nc.vector.tensor_copy(dst, src[:, bass.ds(expert, 1)].rearrange("p o n -> p (o n)")).then_inc(picked, 1)
                i, p = item(s, u, 2)
                if i is not None:
                    dve.wait_ge(down_ps, i + 1)
                    at_least(dve, y_out, 16 * (i - 1))
                    nc.vector.tensor_tensor(y[p][:, 0:2], ps_y[p][:, 0, 0:2 * D].rearrange("p (k d) -> p k d", k=2),
                                            b2[p][:, None, :].broadcast_to([P, 2, D]), ALU.add)
                    nc.vector.tensor_tensor(y[p][:, 2], ps_y[p][:, 1, 0:D], b2[p][:], ALU.add).then_inc(y_done, 1)
            pipeline(dve, tiles, 3, LEAD, step)

        @block.tensor
        def _(pe):
            pe.wait_ge(weights_in, 16 * WEIGHTS)
            mm = nc.tensor.matmul

            def step(s, u):
                i, p = item(s, u, 2)
                if i is not None:
                    pe.wait_ge(xt_done, 2 * (i + 1))
                    pe.wait_ge(picked, 4 * (i + 1))
                    for m in range(HC):
                        at_least(pe, gelu_done, HC * i + m - 1)
                        for c in range(2):
                            last = mm(ps_up[m % 2][:, 0:TS], w1[p][:, c, m * P:(m + 1) * P], xT[p][:, c],
                                      start=(c == 0), stop=(c == 1))
                        last.then_inc(up_ps, 1)
                i, p = item(s, u, 1)
                if i is not None:
                    pe.wait_ge(x_in, 16 * (i + 1))
                    at_least(pe, xt_done, 2 * i)
                    for c in range(2):
                        for k in range(NK):
                            last = nc.tensor.transpose(ps_x[c][0:KC, k * P:(k + 1) * P], x[p][:, k, c * KC:(c + 1) * KC], ident[:])
                    last.then_inc(xt_ps, 1)
                i, p = item(s, u, 2)
                if i is not None:
                    pe.wait_ge(gelu_done, HC * (i + 1))
                    at_least(pe, y_done, i - 1)
                    for k in range(NK):
                        for m in range(HC):
                            last = mm(ps_y[p][:, k // 2, (k % 2) * D:(k % 2 + 1) * D], hid[p][:, m, k * P:(k + 1) * P],
                                      w2[p][:, m], start=(m == 0), stop=(m == HC - 1))
                    last.then_inc(down_ps, 1)
            pipeline(pe, tiles, 3, LEAD, step)


def build(nc, t, out):
    def dram(name, shape):
        return nc.dram_tensor(name, shape, F32, kind="Internal").ap()

    h_embed, h_attn0, h_experts, h_attn1 = (dram(n, [IMG, P, 2, D]) for n in ("h_embed", "h_attn0", "h_experts", "h_attn1"))
    rows = EXPERTS * capacity() + SPARE_TILES * TS
    sorted_x, sorted_y = dram("sorted_x", [rows, D]), dram("sorted_y", [n_tiles() * TS, D])
    tables0 = {"ident": t["ident"], "cos": t["cos"], "sin": t["sin"]}
    tables1 = {**t, "cos": None, "sin": None}
    with ExitStack() as ctx:
        passed = [ctx.enter_context(nc.semaphore(f"passed_{e}")) for e in ("sp", "pool", "dve", "pe")]
        attention_phase(nc, "a0", passed, t["patches"], h_embed, h_attn0,
                        {"tok": t["w_tok"], "tok_add": t["tok_add"], "qk": t["wqk0"], "v": t["wv0"], "o": t["wo0"]}, tables0, True)
        index_all = ctx.enter_context(nc.sbuf_tensor("index_all", [P, 2 * IMG], I32))
        table = ctx.enter_context(nc.sbuf_tensor("table", [1, 2, n_tiles()], I32))
        route_phase(nc, "r", passed, h_attn0, sorted_x, (index_all, table), tables1, {"wg": t["wg"], "bg": t["bg"]})
        expert_phase(nc, "e", passed, sorted_x, sorted_y, table, tables1,
                     {"w1": t["w1_0"], "b1": t["b1_0"], "w2": t["w2_0"], "b2": t["b2_0"]})
        attention_phase(nc, "a1", passed, h_attn0, h_experts, h_attn1, {"qk": t["wqk1"], "v": t["wv1"], "o": t["wo1"]},
                        tables1, False, (sorted_y, index_all))
        ffn_phase(nc, "f1", passed, h_attn1, out,
                  {"w1": t["w1_1"], "b1": t["b1_1"], "w2": t["w2_1"], "b2": t["b2_1"], "alpha_e": t["alpha_e"], "alpha_r": t["alpha_r"]},
                  tables1, 1, ACT.Gelu_apprx_tanh, True, True)


def shape_constants():
    i = np.arange(D // 2, dtype=np.float64)
    theta = 10000.0 ** (-2.0 * i / D)
    angle = np.repeat(np.arange(1, PADT + 1, dtype=np.float64)[:, None] * theta[None, :], 2, axis=-1)
    sign = np.tile([-1.0, 1.0], D // 2)

    def tiles(a):
        return np.ascontiguousarray(a.reshape(2, P, D).transpose(1, 0, 2).astype(np.float32))
    in_mask = np.zeros((KC, 2, 3), np.float32)
    out_mask = np.zeros((P, HC, 9), np.float32)
    for a, e in enumerate(E_CHOICES):
        in_mask[:, :, a] = (np.arange(D).reshape(2, KC).T < e)
        for b, r in enumerate(R_CHOICES):
            out_mask[:, :, 3 * a + b] = (np.arange(HIDDEN).reshape(HC, P).T < r * e)
    return {"ident": np.eye(P, dtype=np.float32), "cos": tiles(np.cos(angle)), "sin": tiles(np.sin(angle) * sign),
            "in_mask": in_mask, "out_mask": out_mask,
            "valid": np.tile(np.stack([np.ones(P), np.arange(P) < T1], 1), 2).astype(np.float32),
            "region": np.tile(np.arange(EXPERTS, dtype=np.float32) * capacity(), (P, 1)),
            "tile_no": np.arange(n_tiles(), dtype=np.float32)[None],
            "tile_row": np.tile(np.arange(n_tiles(), dtype=np.float32) * TS, (P, 1))}


def kernel(**inputs):
    import concourse.bacc as bacc
    from concourse.bass_utils import run_bass_kernel_spmd as run

    x = {k: np.asarray(v) for k, v in inputs.items()}

    def chunks(w, rows):
        return np.ascontiguousarray(w.reshape(-1, rows, w.shape[-1]).transpose(1, 0, 2))

    def every_partition(v):
        return np.ascontiguousarray(np.broadcast_to(v, (P,) + v.shape))

    side, n = 16, 14
    pixels = x["x"].reshape(IMG, 3, n, side, n, side).transpose(0, 1, 3, 5, 2, 4).reshape(IMG, PATCH, n * n)
    patches = np.zeros((IMG, P, PC, PADT), np.float32)
    patches[:, :, :, 1:TOK] = pixels.reshape(IMG, PC, P, n * n).transpose(0, 2, 1, 3)
    tok_add = every_partition(x["L0_tok_b"])[:, None, :].repeat(2, axis=1)
    tok_add[0, 0] = x["cls_tok"][0, 0]
    arrays = {
        "patches": patches, "tok_add": tok_add, "w_tok": chunks(x["L0_tok_W"].T, P),
        "wqk0": chunks(np.concatenate([x["L0_attn_W_q"].T, x["L0_attn_W_k"].T], axis=1), KC),
        "wv0": chunks(x["L0_attn_W_v"].T, KC), "wo0": chunks(x["L0_attn_W_o"].T, KC),
        "wqk1": chunks(np.concatenate([x["L1_attn_wq"].T, x["L1_attn_wk"].T], axis=1), KC),
        "wv1": chunks(x["L1_attn_wv"].T, KC), "wo1": chunks(x["L1_attn_wo"].T, KC),
        "w1_0": np.ascontiguousarray(x["L0_ffn_W1"].reshape(EXPERTS, 2, KC, HIDDEN).transpose(2, 0, 1, 3)),
        "b1_0": np.ascontiguousarray(x["L0_ffn_b1"].reshape(EXPERTS, HC, P).transpose(2, 0, 1)),
        "w2_0": np.ascontiguousarray(x["L0_ffn_W2"].reshape(EXPERTS, HC, P, D).transpose(2, 0, 1, 3)),
        "b2_0": every_partition(x["L0_ffn_b2"]),
        "wg": chunks(x["L0_ffn_Wg"], KC), "bg": every_partition(x["L0_ffn_bg"])[:, None, :].repeat(4, axis=1),
        "w1_1": chunks(x["L1_ffn_w_fc"].T, KC)[:, None], "b1_1": np.ascontiguousarray(x["L1_ffn_b_fc"].reshape(1, HC, P).transpose(2, 0, 1)),
        "w2_1": chunks(x["L1_ffn_w_proj"].T, P)[:, None], "b2_1": every_partition(x["L1_ffn_b_proj"][None]),
        "alpha_e": every_partition(x["L1_ffn_alpha_e"]), "alpha_r": every_partition(x["L1_ffn_alpha_r"]),
        **shape_constants(),
    }
    nc = bacc.Bacc("TRN2", target_bir_lowering=False, num_devices=1)
    tensors = {k: nc.dram_tensor(f"in_{k}", a.shape, F32, kind="ExternalInput").ap() for k, a in arrays.items()}
    out = nc.dram_tensor("out", (IMG, TOK, D), F32, kind="ExternalOutput").ap()
    build(nc, tensors, out)
    result = run(nc, [{f"in_{k}": np.ascontiguousarray(a) for k, a in arrays.items()}], core_ids=[0])
    return result.results[0]["out"]
```

```python
from contextlib import ExitStack

import numpy as np

import concourse.bass as bass
from concourse import mybir

F32 = mybir.dt.float32
F32R = mybir.dt.float32r
BF16 = mybir.dt.bfloat16
I32 = mybir.dt.int32
ALU = mybir.AluOpType
ACT = mybir.ActivationFunctionType
AX_X = mybir.AxisListType.X

P = 128
IMG = 64
TOK = 197
PADT = 2 * P
T1 = TOK - P
D = 192
KC = 96
PATCH = 768
PC = PATCH // P
HEADS = 12
DH = D // HEADS
HIDDEN = 768
HC = HIDDEN // P
EXPERTS = 4
SLOTS = 6
SK = SLOTS * DH
MROWS = 3
SCALE = float(DH) ** -0.5
EPS = 1e-5
NEG = -1e9
UNROLL = 2
LEAD = 6
ROUTE_LEAD = 8
FFN_LEAD = 8
TS = 3 * P
SPARE_TILES = EXPERTS + 1
E_CHOICES = (96, 144, 192)
R_CHOICES = (2, 3, 4)
SIZES = tuple(sorted({r * e for r in R_CHOICES for e in E_CHOICES}))


def at_least(eng, sem, value):
    if isinstance(value, int) and value <= 0:
        return
    eng.wait_ge(sem, value)


def wait_apart(eng, sem, value, passed):
    if isinstance(value, int) and value <= 0:
        return
    eng.wait_ge(sem, value)
    if not isinstance(value, int):
        eng.sem_inc(passed, 1)


def pipeline(eng, items, depth, lead, step, unroll=UNROLL):
    steps = items + depth - 1
    full = lead + (items - 2 - lead) // unroll * unroll
    for s in range(lead):
        step(s, s % unroll)
    with eng.Fori(lead, full, unroll) as s:
        for u in range(unroll):
            step(s + u, u)
    for s in range(full, steps):
        step(s, s % unroll)


DB = D - P
W_HI, W_LO, WB_HI, WB_LO = range(4)
X_HI, X_LO, XB = range(3)
UP_BANKS = 3
PRODUCTS = ((W_HI, X_HI), (W_LO, X_HI), (W_HI, X_LO), (WB_HI, XB), (WB_LO, XB))


def n_tiles():
    return (IMG * TOK + EXPERTS * (TS - 1)) // TS + 1


def capacity():
    return -(-(IMG * TOK) // TS) * TS + TS


def attention_phase(nc, name, passed, x_dram, h_in, h_out, w, tables, embed, experts=None):
    with ExitStack() as ctx:
        def sb(n, shape, dt=F32):
            return ctx.enter_context(nc.sbuf_tensor(f"{name}_{n}", shape, dt))

        def sem(n):
            return ctx.enter_context(nc.semaphore(f"{name}_{n}"))

        def psum(n, shape, dt=F32):
            return ctx.enter_context(nc.psum_tensor(f"{name}_{n}", shape, dt))

        rope = tables["cos"] is not None
        ident = sb("ident", [P, P])
        ident_b = sb("ident_b", [P, P], BF16)
        mask_q = sb("mask_q", [P, P], BF16)
        mask_k = sb("mask_k", [P, P], BF16)
        neg_half = sb("neg_half", [P, 2])
        wqk_in = sb("wqk_in", [P, 2, 2 * D])
        wqk = sb("wqk", [P, 4, 2 * D])
        wv = sb("wv", [P, 2, D])
        wo = sb("wo", [KC, 2, D])
        if rope:
            cos = sb("cos", [P, 2, D])
            sin = sb("sin", [P, 2, D])
        if embed:
            w_tok = sb("w_tok", [P, PC, D])
            tok_add = sb("tok_add", [P, 2, D])
            patches = sb("patches", [P, 2, PC, PADT])
        else:
            y_rows, index_all = experts
            h_before = sb("h_before", [P, 2, 2, D])
            gathered = sb("gathered", [P, 2, 2, D])
            row_of = [sb(f"row_of{u}", [P, 2], I32) for u in range(2)]
        h = sb("h", [P, 2, 2, D])
        stats = sb("stats", [P, 2, 6])
        mv = sb("mv", [P, 2, 2])
        veps = sb("veps", [P, 2])
        rstd = sb("rstd", [P, 2])
        xn = sb("xn", [P, 2, D + DB])
        xT = sb("xT", [P, 2, PADT])
        xs = sb("xs", [P, 3, PADT])
        if rope:
            rc = sb("rc", [P, 2, 2 * D])
            rs = sb("rs", [P, 2, 2 * D])
        qk = sb("qk", [P, 2, 2 * D])
        rest = sb("rest", [P, 2, 2 * D])
        stack = [sb(f"stack{u}", [P, 2, 2, HEADS, SLOTS, DH], BF16) for u in range(2)]
        QT = [sb(f"QT{u}", [P, HEADS, TOK], BF16) for u in range(2)]
        KT = [sb(f"KT{u}", [P, HEADS, TOK], BF16) for u in range(2)]
        V = [sb(f"V{u}", [P, 2, HEADS, 2 * DH]) for u in range(2)]
        mx = sb("mx", [P, 2, HEADS])
        nm = sb("nm", [P, 2, HEADS])
        nm_rest = sb("nm_rest", [P, 2, HEADS])
        nm_parts = sb("nm_parts", [P, 2, MROWS, HEADS], BF16)
        mT = sb("mT", [MROWS * HEADS, TOK], BF16)
        probs0 = sb("probs0", [P, HEADS, TOK])
        probs1 = sb("probs1", [T1, HEADS, T1])
        OT = sb("OT", [P, 3, PADT])
        inv = sb("inv", [P, 2, HEADS])
        ON = sb("ON", [P, 2, HEADS, DH])
        ONT = sb("ONT", [KC, 2, PADT])
        h_res = sb("h_res", [P, 2, 2, D])
        y = sb("y", [P, 2, 2, D])
        ps_front = psum("ps_front", [P, 512])
        ps_qk = psum("ps_qk", [P, 512])
        ps_b = [psum(f"ps_b{n}", [P, 512]) for n in range(2)]
        ps_c = [psum(f"ps_c{n}", [P, 512]) for n in range(2)]
        ps_o = psum("ps_o", [P, 2, 512])

        weights_in = sem("weights_in")
        n_weights = 4 + 2 * rope + 2 * embed
        passed_sp, passed_pool, passed_dve, passed_pe = passed
        ident_sem, consts = sem("ident"), sem("consts")
        if embed:
            patches_in, tok_done = sem("patches_in"), sem("tok_done")
        else:
            h_in_sem, index_in, rows_in = sem("h_in"), sem("index_in"), sem("rows_in")
        h_ready, h_kept = sem("h_ready"), sem("h_kept")
        stats_done, mv_done, veps_done, rstd_done = sem("stats_done"), sem("mv_done"), sem("veps_done"), sem("rstd_done")
        xn_done, xt_ps, xt_done = sem("xn_done"), sem("xt_ps"), sem("xt_done")
        w_split, xs_hi, xs_lo = sem("w_split"), sem("xs_hi"), sem("xs_lo")
        qk_ps, v_ps, v_done = sem("qk_ps"), sem("v_ps"), sem("v_done")
        rope_done, qk_done = sem("rope_done"), sem("qk_done")
        hi_done, rest_done, mid_done, lo_done, dup_done = sem("hi_done"), sem("rest_done"), sem("mid_done"), sem("lo_done"), sem("dup_done")
        stack_ps, stack_act, stack_dve = sem("stack_ps"), sem("stack_act"), sem("stack_dve")
        sq_ps, max_done = sem("sq_ps"), sem("max_done")
        nm_sem, mt_ps, mt_done, mrows_in = sem("nm"), sem("mt_ps"), sem("mt_done"), sem("mrows_in")
        sk_ps, exp_done = sem("sk_ps"), sem("exp_done")
        av_ps, o_done, ot_ps, inv_done, on_done, ont_ps, ont_done = (sem(n) for n in (
            "av_ps", "o_done", "ot_ps", "inv_done", "on_done", "ont_ps", "ont_done"))
        y_ps, hres_in, y_done, y_out = sem("y_ps"), sem("hres_in"), sem("y_done"), sem("y_out")

        CONSTS = 11 + (not embed)
        NT = 6
        ACT_T = (0, 2, 4)
        DVE_T = (1, 3, 5)
        NS = 8
        DUPS = 8
        DEPTH = 5
        E, PR, M, O, Y = range(DEPTH)
        block = ctx.enter_context(nc.Block())

        def item(s, u, stage):
            if isinstance(s, int) and not 0 <= s - stage < IMG:
                return None, None
            return s - stage, (u - stage) % 2

        def score_banks(k):
            return (range(2 * k, 2 * k + 2), False) if k < 6 else (range(6 * (k - 6), 6 * (k - 5)), True)

        def four(ap):
            return ap.rearrange("p (j h d) -> p j h d", j=2, h=HEADS)

        def stack_bank(k):
            return ps_b[k % 2][0:SK, :].bitcast(BF16).rearrange("p (h t) -> p h t", h=4)

        def stack_dst(k, p):
            return (QT[p] if k < 3 else KT[p])[0:SK, 4 * (k % 3):4 * (k % 3) + 4]

        @block.sync
        def _(sp):
            sp.dma_start(wqk_in[:], w["qk"]).then_inc(weights_in, 16)
            sp.dma_start(wv[:], w["v"]).then_inc(weights_in, 16)
            sp.dma_start(wo[:], w["o"]).then_inc(weights_in, 16)
            sp.dma_start(ident[:], tables["ident"]).then_inc(weights_in, 16)
            if rope:
                sp.dma_start(cos[:], tables["cos"]).then_inc(weights_in, 16)
                sp.dma_start(sin[:], tables["sin"]).then_inc(weights_in, 16)
            if embed:
                sp.dma_start(w_tok[:], w["tok"]).then_inc(weights_in, 16)
                sp.dma_start(tok_add[:], w["tok_add"]).then_inc(weights_in, 16)

            def load(i, p):
                if embed:
                    wait_apart(sp, tok_done, i - 1, passed_sp)
                    wait_apart(sp, patches_in, 16 * i, passed_sp)
                    sp.dma_start(patches[:, p], x_dram[i]).then_inc(patches_in, 16)
                else:
                    wait_apart(sp, h_ready, i - 1, passed_sp)
                    wait_apart(sp, h_in_sem, 16 * i, passed_sp)
                    sp.dma_start(h_before[:, p], x_dram[i]).then_inc(h_in_sem, 16)

            def step(s, u):
                i, p = item(s, u, O)
                if i is not None:
                    wait_apart(sp, mrows_in, 16 * i, passed_sp)
                    wait_apart(sp, mt_done, i + 1, passed_sp)
                    sp.dma_start(QT[p][SK:SK + MROWS], mT[:]).then_inc(mrows_in, 16)
                i, p = item(s, u, Y)
                if i is not None:
                    wait_apart(sp, y_out, 16 * i, passed_sp)
                    wait_apart(sp, y_done, i + 1, passed_sp)
                    sp.dma_start(h_out[i], y[:, p]).then_inc(y_out, 16)
                if isinstance(s, int) and s == 0:
                    load(0, 0)
                if not isinstance(s, int) or s + 1 < IMG:
                    load(s + 1, 1 - u)
                i, p = item(s, u, O)
                if i is not None:
                    wait_apart(sp, h_kept, 16 * (i + 1), passed_sp)
                    wait_apart(sp, hres_in, 16 * i, passed_sp)
                    wait_apart(sp, y_done, i - 1, passed_sp)
                    sp.dma_start(h_res[:, p], h_in[i]).then_inc(hres_in, 16)
                i, p = item(s, u, E)
                if i is not None:
                    wait_apart(sp, h_kept, 16 * i, passed_sp)
                    wait_apart(sp, h_ready, i + 1, passed_sp)
                    sp.dma_start(h_in[i], h[:, p]).then_inc(h_kept, 16)
            pipeline(sp, IMG, DEPTH, LEAD, step)
            sp.wait_ge(y_out, 16 * IMG)
            sp.wait_ge(h_kept, 16 * IMG)

        @block.gpsimd
        def _(pool):
            setup = [lambda: nc.gpsimd.memset(mask_q[:], 0.0), lambda: nc.gpsimd.memset(mask_k[:], 0.0),
                     lambda: nc.gpsimd.memset(neg_half[:], -0.5), lambda: nc.gpsimd.memset(OT[:], 1.0),
                     lambda: nc.gpsimd.memset(mx[:], 0.0)]
            for n, fill in enumerate(setup):
                at_least(pool, consts, n)
                fill().then_inc(consts, 1)
            for u in range(2):
                pool.wait_ge(consts, 5 + 2 * u)
                nc.gpsimd.memset(V[u][:], 1.0).then_inc(consts, 1)
                pool.wait_ge(consts, 6 + 2 * u)
                nc.gpsimd.memset(KT[u][SK:P], 1.0).then_inc(consts, 1)
            pool.wait_ge(consts, 9)
            nc.gpsimd.affine_select(out=mask_q[:], in_=mask_q[:], compare_op=ALU.is_ge, fill=NEG, base=0,
                                    pattern=[[-1, P]], channel_multiplier=1).then_inc(consts, 1)
            pool.wait_ge(consts, 10)
            nc.gpsimd.affine_select(out=mask_k[:], in_=mask_k[:], compare_op=ALU.is_ge, fill=NEG, base=0,
                                    pattern=[[1, P]], channel_multiplier=-1).then_inc(consts, 1)
            if not embed:
                pool.wait_ge(consts, 11)
                nc.gpsimd.memset(gathered[:], 0.0).then_inc(consts, 1)
            pool.wait_ge(consts, CONSTS)

            def gather(i, p):
                at_least(pool, h_ready, i - 1)
                wait_apart(pool, rows_in, 32 * i, passed_pool)
                at = index_all[:, 2 * i:2 * i + 2] if isinstance(i, int) else index_all[:, bass.ds(2 * i, 2)]
                nc.gpsimd.tensor_copy(row_of[p][:], at).then_inc(index_in, 1)
                wait_apart(pool, index_in, i + 1, passed_pool)
                for t, n in ((0, P), (1, T1)):
                    nc.gpsimd.indirect_dma_start(out=gathered[0:n, p, t], out_offset=None, in_=y_rows,
                                                 in_offset=bass.IndirectOffsetOnAxis(ap=row_of[p][0:n, t:t + 1], axis=0))\
                        .then_inc(rows_in, 16)

            def rotated(i, t):
                if rope:
                    pool.wait_ge(rope_done, 3 * (2 * i + t + 1))
                    nc.gpsimd.tensor_tensor(qk[:, t], rc[:, t], rs[:, t], ALU.add).then_inc(qk_done, 1)

            def without_first(i, p, t):
                n = 2 * i + t + 1
                pool.wait_ge(hi_done, n)
                pool.wait_ge(qk_done, n)
                at_least(pool, lo_done, 2 * (n - 2))
                nc.gpsimd.tensor_tensor(four(rest[:, t]), four(qk[:, t]), stack[p][:, t, :, :, 0, :], ALU.subtract)\
                    .then_inc(rest_done, 1)

            def third_part(i, p, t):
                n = 2 * i + t + 1
                pool.wait_ge(mid_done, n)
                pool.wait_ge(rest_done, n)
                for j, slot in ((0, 4), (1, 5)):
                    nc.gpsimd.tensor_tensor(stack[p][:, t, j, :, slot, :], four(rest[:, t])[:, j],
                                            stack[p][:, t, j, :, 1 + j, :], ALU.subtract).then_inc(lo_done, 1)

            def step(s, u):
                if not embed:
                    if isinstance(s, int) and s == 0:
                        gather(0, 0)
                    if not isinstance(s, int) or s + 1 < IMG:
                        gather(s + 1, 1 - u)
                i, p = item(s, u, PR)
                if i is not None:
                    rotated(i, 0)
                    without_first(i, p, 0)
                    rotated(i, 1)
                    third_part(i, p, 0)
                i, p = item(s, u, E)
                if i is not None:
                    wait_apart(pool, mv_done, 2 * (i + 1), passed_pool)
                    nc.gpsimd.tensor_scalar_add(veps[:], mv[:, :, 1], EPS).then_inc(veps_done, 1)
                    pool.wait_ge(veps_done, i + 1)
                    nc.gpsimd.tensor_tensor(rstd[:], veps[:], neg_half[:], ALU.pow).then_inc(rstd_done, 1)
                i, p = item(s, u, PR)
                if i is not None:
                    without_first(i, p, 1)
                    third_part(i, p, 1)
                i, p = item(s, u, M)
                if i is not None:
                    wait_apart(pool, mt_ps, i, passed_pool)
                    wait_apart(pool, max_done, NS * (i + 1), passed_pool)
                    nc.gpsimd.tensor_scalar_mul(nm[:], mx[:], -1.0).then_inc(nm_sem, 1)
                    wait_apart(pool, nm_sem, 5 * i + 1, passed_pool)
                    nc.gpsimd.tensor_copy(nm_parts[:, :, 0], nm[:]).then_inc(nm_sem, 1)
                    pool.wait_ge(nm_sem, 5 * i + 2)
                    nc.gpsimd.tensor_tensor(nm_rest[:], nm[:], nm_parts[:, :, 0], ALU.subtract).then_inc(nm_sem, 1)
                    wait_apart(pool, nm_sem, 5 * i + 3, passed_pool)
                    nc.gpsimd.tensor_copy(nm_parts[:, :, 1], nm_rest[:]).then_inc(nm_sem, 1)
                    pool.wait_ge(nm_sem, 5 * i + 4)
                    nc.gpsimd.tensor_tensor(nm_parts[:, :, 2], nm_rest[:], nm_parts[:, :, 1], ALU.subtract)\
                        .then_inc(nm_sem, 1)
            pipeline(pool, IMG, DEPTH, LEAD, step)

        @block.scalar
        def _(act):
            act.wait_ge(weights_in, 16 * n_weights)
            nc.scalar.copy(ident_b[:], ident[:]).then_inc(ident_sem, 1)
            act.wait_ge(consts, CONSTS)

            def step(s, u):
                def tokens():
                    i, p = item(s, u, E)
                    if i is not None:
                        act.wait_ge(xt_ps, i + 1)
                        at_least(act, v_ps, i)
                        nc.scalar.copy(xT[:], ps_front[:].rearrange("p (c t) -> p c t", c=2)).then_inc(xt_done, 1)

                def first_part_of_tokens():
                    i, p = item(s, u, E)
                    if i is not None:
                        act.wait_ge(xt_done, i + 1)
                        nc.scalar.copy(xs[:, X_HI:XB + 1:XB - X_HI].bitcast(F32R), xT[:]).then_inc(xs_hi, 1)

                def value():
                    i, p = item(s, u, PR)
                    if i is not None:
                        act.wait_ge(v_ps, i + 1)
                        at_least(act, av_ps, i - 1)
                        nc.scalar.copy(V[p][:, :, :, 0:DH],
                                       ps_front[:, 0:2 * D].rearrange("p (t h d) -> p t h d", t=2, h=HEADS))\
                            .then_inc(v_done, 1)

                def first_part(t):
                    i, p = item(s, u, PR)
                    if i is not None:
                        act.wait_ge(qk_done, 2 * i + t + 1)
                        at_least(act, stack_ps, NT * (i - 1))
                        nc.scalar.copy(stack[p][:, t, :, :, 0, :], four(qk[:, t])).then_inc(hi_done, 1)

                def second_part(t):
                    i, p = item(s, u, PR)
                    if i is not None:
                        act.wait_ge(rest_done, 2 * i + t + 1)
                        nc.scalar.copy(stack[p][:, t, 0, :, 1, :], four(rest[:, t])[:, 0])
                        nc.scalar.copy(stack[p][:, t, 1, :, 2, :], four(rest[:, t])[:, 1]).then_inc(mid_done, 1)

                def stacks(k):
                    i, p = item(s, u, M)
                    if i is not None:
                        act.wait_ge(stack_ps, NT * i + k + 1)
                        at_least(act, sk_ps, NS * (i - 1))
                        nc.scalar.copy(stack_dst(k, p), stack_bank(k)[:, :, 0:TOK]).then_inc(stack_act, 1)

                def maxima():
                    i, p = item(s, u, O)
                    if i is not None:
                        act.wait_ge(mt_ps, i + 1)
                        at_least(act, mrows_in, 16 * i)
                        m_bank = ps_c[1][0:MROWS * HEADS, 0:PADT // 2].bitcast(BF16)
                        nc.scalar.copy(mT[:, T1:TOK], m_bank[:, 0:P])
                        nc.scalar.copy(mT[:, 0:T1], m_bank[:, P:TOK]).then_inc(mt_done, 1)

                def exponentials(k):
                    i, p = item(s, u, O)
                    if i is not None:
                        heads, small = score_banks(k)
                        n = len(heads)
                        act.wait_ge(sk_ps, NS * i + k + 1)
                        at_least(act, av_ps, i)
                        rows, width, dst = (T1, T1, probs1) if small else (P, TOK, probs0)
                        nc.scalar.activation(dst[:, heads[0]:heads[0] + n],
                                             ps_c[k % 2][0:rows, 0:n * width].rearrange("p (h q) -> p h q", h=n),
                                             ACT.Exp, scale=SCALE).then_inc(exp_done, 1)

                def outputs():
                    i, p = item(s, u, O)
                    if i is not None:
                        act.wait_ge(av_ps, i + 1)
                        at_least(act, ot_ps, i)
                        nc.scalar.copy(OT[:, 0:2, 0:TOK], ps_o[:, 0, 0:2 * TOK].rearrange("p (g q) -> p g q", g=2))
                        nc.scalar.copy(OT[:, 2, 0:TOK], ps_o[:, 1, 0:TOK]).then_inc(o_done, 1)

                def normalized():
                    i, p = item(s, u, O)
                    if i is not None:
                        act.wait_ge(ont_ps, i + 1)
                        at_least(act, y_ps, i)
                        nc.scalar.copy(ONT[:], ps_c[1][0:KC, :].rearrange("p (c t) -> p c t", c=2)).then_inc(ont_done, 1)

                maxima()
                stacks(0)
                first_part(0)
                if rope:
                    second_part(0)
                    stacks(2)
                else:
                    stacks(2)
                    second_part(0)
                exponentials(0)
                exponentials(1)
                stacks(4)
                exponentials(2)
                first_part(1)
                exponentials(3)
                exponentials(4)
                exponentials(5)
                second_part(1)
                exponentials(6)
                exponentials(7)
                outputs()
                value()
                tokens()
                if embed:
                    first_part_of_tokens()
                normalized()
                if not embed:
                    first_part_of_tokens()
            pipeline(act, IMG, DEPTH, LEAD, step)

        @block.vector
        def _(dve):
            dve.wait_ge(weights_in, 16 * n_weights)
            dve.wait_ge(consts, CONSTS)
            for c, hi, lo in ((0, W_HI, W_LO), (1, WB_HI, WB_LO)):
                nc.vector.tensor_copy(wqk[:, hi].bitcast(F32R), wqk_in[:, c]).then_inc(w_split, 1)
                dve.wait_ge(w_split, 2 * c + 1)
                nc.vector.tensor_tensor(wqk[:, lo].bitcast(F32R), wqk_in[:, c], wqk[:, hi], ALU.subtract).then_inc(w_split, 1)

            def step(s, u):
                def statistics():
                    i, p = item(s, u, E)
                    if i is None:
                        return
                    if embed:
                        dve.wait_ge(tok_done, i + 1)
                        at_least(dve, h_kept, 16 * (i - 1))
                        nc.vector.tensor_tensor(h[:, p], ps_front[:, 0:2 * D].rearrange("p (t d) -> p t d", t=2),
                                                tok_add[:], ALU.add).then_inc(h_ready, 1)
                    else:
                        dve.wait_ge(h_in_sem, 16 * (i + 1))
                        dve.wait_ge(rows_in, 32 * (i + 1))
                        at_least(dve, h_kept, 16 * (i - 1))
                        nc.vector.tensor_tensor(h[:, p], h_before[:, p], gathered[:, p], ALU.add).then_inc(h_ready, 1)
                    dve.wait_ge(h_ready, i + 1)
                    for t in range(2):
                        nc.vector.bn_stats(stats[:, t], h[:, p, t]).then_inc(stats_done, 1)
                    wait_apart(dve, veps_done, i, passed_dve)
                    wait_apart(dve, stats_done, 2 * (i + 1), passed_dve)
                    for t in range(2):
                        nc.vector.bn_aggr(mv[:, t], stats[:, t]).then_inc(mv_done, 1)

                def normalize():
                    i, p = item(s, u, E)
                    if i is not None:
                        dve.wait_ge(rstd_done, i + 1)
                        at_least(dve, xt_ps, i)
                        for t in range(2):
                            nc.vector.tensor_scalar(xn[:, t, 0:D], h[:, p, t], mv[:, t, 0:1], rstd[:, t:t + 1],
                                                    ALU.subtract, ALU.mult).then_inc(xn_done, 1)
                        dve.wait_ge(xn_done, 3 * i + 2)
                        nc.vector.tensor_copy(xn[:, :, D:D + DB], xn[:, :, P:D]).then_inc(xn_done, 1)

                def rests():
                    i, p = item(s, u, E)
                    if i is not None:
                        dve.wait_ge(xs_hi, i + 1)
                        nc.vector.tensor_tensor(xs[:, X_LO].bitcast(F32R), xT[:, 0], xs[:, X_HI], ALU.subtract).then_inc(xs_lo, 1)
                        nc.vector.tensor_tensor(xs[DB:P, XB].bitcast(F32R), xT[DB:P, 1], xs[DB:P, XB], ALU.subtract)\
                            .then_inc(xs_lo, 1)

                def rotate(t):
                    i, p = item(s, u, PR)
                    if i is None:
                        return
                    n = 2 * i + t + 1
                    dve.wait_ge(qk_ps, n)
                    q = ps_qk[:, 0:2 * D]
                    if rope:
                        at_least(dve, qk_done, n - 2)
                        bc = cos[:, t, None, :].broadcast_to([P, 2, D])
                        nc.vector.tensor_tensor(rc[:, t].rearrange("p (j d) -> p j d", j=2),
                                                q.rearrange("p (j d) -> p j d", j=2), bc, ALU.mult).then_inc(rope_done, 1)
                        for e in range(2):
                            qs = q.rearrange("p (j d e) -> p j d e", j=2, e=2)[:, :, :, 1 - e]
                            sn = sin[:, t, :].rearrange("p (d e) -> p d e", e=2)[:, None, :, e].broadcast_to([P, 2, D // 2])
                            nc.vector.tensor_tensor(rs[:, t].rearrange("p (j d e) -> p j d e", j=2, e=2)[:, :, :, e],
                                                    qs, sn, ALU.mult).then_inc(rope_done, 1)
                    else:
                        at_least(dve, rest_done, n - 2)
                        nc.vector.tensor_copy(qk[:, t], q).then_inc(qk_done, 1)

                def stacks(k):
                    i, p = item(s, u, M)
                    if i is not None:
                        dve.wait_ge(stack_ps, NT * i + k + 1)
                        at_least(dve, sk_ps, NS * (i - 1))
                        nc.vector.tensor_copy(stack_dst(k, p), stack_bank(k)[:, :, 0:TOK]).then_inc(stack_dve, 1)

                def maximum(k):
                    i, p = item(s, u, M)
                    if i is not None:
                        heads, small = score_banks(k)
                        n = len(heads)
                        if k == 0:
                            at_least(dve, nm_sem, 5 * i)
                        dve.wait_ge(sq_ps, NS * i + k + 1)
                        rows, width, t = (T1, T1, 1) if small else (P, TOK, 0)
                        nc.vector.tensor_reduce(mx[0:rows, t, heads[0]:heads[0] + n],
                                                ps_b[k % 2][0:rows, 0:n * width].rearrange("p (h q) -> p h q", h=n),
                                                AX_X, ALU.max).then_inc(max_done, 1)

                def duplicate(t):
                    i, p = item(s, u, PR)
                    if i is not None:
                        dve.wait_ge(mid_done, 2 * i + t + 1)
                        q, k = stack[p][:, t, 0], stack[p][:, t, 1]
                        nc.vector.tensor_copy(q[:, :, 2:4], q[:, :, 0:2]).then_inc(dup_done, 1)
                        nc.vector.tensor_copy(q[:, :, 5], q[:, :, 0]).then_inc(dup_done, 1)
                        nc.vector.tensor_copy(k[:, :, 1:5:3], k[:, :, 0:1].broadcast_to([P, HEADS, 2, DH])).then_inc(dup_done, 1)
                        nc.vector.tensor_copy(k[:, :, 3], k[:, :, 2]).then_inc(dup_done, 1)

                def divide():
                    i, p = item(s, u, O)
                    if i is not None:
                        dve.wait_ge(ot_ps, i + 1)
                        at_least(dve, ont_ps, i)
                        o = ps_o[:, :, 0:2 * D].rearrange("p t (h e) -> p t h e", h=HEADS)
                        nc.vector.reciprocal(inv[:], o[:, :, :, DH]).then_inc(inv_done, 1)
                        dve.wait_ge(inv_done, i + 1)
                        for t in range(2):
                            nc.vector.tensor_tensor(ON[:, t], o[:, t, :, 0:DH], inv[:, t, :, None].broadcast_to([P, HEADS, DH]),
                                                    ALU.mult).then_inc(on_done, 1)

                def residual():
                    i, p = item(s, u, Y)
                    if i is not None:
                        dve.wait_ge(y_ps, i + 1)
                        dve.wait_ge(hres_in, 16 * (i + 1))
                        at_least(dve, y_out, 16 * (i - 1))
                        nc.vector.tensor_tensor(y[:, p], ps_c[0][:, 0:2 * D].rearrange("p (t d) -> p t d", t=2),
                                                h_res[:, p], ALU.add).then_inc(y_done, 1)

                rotate(0)
                residual()
                stacks(1)
                rotate(1)
                stacks(3)
                statistics()
                stacks(5)
                duplicate(0)
                maximum(0)
                maximum(1)
                maximum(2)
                maximum(3)
                normalize()
                duplicate(1)
                maximum(4)
                maximum(5)
                divide()
                maximum(6)
                maximum(7)
                rests()
            pipeline(dve, IMG, DEPTH, LEAD, step)

        @block.tensor
        def _(pe):
            pe.wait_ge(weights_in, 16 * n_weights)
            pe.wait_ge(consts, CONSTS)
            pe.wait_ge(ident_sem, 1)
            pe.wait_ge(w_split, 4)
            mm = nc.tensor.matmul

            def scores(bank, k, left, right, rows, first, mask, big):
                heads, small = score_banks(k)
                (l0, l1), (r0, r1), m0 = first if small else big
                width = r1 - r0
                for n, hd in enumerate(heads):
                    mm(bank[0:l1 - l0, n * width:(n + 1) * width], left[0:rows, hd, l0:l1], right[0:rows, hd, r0:r1],
                       start=(n == 0), stop=False, skip_group_check=True)
                span = width - m0 if m0 else min(width, l1 - l0)
                out = bank[0:l1 - l0, 0:len(heads) * width].rearrange("p (h q) -> p h q", h=len(heads))[:, :, m0:m0 + span]
                rhs = mask[0:l1 - l0, None, 0:span].broadcast_to([l1 - l0, len(heads), span])
                return mm(out, ident_b[0:l1 - l0, 0:l1 - l0], rhs, start=False, stop=True, skip_group_check=True)

            def step(s, u):
                def embedding(pieces):
                    i, p = item(s, u, E)
                    if i is None or not embed:
                        return
                    for n in pieces:
                        t, c = divmod(n, PC)
                        if n == 0:
                            pe.wait_ge(patches_in, 16 * (i + 1))
                            at_least(pe, xt_done, i)
                        last = mm(ps_front[:, t * D:(t + 1) * D], patches[:, p, c, t * P:(t + 1) * P], w_tok[:, c],
                                  start=(c == 0), stop=(c == PC - 1))
                        if n == 2 * PC - 1:
                            last.then_inc(tok_done, 1)

                def transpose_tokens():
                    i, p = item(s, u, E)
                    if i is None:
                        return
                    pe.wait_ge(xn_done, 3 * (i + 1))
                    at_least(pe, v_done, i)
                    for c in range(2):
                        for t in range(2):
                            last = nc.tensor.transpose(ps_front[:, c * PADT + t * P:c * PADT + (t + 1) * P],
                                                       xn[:, t, c * P:(c + 1) * P], ident[:])
                    last.then_inc(xt_ps, 1)

                def project_qk(t):
                    i, p = item(s, u, PR)
                    if i is None:
                        return
                    pe.wait_ge(xs_lo, 2 * (i + 1))
                    at_least(pe, rope_done if rope else qk_done, (3 if rope else 1) * (2 * i + t))
                    for n, (ws, x) in enumerate(PRODUCTS):
                        last = mm(ps_qk[:, 0:2 * D], xs[:, x, t * P:(t + 1) * P].bitcast(F32R), wqk[:, ws].bitcast(F32R),
                                  start=(n == 0), stop=(n == len(PRODUCTS) - 1))
                    last.then_inc(qk_ps, 1)

                def project_v():
                    i, p = item(s, u, PR)
                    if i is None:
                        return
                    if embed:
                        if item(s, u, E)[0] is not None:
                            pe.wait_ge(h_ready, i + 2)
                    else:
                        pe.wait_ge(xt_done, i + 1)
                    for t in range(2):
                        for c in range(2):
                            last = mm(ps_front[:, t * D:(t + 1) * D], xT[:, c, t * P:(t + 1) * P], wv[:, c],
                                      start=(c == 0), stop=(c == 1))
                    last.then_inc(v_ps, 1)

                def transpose_stacks(k):
                    i, p = item(s, u, M)
                    if i is None:
                        return
                    if k == 0:
                        pe.wait_ge(lo_done, 4 * (i + 1))
                        pe.wait_ge(dup_done, DUPS * (i + 1))
                    if k < 2:
                        at_least(pe, max_done, NS * i)
                    elif k - 2 in ACT_T:
                        pe.wait_ge(stack_act, len(ACT_T) * i + ACT_T.index(k - 2) + 1)
                    else:
                        pe.wait_ge(stack_dve, len(DVE_T) * i + DVE_T.index(k - 2) + 1)
                    for n in range(4):
                        for t in range(2):
                            last = nc.tensor.transpose(stack_bank(k)[:, n, t * P:(t + 1) * P],
                                                       stack[p][:, t, k // 3, 4 * (k % 3) + n].rearrange("p s d -> p (s d)"),
                                                       ident_b[:])
                    last.then_inc(stack_ps, 1)

                def row_scores(k):
                    i, p = item(s, u, M)
                    if i is None:
                        return
                    if k < 2:
                        pe.wait_ge(stack_act, len(ACT_T) * (i + 1))
                        pe.wait_ge(stack_dve, len(DVE_T) * (i + 1))
                    else:
                        pe.wait_ge(max_done, NS * i + k - 1)
                    scores(ps_b[k % 2], k, QT[p], KT[p], SK, ((0, T1), (0, T1), 0), mask_q,
                           ((T1, TOK), (0, TOK), T1)).then_inc(sq_ps, 1)

                def transpose_maxima():
                    i, p = item(s, u, O)
                    if i is None:
                        return
                    at_least(pe, ont_done, i)
                    wait_apart(pe, nm_sem, 5 * (i + 1), passed_pe)
                    m_bank = ps_c[1][0:MROWS * HEADS, 0:PADT // 2].bitcast(BF16)
                    parts = nm_parts[:].rearrange("p t r h -> p t (r h)")
                    nc.tensor.transpose(m_bank[:, 0:P], parts[:, 0], ident_b[:])
                    nc.tensor.transpose(m_bank[:, P:TOK], parts[0:T1, 1], ident_b[0:T1, 0:T1]).then_inc(mt_ps, 1)

                def key_scores(k):
                    i, p = item(s, u, O)
                    if i is None:
                        return
                    if k == 0:
                        pe.wait_ge(mrows_in, 16 * (i + 1))
                        at_least(pe, y_done, i)
                    elif k > 1:
                        pe.wait_ge(exp_done, NS * i + k - 1)
                    scores(ps_c[k % 2], k, KT[p], QT[p], SK + MROWS, ((P, TOK), (P, TOK), 0), mask_k,
                           ((0, P), (0, TOK), 0)).then_inc(sk_ps, 1)

                def weigh_values():
                    i, p = item(s, u, O)
                    if i is None:
                        return
                    pe.wait_ge(exp_done, NS * (i + 1))
                    pe.wait_ge(v_done, i + 1)
                    at_least(pe, on_done, 2 * i)
                    for hd in range(HEADS):
                        g, q0 = hd // 4, 32 * (hd % 4)
                        o = ps_o[q0:q0 + 2 * DH, g // 2, (g % 2) * TOK:(g % 2 + 1) * TOK]
                        mm(o, V[p][:, 0, hd], probs0[:, hd], start=True, stop=True, tile_position=(0, q0))
                        last = mm(o[:, P:TOK], V[p][0:T1, 1, hd], probs1[:, hd], start=False, stop=True,
                                  tile_position=(0, q0), skip_group_check=True)
                    last.then_inc(av_ps, 1)

                def transpose_outputs():
                    i, p = item(s, u, O)
                    if i is None:
                        return
                    pe.wait_ge(o_done, i + 1)
                    for t in range(2):
                        for g in range(3):
                            last = nc.tensor.transpose(ps_o[:, t, g * P:(g + 1) * P], OT[:, g, t * P:(t + 1) * P], ident[:])
                    last.then_inc(ot_ps, 1)

                def transpose_normalized():
                    i, p = item(s, u, O)
                    if i is None:
                        return
                    pe.wait_ge(on_done, 2 * (i + 1))
                    for c in range(2):
                        for t in range(2):
                            last = nc.tensor.transpose(ps_c[1][0:KC, c * PADT + t * P:c * PADT + (t + 1) * P],
                                                       ON[:, t].rearrange("p h d -> p (h d)")[:, c * KC:(c + 1) * KC], ident[:])
                    last.then_inc(ont_ps, 1)

                def project_output():
                    i, p = item(s, u, Y)
                    if i is None:
                        return
                    pe.wait_ge(ont_done, i + 1)
                    for t in range(2):
                        for c in range(2):
                            last = mm(ps_c[0][:, t * D:(t + 1) * D], ONT[:, c, t * P:(t + 1) * P], wo[:, c],
                                      start=(c == 0), stop=(c == 1))
                    last.then_inc(y_ps, 1)

                embedding(range(0, 4))
                if embed:
                    project_qk(0)
                    project_output()
                else:
                    project_output()
                    project_qk(0)
                transpose_maxima()
                embedding(range(4, 8))
                transpose_stacks(0)
                transpose_stacks(1)
                project_qk(1)
                embedding(range(8, 12))
                transpose_stacks(2)
                transpose_stacks(3)
                key_scores(0)
                key_scores(1)
                transpose_stacks(4)
                key_scores(2)
                transpose_stacks(5)
                key_scores(3)
                for k in range(4):
                    key_scores(4 + k)
                    row_scores(k)
                row_scores(4)
                weigh_values()
                project_v()
                row_scores(5)
                transpose_outputs()
                transpose_tokens()
                row_scores(6)
                row_scores(7)
                transpose_normalized()
            pipeline(pe, IMG, DEPTH, LEAD, step)


def ffn_phase(nc, name, passed, h_in, h_out, w, tables):
    pairs = IMG // 2
    with ExitStack() as ctx:
        def sb(n, shape, dt=F32):
            return ctx.enter_context(nc.sbuf_tensor(f"{name}_{n}", shape, dt))

        def sem(n):
            return ctx.enter_context(nc.semaphore(f"{name}_{n}"))

        def psum(n, shape, dt=F32):
            return ctx.enter_context(nc.psum_tensor(f"{name}_{n}", shape, dt))

        ident = sb("ident", [P, P])
        neg_half = sb("neg_half", [P, 4])
        w1 = sb("w1", [P, 2, HIDDEN])
        w1s = sb("w1s", [P, 4, HIDDEN])
        b1 = sb("b1", [P, HC])
        w2 = sb("w2", [P, HC, D])
        b2 = sb("b2", [P, D])
        h = [sb(f"h{u}", [P, 4, D]) for u in range(4)]
        stats = sb("stats", [P, 4, 6])
        mv = sb("mv", [P, 4, 2])
        veps = sb("veps", [P, 4])
        rstd = sb("rstd", [P, 4])
        xn = [sb(f"xn{u}", [P, 4, D + DB]) for u in range(2)]
        xT = [sb(f"xT{u}", [P, 3, 2, TOK]) for u in range(2)]
        hid = [sb(f"hid{u}", [P, HC, 2, PADT]) for u in range(2)]
        y = [sb(f"y{u}", [P, 4, D]) for u in range(2)]
        ps_x = [psum(f"ps_x{n}", [P, 512]) for n in range(2)]
        ps_up = [psum(f"ps_up{n}", [P, 512]) for n in range(UP_BANKS)]
        ps_y = psum("ps_y", [P, 2, 512])
        alpha_e = sb("alpha_e", [P, 3])
        alpha_r = sb("alpha_r", [P, 3])
        in_mask = sb("in_mask", [P, 2, 3])
        out_mask = sb("out_mask", [P, HC, 9])
        a = sb("a", [P, 3, 3])
        a_in = sb("a_in", [P, 2, 3, 3])
        a_out = sb("a_out", [P, HC, 9])
        c_up = sb("c_up", [P, 2, len(SIZES)])
        c_down = sb("c_down", [P, HC, 3])
        c_b1 = sb("c_b1", [P, HC])
        c_b2 = sb("c_b2", [P, 3])

        passed_sp, passed_pool, passed_dve, _ = passed
        weights_in, mixed, consts = sem("weights_in"), sem("mixed"), sem("consts")
        h_in_sem = sem("h_in")
        stats_done, mv_done, veps_done, rstd_done = sem("stats_done"), sem("mv_done"), sem("veps_done"), sem("rstd_done")
        xn_done, dup_done, xt_ps = sem("xn_done"), sem("dup_done"), sem("xt_ps")
        xt_hi, xt_done = sem("xt_hi"), sem("xt_done")
        up_ps, gelu_done, down_ps = sem("up_ps"), sem("gelu_done"), sem("down_ps")
        bias_done, y_done, y_out = sem("bias_done"), sem("y_done"), sem("y_out")
        WEIGHTS = 9
        STORES = 4
        MIXED = 1 + 2 + 1 + (2 * len(SIZES) - 1 + 3) + 1 + 2 + 1 + 2 + 1 + len(SIZES) + 2 * 3 + 1 + 4
        DEPTH = 3
        L, T, F = range(DEPTH)
        block = ctx.enter_context(nc.Block())

        def item(s, u, stage):
            if isinstance(s, int) and not 0 <= s - stage < pairs:
                return None, None
            return s - stage, (u - stage) % 4

        def x_bank(c, rows=slice(0, P)):
            return ps_x[c][rows].rearrange("p (g t) -> p g t", g=2)[:, :, 0:TOK]

        @block.sync
        def _(sp):
            for dst, src in ((ident, tables["ident"]), (w1, w["w1"]), (b1, w["b1"]), (w2, w["w2"]), (b2, w["b2"]),
                             (alpha_e, w["alpha_e"]), (alpha_r, w["alpha_r"]), (in_mask, tables["in_mask"]),
                             (out_mask, tables["out_mask"])):
                sp.dma_start(dst[:], src).then_inc(weights_in, 16)

            def load(i, p):
                wait_apart(sp, h_in_sem, 16 * i, passed_sp)
                wait_apart(sp, y_done, i - 3, passed_sp)
                src = h_in[bass.ds(2 * i, 2)] if not isinstance(i, int) else h_in[2 * i:2 * i + 2]
                sp.dma_start(h[p][:].rearrange("p (g t) d -> p g t d", g=2), src.rearrange("g p t d -> p g t d"))\
                    .then_inc(h_in_sem, 16)

            def step(s, u):
                if isinstance(s, int) and s == 0:
                    load(0, 0)
                if not isinstance(s, int) or s + 1 < pairs:
                    load(s + 1, (u + 1) % 4)
                i, p = item(s, u, F)
                if i is not None:
                    wait_apart(sp, y_out, 16 * STORES * i, passed_sp)
                    wait_apart(sp, y_done, i + 1, passed_sp)
                    for g in range(2):
                        sp.dma_start(h_out[2 * i + g, 0:P], y[p % 2][:, 2 * g]).then_inc(y_out, 16)
                        sp.dma_start(h_out[2 * i + g, P:TOK], y[p % 2][0:T1, 2 * g + 1]).then_inc(y_out, 16)
            pipeline(sp, pairs, DEPTH, FFN_LEAD, step, 4)
            sp.wait_ge(y_out, 16 * STORES * pairs)

        @block.gpsimd
        def _(pool):
            nc.gpsimd.memset(neg_half[:], -0.5).then_inc(consts, 1)
            for u in range(2):
                pool.wait_ge(consts, u + 1)
                nc.gpsimd.memset(hid[u][:, :, :, TOK:PADT], 0.0).then_inc(consts, 1)
            pool.wait_ge(consts, 3)

            def step(s, u):
                i, p = item(s, u, L)
                if i is not None:
                    wait_apart(pool, mv_done, 4 * (i + 1), passed_pool)
                    nc.gpsimd.tensor_scalar_add(veps[:], mv[:, :, 1], EPS).then_inc(veps_done, 1)
                    pool.wait_ge(veps_done, i + 1)
                    nc.gpsimd.tensor_tensor(rstd[:], veps[:], neg_half[:], ALU.pow).then_inc(rstd_done, 1)
            pipeline(pool, pairs, DEPTH, FFN_LEAD, step, 4)

        @block.scalar
        def _(act):
            act.wait_ge(weights_in, 16 * WEIGHTS)
            act.wait_ge(consts, 3)
            act.wait_ge(mixed, MIXED)

            def step(s, u):
                def gelu(m):
                    i, p = item(s, u, F)
                    if i is not None:
                        act.wait_ge(up_ps, HC * i + m + 1)
                        at_least(act, down_ps, i - 1)
                        nc.scalar.activation(hid[p % 2][:, m, :, 0:TOK],
                                             ps_up[m % UP_BANKS][:, 0:2 * TOK].rearrange("p (g t) -> p g t", g=2),
                                             ACT.Gelu_apprx_tanh, bias=b1[:, m:m + 1]).then_inc(gelu_done, 1)

                for m in range(HC):
                    gelu(m)
                i, p = item(s, u, T)
                if i is not None:
                    act.wait_ge(xt_ps, i + 1)
                    at_least(act, up_ps, HC * (i - 1))
                    for c, slot in ((0, X_HI), (1, XB)):
                        nc.scalar.copy(xT[p % 2][:, slot].bitcast(F32R), x_bank(c)).then_inc(xt_hi, 1)
            pipeline(act, pairs, DEPTH, FFN_LEAD, step, 4)

        @block.vector
        def _(dve):
            dve.wait_ge(weights_in, 16 * WEIGHTS)
            mixes = [0]

            def mixing(ins):
                mixes[0] += 1
                ins.then_inc(mixed, 1)
                dve.wait_ge(mixed, mixes[0])
            tt = nc.vector.tensor_tensor
            mixing(tt(a[:], alpha_e[:, :, None].broadcast_to([P, 3, 3]), alpha_r[:, None, :].broadcast_to([P, 3, 3]), ALU.mult))
            for c in range(2):
                mixing(tt(a_in[:, c], a[:], in_mask[:, c, :, None].broadcast_to([P, 3, 3]), ALU.mult))
            mixing(tt(a_out[:], a[:, None].rearrange("p o i j -> p o (i j)").broadcast_to([P, HC, 9]), out_mask[:], ALU.mult))
            for k in reversed(range(len(SIZES))):
                at_bound = [(i, j) for i, e in enumerate(E_CHOICES) for j, r in enumerate(R_CHOICES) if r * e == SIZES[k]]
                for n, (i, j) in enumerate(at_bound):
                    if n == 0:
                        mixing(nc.vector.tensor_copy(c_up[:, :, k], a_in[:, :, i, j]))
                    else:
                        mixing(tt(c_up[:, :, k], c_up[:, :, k], a_in[:, :, i, j], ALU.add))
                if k + 1 < len(SIZES):
                    mixing(tt(c_up[:, :, k], c_up[:, :, k], c_up[:, :, k + 1], ALU.add))
            mixing(nc.vector.tensor_reduce(c_down[:], a_out[:].rearrange("p m (i j) -> p m i j", i=3), AX_X, ALU.add))
            for k in (1, 0):
                mixing(tt(c_down[:, :, k], c_down[:, :, k], c_down[:, :, k + 1], ALU.add))
            mixing(nc.vector.tensor_reduce(c_b2[:], a[:], AX_X, ALU.add))
            for k in (1, 0):
                mixing(tt(c_b2[:, k:k + 1], c_b2[:, k:k + 1], c_b2[:, k + 1:k + 2], ALU.add))
            mixing(nc.vector.tensor_reduce(c_b1[:], a_out[:], AX_X, ALU.add))
            for k, (n0, n1) in enumerate(zip((0,) + SIZES, SIZES)):
                mixing(tt(w1[:, :, n0:n1], w1[:, :, n0:n1], c_up[:, :, k:k + 1].broadcast_to([P, 2, n1 - n0]), ALU.mult))
            for k, (n0, n1) in enumerate(zip((0,) + E_CHOICES, E_CHOICES)):
                mixing(tt(w2[:, :, n0:n1], w2[:, :, n0:n1], c_down[:, :, k:k + 1].broadcast_to([P, HC, n1 - n0]), ALU.mult))
                mixing(tt(b2[:, n0:n1], b2[:, n0:n1], c_b2[:, k:k + 1].broadcast_to([P, n1 - n0]), ALU.mult))
            mixing(tt(b1[:], b1[:], c_b1[:], ALU.mult))
            for c, hi, lo in ((0, W_HI, W_LO), (1, WB_HI, WB_LO)):
                mixing(nc.vector.tensor_copy(w1s[:, hi].bitcast(F32R), w1[:, c]))
                mixing(tt(w1s[:, lo].bitcast(F32R), w1[:, c], w1s[:, hi], ALU.subtract))
            assert mixes[0] == MIXED, mixes

            def step(s, u):
                i, p = item(s, u, L)
                if i is not None:
                    dve.wait_ge(h_in_sem, 16 * (i + 1))
                    for j in range(4):
                        nc.vector.bn_stats(stats[:, j], h[p][:, j]).then_inc(stats_done, 1)
                    wait_apart(dve, stats_done, 4 * (i + 1), passed_dve)
                    wait_apart(dve, veps_done, i, passed_dve)
                    for j in range(4):
                        nc.vector.bn_aggr(mv[:, j], stats[:, j]).then_inc(mv_done, 1)
                    dve.wait_ge(rstd_done, i + 1)
                    at_least(dve, xt_ps, i - 1)
                    for j in range(4):
                        nc.vector.tensor_scalar(xn[p % 2][:, j, 0:D], h[p][:, j], mv[:, j, 0:1], rstd[:, j:j + 1],
                                                ALU.subtract, ALU.mult).then_inc(xn_done, 1)
                    dve.wait_ge(xn_done, 4 * (i + 1))
                    nc.vector.tensor_copy(xn[p % 2][:, :, D:D + DB], xn[p % 2][:, :, P:D]).then_inc(dup_done, 1)
                i, p = item(s, u, T)
                if i is not None:
                    dve.wait_ge(xt_hi, 2 * (i + 1))
                    nc.vector.tensor_tensor(xT[p % 2][:, X_LO].bitcast(F32R), x_bank(0), xT[p % 2][:, X_HI], ALU.subtract)\
                        .then_inc(xt_done, 1)
                    nc.vector.tensor_tensor(xT[p % 2][DB:P, XB].bitcast(F32R), x_bank(1, slice(DB, P)), xT[p % 2][DB:P, XB],
                                            ALU.subtract).then_inc(xt_done, 1)
                i, p = item(s, u, F)
                if i is not None:
                    dve.wait_ge(xn_done, 4 * (i + 1))
                    for g in range(2):
                        nc.vector.tensor_tensor(h[p][:, 2 * g:2 * g + 2], h[p][:, 2 * g:2 * g + 2],
                                                b2[:, None, :].broadcast_to([P, 2, D]), ALU.add).then_inc(bias_done, 1)
                    dve.wait_ge(bias_done, 2 * (i + 1))
                    dve.wait_ge(down_ps, i + 1)
                    at_least(dve, y_out, 16 * STORES * (i - 1))
                    for g in range(2):
                        acc = nc.vector.tensor_tensor(y[p % 2][:, 2 * g:2 * g + 2],
                                                      ps_y[:, g, 0:2 * D].rearrange("p (t d) -> p t d", t=2),
                                                      h[p][:, 2 * g:2 * g + 2], ALU.add)
                    acc.then_inc(y_done, 1)
            pipeline(dve, pairs, DEPTH, FFN_LEAD, step, 4)

        @block.tensor
        def _(pe):
            pe.wait_ge(weights_in, 16 * WEIGHTS)
            pe.wait_ge(consts, 3)
            pe.wait_ge(mixed, MIXED)
            mm = nc.tensor.matmul

            def step(s, u):
                i, p = item(s, u, F)
                if i is not None:
                    pe.wait_ge(xt_done, 2 * (i + 1))
                    for m in range(HC):
                        at_least(pe, gelu_done, HC * i + m - UP_BANKS + 1)
                        for n, (ws, xs) in enumerate(PRODUCTS):
                            last = mm(ps_up[m % UP_BANKS][:, 0:2 * TOK], w1s[:, ws, m * P:(m + 1) * P].bitcast(F32R),
                                      xT[p % 2][:, xs].rearrange("p g t -> p (g t)").bitcast(F32R),
                                      start=(n == 0), stop=(n == len(PRODUCTS) - 1))
                        last.then_inc(up_ps, 1)
                i, p = item(s, u, T)
                if i is not None:
                    pe.wait_ge(dup_done, i + 1)
                    at_least(pe, xt_done, 2 * i)
                    for c in range(2):
                        for j in range(4):
                            last = nc.tensor.transpose(ps_x[c][:, j * P:(j + 1) * P], xn[p % 2][:, j, c * P:(c + 1) * P],
                                                       ident[:])
                    last.then_inc(xt_ps, 1)
                i, p = item(s, u, F)
                if i is not None:
                    pe.wait_ge(gelu_done, HC * (i + 1))
                    at_least(pe, y_done, i)
                    for g in range(2):
                        for t in range(2):
                            for m in range(HC):
                                last = mm(ps_y[:, g, t * D:(t + 1) * D], hid[p % 2][:, m, g, t * P:(t + 1) * P],
                                          w2[:, m], start=(m == 0), stop=(m == HC - 1))
                    last.then_inc(down_ps, 1)
            pipeline(pe, pairs, DEPTH, FFN_LEAD, step, 4)


def route_phase(nc, name, passed, h_in, sorted_x, index, tables, w, resident):
    pairs = IMG // 2
    index_all, table = index
    with ExitStack() as ctx:
        def sb(n, shape, dt=F32):
            return ctx.enter_context(nc.sbuf_tensor(f"{name}_{n}", shape, dt))

        def sem(n):
            return ctx.enter_context(nc.semaphore(f"{name}_{n}"))

        def psum(n, shape, dt=F32):
            return ctx.enter_context(nc.psum_tensor(f"{name}_{n}", shape, dt))

        tiles = n_tiles()
        ident = sb("ident", [P, P])
        neg_half = sb("neg_half", [P, 4])
        wg = sb("wg", [KC, 2, EXPERTS])
        bg = sb("bg", [P, 4, EXPERTS])
        valid = sb("valid", [P, 4])
        base = sb("base", [P, EXPERTS])
        region = sb("region", [P, EXPERTS])
        tile_no = sb("tile_no", [1, tiles])
        tile_row = sb("tile_row", [P, tiles])
        before = sb("before", [P, P], BF16)
        ones = sb("ones", [P, P], BF16)
        zeros = sb("zeros", [P, TS // P, D])
        h = [sb(f"h{u}", [P, 4, D]) for u in range(4)]
        stats = sb("stats", [P, 4, 6])
        mv = sb("mv", [P, 2, 4, 2])
        veps = sb("veps", [P, 4])
        rstd = sb("rstd", [P, 2, 4])
        xn = [sb(f"xn{u}", [P, 4, D]) for u in range(4)]
        xT = sb("xT", [KC, 2, 4 * P])
        logits = sb("logits", [P, 4, EXPERTS])
        top = sb("top", [P, 4])
        eq = sb("eq", [P, 4, EXPERTS])
        at_top = sb("at_top", [P, 4, EXPERTS])
        taken = sb("taken", [P, EXPERTS - 1, 4])
        onehot = sb("onehot", [P, 4, EXPERTS], BF16)
        rows = sb("rows", [P, 4, EXPERTS])
        picked = sb("picked", [P, 4, EXPERTS])
        row = sb("row", [P, 4])
        row_i = [sb(f"row_i{u}", [P, 4], I32) for u in range(2)]
        count = sb("count", [P, EXPERTS])
        more = sb("more", [P, EXPERTS, tiles])
        n_of = sb("n_of", [P, EXPERTS])
        start = sb("start", [P, EXPERTS])
        jump = sb("jump", [P, EXPERTS])
        past = sb("past", [1, EXPERTS, tiles])
        jumps = sb("jumps", [1, EXPERTS, tiles])
        total = sb("total", [1, 2, tiles])
        total2 = sb("total2", [1, tiles])
        row_all = sb("row_all", [P, 2 * IMG])
        moved = sb("moved", [P, EXPERTS - 1, 2 * IMG])
        base_i = sb("base_i", [1, EXPERTS], I32)
        ps_x = [psum(f"ps_x{n}", [P, 512]) for n in range(2)]
        ps_g = psum("ps_g", [P, 512])
        ps_r = psum("ps_r", [P, 512])

        passed_sp, passed_pool, passed_dve, _ = passed
        weights_in, consts, h_in_sem = sem("weights_in"), sem("consts"), sem("h_in")
        stats_done, mv_done, veps_done, rstd_done = sem("stats_done"), sem("mv_done"), sem("veps_done"), sem("rstd_done")
        xn_done, xt_ps, xt_done, gate_ps = sem("xn_done"), sem("xt_ps"), sem("xt_done"), sem("gate_ps")
        picks, onehot_done, rank_ps, ranks, scattered = sem("picks"), sem("onehot_done"), sem("rank_ps"), sem("ranks"), sem("scattered")
        table_step, table_done, zeroed = sem("table_step"), sem("table_done"), sem("zeroed")
        experts_in = sem("experts_in")
        PICKS = 4 + (EXPERTS - 1)
        RANKS = 6
        WEIGHTS = 7
        CONSTS = 6
        DEPTH = 4
        L, N, G, R = range(DEPTH)
        block = ctx.enter_context(nc.Block())

        def item(s, u, stage):
            if isinstance(s, int) and not 0 <= s - stage < pairs:
                return None, None
            return s - stage, (u - stage) % 4

        @block.sync
        def _(sp):
            for dst, src in ((ident, "ident"), (wg, "wg"), (bg, "bg"), (valid, "valid"), (region, "region"),
                             (tile_no, "tile_no"), (tile_row, "tile_row")):
                sp.dma_start(dst[:], (w if src in w else tables)[src]).then_inc(weights_in, 16)
            pieces = [(resident[k][:, e], w[k][:, e]) for e in range(EXPERTS) for k in ("w1", "w2")]
            pieces += [(resident[k][:], w[k]) for k in ("b1", "b2")]

            def load(i, p):
                wait_apart(sp, h_in_sem, 16 * i, passed_sp)
                wait_apart(sp, xn_done, 4 * (i - 3), passed_sp)
                src = h_in[bass.ds(2 * i, 2)] if not isinstance(i, int) else h_in[2 * i:2 * i + 2]
                sp.dma_start(h[p][:].rearrange("p (g t) d -> p g t d", g=2), src.rearrange("g p t d -> p g t d"))\
                    .then_inc(h_in_sem, 16)

            def step(s, u):
                if isinstance(s, int) and s == 0:
                    load(0, 0)
                if not isinstance(s, int) or s + 1 < pairs:
                    load(s + 1, (u + 1) % 4)
                if isinstance(s, int) and s < ROUTE_LEAD:
                    for dst, src in pieces[s::ROUTE_LEAD]:
                        sp.dma_start(dst, src).then_inc(experts_in, 16)
            pipeline(sp, pairs, DEPTH, ROUTE_LEAD, step, 4)
            sp.wait_ge(experts_in, 16 * len(pieces))
            sp.wait_ge(consts, CONSTS)
            spare = EXPERTS * capacity()
            for n in range(SPARE_TILES):
                sp.dma_start(sorted_x[spare + n * TS:spare + (n + 1) * TS].rearrange("(k p) d -> p k d", p=P), zeros[:])\
                    .then_inc(zeroed, 16)
            sp.wait_ge(table_done, 1)
            for e in range(EXPERTS):
                first = sp.value_load(base_i[0:1, e:e + 1], min_val=0, max_val=spare - TS)
                sp.dma_start(sorted_x[bass.ds(first, TS)].rearrange("(k p) d -> p k d", p=P), zeros[:]).then_inc(zeroed, 16)
            sp.wait_ge(zeroed, 16 * (SPARE_TILES + EXPERTS))

        @block.gpsimd
        def _(pool):
            setup = [lambda: nc.gpsimd.memset(neg_half[:], -0.5), lambda: nc.gpsimd.memset(ones[:], 1.0),
                     lambda: nc.gpsimd.memset(before[:], 0.0), lambda: nc.gpsimd.memset(zeros[:], 0.0),
                     lambda: nc.gpsimd.memset(row_all[:], 0.0),
                     lambda: nc.gpsimd.affine_select(out=before[:], in_=before[:], compare_op=ALU.is_ge, fill=1.0, base=0,
                                                     pattern=[[-1, P]], channel_multiplier=1)]
            for n, fill in enumerate(setup):
                at_least(pool, consts, n)
                fill().then_inc(consts, 1)
            pool.wait_ge(consts, CONSTS)

            def step(s, u):
                i, p = item(s, u, L)
                if i is not None:
                    wait_apart(pool, mv_done, 4 * (i + 1), passed_pool)
                    wait_apart(pool, rstd_done, i, passed_pool)
                    nc.gpsimd.tensor_scalar_add(veps[:], mv[:, p % 2, :, 1], EPS).then_inc(veps_done, 1)
                    pool.wait_ge(veps_done, i + 1)
                    at_least(pool, xn_done, 4 * (i - 1))
                    nc.gpsimd.tensor_tensor(rstd[:, p % 2], veps[:], neg_half[:], ALU.pow).then_inc(rstd_done, 1)
                i, p = item(s, u, R)
                if i is not None:
                    wait_apart(pool, ranks, RANKS * (i + 1), passed_pool)
                    wait_apart(pool, scattered, 64 * i, passed_pool)
                    for j in range(4):
                        n = P if j % 2 == 0 else T1
                        nc.gpsimd.indirect_dma_start(out=sorted_x, out_offset=bass.IndirectOffsetOnAxis(ap=row_i[p % 2][0:n, j:j + 1], axis=0),
                                                     in_=xn[p][0:n, j], in_offset=None).then_inc(scattered, 16)
            pipeline(pool, pairs, DEPTH, ROUTE_LEAD, step, 4)
            pool.wait_ge(scattered, 64 * pairs)

        @block.scalar
        def _(act):
            act.wait_ge(weights_in, 16 * WEIGHTS)

            def step(s, u):
                i, p = item(s, u, G)
                if i is not None:
                    act.wait_ge(xt_ps, i + 1)
                    at_least(act, gate_ps, i)
                    for c in range(2):
                        nc.scalar.copy(xT[:, c], ps_x[c][0:KC]).then_inc(xt_done, 1)
            pipeline(act, pairs, DEPTH, ROUTE_LEAD, step, 4)

        @block.vector
        def _(dve):
            dve.wait_ge(weights_in, 16 * WEIGHTS)
            dve.wait_ge(consts, CONSTS)
            nc.vector.tensor_copy(count[:], region[:]).then_inc(table_step, 1)
            tt = nc.vector.tensor_tensor
            for e in range(EXPERTS):
                nc.vector.memset(base[:, e:e + 1], float(e * capacity())).then_inc(table_step, 1)
            dve.wait_ge(table_step, 1 + EXPERTS)

            def step(s, u):
                i, p = item(s, u, L)
                if i is not None:
                    wait_apart(dve, mv_done, 4 * i, passed_dve)
                    dve.wait_ge(h_in_sem, 16 * (i + 1))
                    for j in range(4):
                        nc.vector.bn_stats(stats[:, j], h[p][:, j]).then_inc(stats_done, 1)
                    wait_apart(dve, stats_done, 4 * (i + 1), passed_dve)
                    wait_apart(dve, veps_done, i - 1, passed_dve)
                    wait_apart(dve, xn_done, 4 * (i - 1), passed_dve)
                    for j in range(4):
                        nc.vector.bn_aggr(mv[:, p % 2, j], stats[:, j]).then_inc(mv_done, 1)
                i, p = item(s, u, R)
                if i is not None:
                    k = [0]

                    def pick(ins):
                        k[0] += 1
                        ins.then_inc(picks, 1)
                        dve.wait_ge(picks, PICKS * i + k[0])
                    dve.wait_ge(gate_ps, i + 1)
                    pick(tt(logits[:], ps_g[:, 0:4 * EXPERTS].rearrange("p (j n) -> p j n", j=4), bg[:], ALU.add))
                    pick(nc.vector.tensor_reduce(top[:], logits[:], AX_X, ALU.max))
                    pick(tt(eq[:], logits[:], top[:, :, None].broadcast_to([P, 4, EXPERTS]), ALU.is_equal))
                    pick(tt(at_top[:], eq[:], valid[:, :, None].broadcast_to([P, 4, EXPERTS]), ALU.mult))
                    at_least(dve, rank_ps, i)
                    nc.vector.tensor_copy(onehot[:, :, 0], at_top[:, :, 0]).then_inc(onehot_done, 1)
                    so_far = at_top[:, :, 0]
                    for n in range(1, EXPERTS):
                        nc.vector.tensor_tensor(onehot[:, :, n], at_top[:, :, n], so_far, ALU.is_gt).then_inc(onehot_done, 1)
                        pick(tt(taken[:, n - 1], at_top[:, :, n], so_far, ALU.max))
                        so_far = taken[:, n - 1]
                i, p = item(s, u, N)
                if i is not None:
                    dve.wait_ge(rstd_done, i + 1)
                    at_least(dve, scattered, 64 * (i - 3))
                    for j in range(4):
                        nc.vector.tensor_scalar(xn[p][:, j], h[p][:, j], mv[:, p % 2, j, 0:1], rstd[:, p % 2, j:j + 1],
                                                ALU.subtract, ALU.mult).then_inc(xn_done, 1)
                i, p = item(s, u, R)
                if i is not None:
                    k = [0]

                    def rank(ins):
                        k[0] += 1
                        ins.then_inc(ranks, 1)
                        dve.wait_ge(ranks, RANKS * i + k[0])
                    dve.wait_ge(rank_ps, i + 1)
                    rank(tt(rows[:], ps_r[:, 0:4 * EXPERTS].rearrange("p (j n) -> p j n", j=4),
                            base[:, None, :].broadcast_to([P, 4, EXPERTS]), ALU.add))
                    rank(tt(picked[:], rows[:], onehot[:], ALU.mult))
                    rank(nc.vector.tensor_reduce(row[:], picked[:], AX_X, ALU.add))
                    at_least(dve, scattered, 64 * (i - 1))
                    rank(nc.vector.tensor_copy(row_i[p % 2][:], row[:]))
                    rank(tt(base[:], base[:], ps_r[:, 4 * EXPERTS:5 * EXPERTS], ALU.add))
                    at = row_all[:, bass.ds(4 * i, 4)] if not isinstance(i, int) else row_all[:, 4 * i:4 * i + 4]
                    rank(nc.vector.tensor_copy(at, row[:]))
            pipeline(dve, pairs, DEPTH, ROUTE_LEAD, step, 4)

            steps = [1 + EXPERTS]

            def then(ins):
                steps[0] += 1
                ins.then_inc(table_step, 1)
                dve.wait_ge(table_step, steps[0])
            E = EXPERTS
            then(tt(count[:], base[:], region[:], ALU.subtract))
            then(tt(more[:], count[:, :, None].broadcast_to([P, E, tiles]), tile_row[:, None, :].broadcast_to([P, E, tiles]), ALU.is_gt))
            then(nc.vector.tensor_reduce(n_of[:], more[:], AX_X, ALU.add))
            then(nc.vector.tensor_copy(start[:], n_of[:]))
            for e in range(1, E):
                then(tt(start[:, e:e + 1], start[:, e:e + 1], start[:, e - 1:e], ALU.add))
            then(nc.vector.tensor_scalar(jump[:], n_of[:], -float(TS), float(capacity()), ALU.mult, ALU.add))
            then(tt(past[:], tile_no[:, None, :].broadcast_to([1, E, tiles]), start[0:1, :, None].broadcast_to([1, E, tiles]), ALU.is_ge))
            then(tt(jumps[:], past[:], jump[0:1, :, None].broadcast_to([1, E, tiles]), ALU.mult))
            then(nc.vector.tensor_reduce(total[:, 0], jumps[:].rearrange("o e t -> o t e"), AX_X, ALU.add))
            then(nc.vector.tensor_reduce(total[:, 1], past[:, 0:E - 1].rearrange("o e t -> o t e"), AX_X, ALU.add))
            then(tt(total2[:], total[:, 0], tile_row[0:1], ALU.add))
            then(nc.vector.tensor_copy(table[:, 0], total2[:]))
            then(nc.vector.tensor_copy(table[:, 1], total[:, 1]))
            nc.vector.tensor_copy(base_i[:], base[0:1, :]).then_inc(table_done, 1)
            for e in range(1, E):
                then(nc.vector.tensor_scalar(moved[:, e - 1], row_all[:], float(e * capacity()), jump[:, e - 1:e],
                                             ALU.is_ge, ALU.mult))
            for e in range(1, E):
                then(tt(row_all[:], row_all[:], moved[:, e - 1], ALU.subtract))
            then(nc.vector.tensor_copy(index_all[:], row_all[:]))

        @block.tensor
        def _(pe):
            pe.wait_ge(weights_in, 16 * WEIGHTS)
            pe.wait_ge(consts, CONSTS)
            mm = nc.tensor.matmul

            def step(s, u):
                i, p = item(s, u, G)
                if i is not None:
                    pe.wait_ge(xn_done, 4 * (i + 1))
                    at_least(pe, xt_done, 2 * i)
                    for c in range(2):
                        for j in range(4):
                            last = nc.tensor.transpose(ps_x[c][0:KC, j * P:(j + 1) * P], xn[p][:, j, c * KC:(c + 1) * KC], ident[:])
                    last.then_inc(xt_ps, 1)
                i, p = item(s, u, R)
                if i is not None:
                    pe.wait_ge(onehot_done, EXPERTS * (i + 1))
                    at_least(pe, ranks, RANKS * i)
                    for j in range(4):
                        mm(ps_r[:, j * EXPERTS:(j + 1) * EXPERTS], before[:], onehot[:, j], start=True, stop=(j == 0))
                        for q in range(j):
                            mm(ps_r[:, j * EXPERTS:(j + 1) * EXPERTS], ones[:], onehot[:, q], start=False, stop=(q == j - 1))
                    for j in range(4):
                        last = mm(ps_r[:, 4 * EXPERTS:5 * EXPERTS], ones[:], onehot[:, j], start=(j == 0), stop=(j == 3))
                    last.then_inc(rank_ps, 1)
                i, p = item(s, u, G)
                if i is not None:
                    pe.wait_ge(xt_done, 2 * (i + 1))
                    at_least(pe, picks, PICKS * (i - 1) + 1)
                    for j in range(4):
                        for c in range(2):
                            last = mm(ps_g[:, j * EXPERTS:(j + 1) * EXPERTS], xT[:, c, j * P:(j + 1) * P], wg[:, c],
                                      start=(c == 0), stop=(c == 1))
                    last.then_inc(gate_ps, 1)
            pipeline(pe, pairs, DEPTH, ROUTE_LEAD, step, 4)


def expert_phase(nc, name, passed, sorted_x, sorted_y, table, tables, resident):
    with ExitStack() as ctx:
        def sb(n, shape, dt=F32):
            return ctx.enter_context(nc.sbuf_tensor(f"{name}_{n}", shape, dt))

        def sem(n):
            return ctx.enter_context(nc.semaphore(f"{name}_{n}"))

        def psum(n, shape, dt=F32):
            return ctx.enter_context(nc.psum_tensor(f"{name}_{n}", shape, dt))

        tiles = n_tiles()
        NK = TS // P
        ident = sb("ident", [P, P])
        w1_in, b1_all, w2_all, b2_all = (resident[k] for k in ("w1", "b1", "w2", "b2"))
        w1_all = sb("w1_all", [P, EXPERTS, 4 * HIDDEN])
        w1 = [sb(f"w1_{u}", [P, 4, HIDDEN]) for u in range(2)]
        b1 = [sb(f"b1_{u}", [P, HC]) for u in range(2)]
        w2 = [sb(f"w2_{u}", [P, HC, D]) for u in range(2)]
        b2 = [sb(f"b2_{u}", [P, D]) for u in range(2)]
        x = [sb(f"x{u}", [P, NK, D + DB]) for u in range(2)]
        xT = [sb(f"xT{u}", [P, 3, TS]) for u in range(2)]
        hid = [sb(f"hid{u}", [P, HC, TS]) for u in range(2)]
        y = [sb(f"y{u}", [P, NK, D]) for u in range(2)]
        ps_x = [psum(f"ps_x{n}", [P, 512]) for n in range(2)]
        ps_up = [psum(f"ps_up{n}", [P, 512]) for n in range(UP_BANKS)]
        ps_y = psum("ps_y", [P, 2, 512])

        passed_sp, _, passed_dve, _ = passed
        weights_in, x_in, picked = sem("weights_in"), sem("x_in"), sem("picked")
        w1_hi, w1_split = sem("w1_hi"), sem("w1_split")
        xt_ps, xt_hi, xt_done = sem("xt_ps"), sem("xt_hi"), sem("xt_done")
        up_ps, gelu_done, down_ps, y_done, y_out = sem("up_ps"), sem("gelu_done"), sem("down_ps"), sem("y_done"), sem("y_out")
        block = ctx.enter_context(nc.Block())

        def item(s, u, stage):
            if isinstance(s, int) and not 0 <= s - stage < tiles:
                return None, None
            return s - stage, (u - stage) % 2

        def w1_part(n, slot):
            return w1_all[:, n // 2, slot * HIDDEN:(slot + 1) * HIDDEN]

        def rows_of(eng, i):
            at = table[0:1, 0, i:i + 1] if isinstance(i, int) else table[0:1, 0, bass.ds(i, 1)]
            return eng.value_load(at, min_val=0, max_val=EXPERTS * capacity() + (SPARE_TILES - 1) * TS)

        @block.sync
        def _(sp):
            sp.dma_start(ident[:], tables["ident"]).then_inc(weights_in, 16)

            def step(s, u):
                i, p = item(s, u, 0)
                if i is not None:
                    wait_apart(sp, x_in, 32 * i, passed_sp)
                    wait_apart(sp, xt_ps, i - 1, passed_sp)
                    tile = sorted_x[bass.ds(rows_of(sp, i), TS)].rearrange("(k p) d -> p k d", p=P)
                    sp.dma_start(x[p][:, :, 0:D], tile).then_inc(x_in, 16)
                    sp.dma_start(x[p][:, :, D:D + DB], tile[:, :, P:D]).then_inc(x_in, 16)
                i, p = item(s, u, 2)
                if i is not None:
                    wait_apart(sp, y_out, 16 * i, passed_sp)
                    wait_apart(sp, y_done, i + 1, passed_sp)
                    at = sorted_y[i * TS:(i + 1) * TS] if isinstance(i, int) else sorted_y[bass.ds(i * TS, TS)]
                    sp.dma_start(at.rearrange("(k p) d -> p k d", p=P), y[p][:])\
                        .then_inc(y_out, 16)
            pipeline(sp, tiles, 3, LEAD, step)
            sp.wait_ge(y_out, 16 * tiles)

        @block.scalar
        def _(act):
            for n in range(2 * EXPERTS):
                nc.scalar.copy(w1_part(n, (W_HI, WB_HI)[n % 2]).bitcast(F32R), w1_in[:, n // 2, n % 2]).then_inc(w1_hi, 1)

            def step(s, u):
                i, p = item(s, u, 2)
                if i is not None:
                    act.wait_ge(picked, 4 * (i + 1))
                    for m in range(HC):
                        act.wait_ge(up_ps, HC * i + m + 1)
                        at_least(act, down_ps, i - 1)
                        nc.scalar.activation(hid[p][:, m], ps_up[m % UP_BANKS][:, 0:TS], ACT.Gelu, bias=b1[p][:, m:m + 1])\
                            .then_inc(gelu_done, 1)
                i, p = item(s, u, 1)
                if i is not None:
                    act.wait_ge(xt_ps, i + 1)
                    at_least(act, up_ps, HC * (i - 1))
                    for c, slot in ((0, X_HI), (1, XB)):
                        nc.scalar.copy(xT[p][:, slot].bitcast(F32R), ps_x[c][:, 0:TS]).then_inc(xt_hi, 1)
            pipeline(act, tiles, 3, LEAD, step)

        @block.vector
        def _(dve):
            for n in range(2 * EXPERTS):
                hi, lo = (w1_part(n, k) for k in ((W_HI, W_LO), (WB_HI, WB_LO))[n % 2])
                dve.wait_ge(w1_hi, n + 1)
                nc.vector.tensor_tensor(lo.bitcast(F32R), w1_in[:, n // 2, n % 2], hi, ALU.subtract).then_inc(w1_split, 1)
            dve.wait_ge(w1_split, 2 * EXPERTS)

            def step(s, u):
                i, p = item(s, u, 1)
                if i is not None:
                    at = table[0:1, 1, i:i + 1] if isinstance(i, int) else table[0:1, 1, bass.ds(i, 1)]
                    expert = dve.value_load(at, min_val=0, max_val=EXPERTS - 1)
                    wait_apart(dve, down_ps, i - 1, passed_dve)
                    wait_apart(dve, y_done, i - 1, passed_dve)
                    for dst, src in ((w1[p][:].rearrange("p c n -> p (c n)").bitcast(F32R), w1_all), (b1[p][:], b1_all),
                                     (w2[p][:].rearrange("p c n -> p (c n)"), w2_all), (b2[p][:], b2_all)):
                        nc.vector.tensor_copy(dst, src[:, bass.ds(expert, 1)].rearrange("p o n -> p (o n)")).then_inc(picked, 1)
                    dve.wait_ge(xt_hi, 2 * (i + 1))
                    nc.vector.tensor_tensor(xT[p][:, X_LO].bitcast(F32R), ps_x[0][:, 0:TS], xT[p][:, X_HI], ALU.subtract)\
                        .then_inc(xt_done, 1)
                    nc.vector.tensor_tensor(xT[p][DB:P, XB].bitcast(F32R), ps_x[1][DB:P, 0:TS], xT[p][DB:P, XB],
                                            ALU.subtract).then_inc(xt_done, 1)
                i, p = item(s, u, 2)
                if i is not None:
                    dve.wait_ge(down_ps, i + 1)
                    at_least(dve, y_out, 16 * (i - 1))
                    nc.vector.tensor_tensor(y[p][:, 0:2], ps_y[:, 0, 0:2 * D].rearrange("p (k d) -> p k d", k=2),
                                            b2[p][:, None, :].broadcast_to([P, 2, D]), ALU.add)
                    nc.vector.tensor_tensor(y[p][:, 2], ps_y[:, 1, 0:D], b2[p][:], ALU.add).then_inc(y_done, 1)
            pipeline(dve, tiles, 3, LEAD, step)

        @block.tensor
        def _(pe):
            pe.wait_ge(weights_in, 16)
            mm = nc.tensor.matmul

            def step(s, u):
                i, p = item(s, u, 2)
                if i is not None:
                    pe.wait_ge(xt_done, 2 * (i + 1))
                    pe.wait_ge(picked, 4 * (i + 1))
                    for m in range(HC):
                        at_least(pe, gelu_done, HC * i + m - UP_BANKS + 1)
                        for n, (ws, xs) in enumerate(PRODUCTS):
                            last = mm(ps_up[m % UP_BANKS][:, 0:TS], w1[p][:, ws, m * P:(m + 1) * P].bitcast(F32R),
                                      xT[p][:, xs].bitcast(F32R), start=(n == 0), stop=(n == len(PRODUCTS) - 1))
                        last.then_inc(up_ps, 1)
                i, p = item(s, u, 1)
                if i is not None:
                    pe.wait_ge(x_in, 32 * (i + 1))
                    at_least(pe, xt_done, 2 * i)
                    for c in range(2):
                        for k in range(NK):
                            last = nc.tensor.transpose(ps_x[c][:, k * P:(k + 1) * P], x[p][:, k, c * P:(c + 1) * P], ident[:])
                    last.then_inc(xt_ps, 1)
                i, p = item(s, u, 2)
                if i is not None:
                    pe.wait_ge(gelu_done, HC * (i + 1))
                    at_least(pe, y_done, i)
                    for k in range(NK):
                        for m in range(HC):
                            last = mm(ps_y[:, k // 2, (k % 2) * D:(k % 2 + 1) * D], hid[p][:, m, k * P:(k + 1) * P],
                                      w2[p][:, m], start=(m == 0), stop=(m == HC - 1))
                    last.then_inc(down_ps, 1)
            pipeline(pe, tiles, 3, LEAD, step)


def build(nc, t, out):
    def dram(name, shape):
        return nc.dram_tensor(name, shape, F32, kind="Internal").ap()

    h_embed, h_attn0, h_experts, h_attn1 = (dram(n, [IMG, P, 2, D]) for n in ("h_embed", "h_attn0", "h_experts", "h_attn1"))
    rows = EXPERTS * capacity() + SPARE_TILES * TS
    sorted_x, sorted_y = dram("sorted_x", [rows, D]), dram("sorted_y", [n_tiles() * TS, D])
    tables0 = {"ident": t["ident"], "cos": t["cos"], "sin": t["sin"]}
    tables1 = {**t, "cos": None, "sin": None}
    with ExitStack() as ctx:
        passed = [ctx.enter_context(nc.semaphore(f"passed_{e}")) for e in ("sp", "pool", "dve", "pe")]
        attention_phase(nc, "a0", passed, t["patches"], h_embed, h_attn0,
                        {"tok": t["w_tok"], "tok_add": t["tok_add"], "qk": t["wqk0"], "v": t["wv0"], "o": t["wo0"]}, tables0, True)
        index_all = ctx.enter_context(nc.sbuf_tensor("index_all", [P, 2 * IMG], I32))
        table = ctx.enter_context(nc.sbuf_tensor("table", [1, 2, n_tiles()], I32))
        with ExitStack() as weights:
            resident = {k: weights.enter_context(nc.sbuf_tensor(f"experts_{k}", shape, F32)) for k, shape in (
                ("w1", [P, EXPERTS, 2, HIDDEN]), ("b1", [P, EXPERTS, HC]), ("w2", [P, EXPERTS, HC * D]), ("b2", [P, EXPERTS, D]))}
            route_phase(nc, "r", passed, h_attn0, sorted_x, (index_all, table), tables1,
                        {"wg": t["wg"], "bg": t["bg"], "w1": t["w1_0"], "b1": t["b1_0"],
                         "w2": t["w2_0"].rearrange("p e c n -> p e (c n)"), "b2": t["b2_0"]}, resident)
            expert_phase(nc, "e", passed, sorted_x, sorted_y, table, tables1, resident)
        attention_phase(nc, "a1", passed, h_attn0, h_experts, h_attn1, {"qk": t["wqk1"], "v": t["wv1"], "o": t["wo1"]},
                        tables1, False, (sorted_y, index_all))
        ffn_phase(nc, "f1", passed, h_attn1, out,
                  {"w1": t["w1_1"], "b1": t["b1_1"], "w2": t["w2_1"], "b2": t["b2_1"], "alpha_e": t["alpha_e"], "alpha_r": t["alpha_r"]},
                  tables1)


def shape_constants():
    i = np.arange(D // 2, dtype=np.float64)
    theta = 10000.0 ** (-2.0 * i / D)
    angle = np.repeat(np.arange(1, PADT + 1, dtype=np.float64)[:, None] * theta[None, :], 2, axis=-1)
    sign = np.tile([-1.0, 1.0], D // 2)

    def tiles(a):
        return np.ascontiguousarray(a.reshape(2, P, D).transpose(1, 0, 2).astype(np.float32))
    in_mask = np.zeros((P, 2, 3), np.float32)
    out_mask = np.zeros((P, HC, 9), np.float32)
    features = np.stack([np.arange(P), P + np.arange(P) % DB], 1)
    for a, e in enumerate(E_CHOICES):
        in_mask[:, :, a] = features < e
        for b, r in enumerate(R_CHOICES):
            out_mask[:, :, 3 * a + b] = (np.arange(HIDDEN).reshape(HC, P).T < r * e)
    return {"ident": np.eye(P, dtype=np.float32), "cos": tiles(np.cos(angle)), "sin": tiles(np.sin(angle) * sign),
            "in_mask": in_mask, "out_mask": out_mask,
            "valid": np.tile(np.stack([np.ones(P), np.arange(P) < T1], 1), 2).astype(np.float32),
            "region": np.tile(np.arange(EXPERTS, dtype=np.float32) * capacity(), (P, 1)),
            "tile_no": np.arange(n_tiles(), dtype=np.float32)[None],
            "tile_row": np.tile(np.arange(n_tiles(), dtype=np.float32) * TS, (P, 1))}


def kernel(**inputs):
    import concourse.bacc as bacc
    from concourse.bass_utils import run_bass_kernel_spmd as run

    x = {k: np.asarray(v) for k, v in inputs.items()}

    def chunks(w, rows):
        return np.ascontiguousarray(w.reshape(-1, rows, w.shape[-1]).transpose(1, 0, 2))

    def stacked(w):
        return np.ascontiguousarray(np.stack([w[:P], np.concatenate([w[P:], w[P:]])], axis=1))

    def padded(w):
        return np.ascontiguousarray(np.concatenate([w, np.zeros((2 * P - D, w.shape[1]), np.float32)]).reshape(2, P, -1).transpose(1, 0, 2))

    def every_partition(v):
        return np.ascontiguousarray(np.broadcast_to(v, (P,) + v.shape))

    side, n = 16, 14
    pixels = x["x"].reshape(IMG, 3, n, side, n, side).transpose(0, 1, 3, 5, 2, 4).reshape(IMG, PATCH, n * n)
    patches = np.zeros((IMG, P, PC, PADT), np.float32)
    patches[:, :, :, 1:TOK] = pixels.reshape(IMG, PC, P, n * n).transpose(0, 2, 1, 3)
    tok_add = every_partition(x["L0_tok_b"])[:, None, :].repeat(2, axis=1)
    tok_add[0, 0] = x["cls_tok"][0, 0]
    arrays = {
        "patches": patches, "tok_add": tok_add, "w_tok": chunks(x["L0_tok_W"].T, P),
        "wqk0": stacked(np.concatenate([x["L0_attn_W_q"].T, x["L0_attn_W_k"].T], axis=1)),
        "wv0": padded(x["L0_attn_W_v"].T), "wo0": chunks(x["L0_attn_W_o"].T, KC),
        "wqk1": stacked(np.concatenate([x["L1_attn_wq"].T, x["L1_attn_wk"].T], axis=1)),
        "wv1": padded(x["L1_attn_wv"].T), "wo1": chunks(x["L1_attn_wo"].T, KC),
        "w1_0": np.stack([stacked(x["L0_ffn_W1"][e]) for e in range(EXPERTS)], axis=1),
        "b1_0": np.ascontiguousarray(x["L0_ffn_b1"].reshape(EXPERTS, HC, P).transpose(2, 0, 1)),
        "w2_0": np.ascontiguousarray(x["L0_ffn_W2"].reshape(EXPERTS, HC, P, D).transpose(2, 0, 1, 3)),
        "b2_0": every_partition(x["L0_ffn_b2"]),
        "wg": chunks(x["L0_ffn_Wg"], KC), "bg": every_partition(x["L0_ffn_bg"])[:, None, :].repeat(4, axis=1),
        "w1_1": stacked(x["L1_ffn_w_fc"].T), "b1_1": np.ascontiguousarray(x["L1_ffn_b_fc"].reshape(HC, P).T),
        "w2_1": chunks(x["L1_ffn_w_proj"].T, P), "b2_1": every_partition(x["L1_ffn_b_proj"]),
        "alpha_e": every_partition(x["L1_ffn_alpha_e"]), "alpha_r": every_partition(x["L1_ffn_alpha_r"]),
        **shape_constants(),
    }
    nc = bacc.Bacc("TRN2", target_bir_lowering=False, num_devices=1)
    tensors = {k: nc.dram_tensor(f"in_{k}", a.shape, F32, kind="ExternalInput").ap() for k, a in arrays.items()}
    out = nc.dram_tensor("out", (IMG, TOK, D), F32, kind="ExternalOutput").ap()
    build(nc, tensors, out)
    result = run(nc, [{f"in_{k}": np.ascontiguousarray(a) for k, a in arrays.items()}], core_ids=[0])
    return result.results[0]["out"]
```
